# Optimizing a Trainium2 kernel written in Bass

```python
import numpy as np
import jax
import jax.numpy as jnp

def _softmax(x, axis=-1):
    return jax.nn.softmax(x, axis=axis)

def _gelu(x):
    return jax.nn.gelu(x, approximate=True)

def _silu(x):
    return jax.nn.silu(x)

def _sigmoid(x):
    return jax.nn.sigmoid(x)

def _layernorm(x, axis=-1, eps=1e-05):
    m = jnp.mean(x, axis=axis, keepdims=True)
    v = jnp.var(x, axis=axis, keepdims=True)
    return (x - m) / jnp.sqrt(v + eps)

def _scatter_add(tgt, idx, src, axis=0):
    return tgt.at[idx].add(src)

def _segment_sum(src, seg, n):
    return jax.ops.segment_sum(src, seg, n)
kernel_name = 'mk_lm_tower_d2_tok_ids512_r4_552d00'

def setup_inputs(seed: int=0):
    np.random.seed(seed)
    _w = jnp.asarray

    def _rec_inputs():
        import jax
        import jax.numpy as jnp
        _rk = jax.random.key(seed)
        x = jax.random.randint(jax.random.fold_in(_rk, 1), (32, 128), 0, 16, jnp.int32)
        return x
    x = _rec_inputs()

    def _L0_tok_setup():
        import jax, jax.numpy as jnp
        import numpy as np
        VOCAB = 16
        D_MODEL = 128
        D_EMB = int(D_MODEL * 0.7)
        D_STFT = D_MODEL - D_EMB
        N_FFT = 64
        HOP = 64
        N_FREQ = N_FFT // 2 + 1
        B, L = (4, 2048)

        def _stft_mag(signal):
            pad = N_FFT // 2
            padded = jnp.pad(signal, ((0, 0), (pad, pad)), mode='reflect')
            n_frames = signal.shape[1] // HOP + 1
            idx = jnp.arange(n_frames)[:, None] * HOP + jnp.arange(N_FFT)[None, :]
            window = 0.5 - 0.5 * jnp.cos(2.0 * jnp.pi * jnp.arange(N_FFT) / N_FFT)
            frames = padded[:, idx] * window.astype(signal.dtype)
            return jnp.abs(jnp.fft.rfft(frames, axis=-1))
        key = jax.random.key(seed)
        k1, k2, k3, k4 = jax.random.split(key, 4)
        input_ids = jax.random.randint(k1, (B, L), 0, VOCAB)
        emb_table = jax.random.normal(k2, (VOCAB, D_EMB), dtype=jnp.float32) * 0.02
        proj_w = jax.random.normal(k3, (VOCAB * N_FREQ, D_STFT), dtype=jnp.float32) * 0.02
        proj_b = jnp.zeros((D_STFT,), dtype=jnp.float32)
        return {'input_ids': input_ids, 'emb_table': emb_table, 'proj_w': proj_w, 'proj_b': proj_b}
    _L0_tok_all = _L0_tok_setup()
    _L0_tok_in = {k: v for k, v in _L0_tok_all.items() if k in ('emb_table', 'proj_w', 'proj_b')}
    del _L0_tok_all

    def _L0_attn_setup():
        import jax, jax.numpy as jnp
        import numpy as np
        NUM_HEADS = 8
        key = jax.random.key(seed)
        k1, k2, k3 = jax.random.split(key, 3)
        B, N, C = (4, 512, 128)
        x = jax.random.normal(k1, (B, N, C), dtype=jnp.float32)
        q_w = jax.random.normal(k2, (C, C), dtype=jnp.float32) * 0.02
        kv_w = jax.random.normal(k3, (2 * C, C), dtype=jnp.float32) * 0.02
        return {'x': x, 'q_w': q_w, 'kv_w': kv_w}
    _L0_attn_all = _L0_attn_setup()
    _L0_attn_in = {k: v for k, v in _L0_attn_all.items() if k in ('q_w', 'kv_w')}
    del _L0_attn_all

    def _L0_ffn_setup():
        import jax, jax.numpy as jnp
        import numpy as np
        K_INPUT, K_PROCESS, K_OUTPUT = (64, 128, 64)

        def _gelu(x):
            return jax.nn.gelu(x, approximate=False)
        key = jax.random.key(seed)
        ks = jax.random.split(key, 6)
        d_model, n_in, n_proc, n_out, d_pv = (128, 512, 256, 512, 64)
        B, S = (2, 256)

        def xavier(k, shape):
            std = (2.0 / (shape[0] + shape[1])) ** 0.5
            return jax.random.normal(k, shape, dtype=jnp.float32) * std
        return {'x': jax.random.normal(ks[0], (B, S, d_model), dtype=jnp.float32), 'input_patterns': xavier(ks[1], (n_in, d_model)), 'process_input_weights': xavier(ks[2], (n_proc, n_in)), 'process_values': xavier(ks[3], (n_proc, d_pv)), 'output_input_weights': xavier(ks[4], (n_out, d_pv)), 'output_patterns': xavier(ks[5], (n_out, d_model))}
    _L0_ffn_all = _L0_ffn_setup()
    _L0_ffn_in = {k: v for k, v in _L0_ffn_all.items() if k in ('input_patterns', 'process_input_weights', 'process_values', 'output_input_weights', 'output_patterns')}
    del _L0_ffn_all

    def _L1_attn_setup():
        import jax, jax.numpy as jnp
        import numpy as np
        B, T, C, DH, CS = (8, 512, 128, 128, 64)

        def _forward(x, Wq, Wk, Wv, Wg, bg, A, sink, v_null):
            b, t, c = x.shape
            dh = Wq.shape[0]
            nc = t // CS
            scale = dh ** (-0.5)
            q = (x @ Wq.T)[:, None]
            k = (x @ Wk.T)[:, None]
            v = (x @ Wv.T)[:, None]
            g = jax.nn.sigmoid(x @ Wg.T + bg)[:, None]

            def to_chunks(a):
                return a.reshape(b, 1, nc, CS, dh).transpose(2, 0, 1, 3, 4)
            qc, kc, gc = (to_chunks(q), to_chunks(k), to_chunks(g))
            hist0 = jnp.zeros((b, 1, nc, dh), x.dtype)
            last0 = jnp.zeros((b, 1, dh), x.dtype)
            chunk_ids = jnp.arange(nc)

            def step(carry, inp):
                hist, last = carry
                i, qi, ki, gi = inp
                scores = jnp.einsum('bhcd,bhnd->bhcn', ki, hist) * scale
                valid = jnp.arange(nc) < i
                w = jax.nn.softmax(jnp.where(valid, scores, -1e+30), axis=-1)
                q_retr = jnp.einsum('bhcn,bhnd->bhcd', w, hist)
                q_init = jnp.where(i > 0, last[:, :, None, :] + q_retr, 0.0)
                q_out = jnp.cumsum(gi * qi, axis=2) + q_init
                final = q_out[:, :, -1, :]
                hist = hist.at[:, :, i, :].set(final)
                return ((hist, final), q_out)
            _, q_chunks = jax.lax.scan(step, (hist0, last0), (chunk_ids, qc, kc, gc))
            Qc = q_chunks.transpose(1, 2, 0, 3, 4).reshape(b, 1, t, dh)
            mean_s = 0.5 * (Qc.mean(-1, keepdims=True) + k.mean(-1, keepdims=True))
            std_s = 0.5 * (jnp.std(Qc, -1, keepdims=True, ddof=1) + jnp.std(k, -1, keepdims=True, ddof=1))
            Qn = (Qc - mean_s) / (std_s + 1e-06)
            Kn = (k - mean_s) / (std_s + 1e-06)
            inv_freq = 1.0 / 10000.0 ** (jnp.arange(0, dh, 2, dtype=jnp.float32) / dh)
            freqs = jnp.arange(t, dtype=jnp.float32)[:, None] * inv_freq[None, :]
            cos, sin = (jnp.cos(freqs), jnp.sin(freqs))

            def rope(a):
                x1, x2 = (a[..., 0::2], a[..., 1::2])
                return jnp.concatenate([-x2 * sin + x1 * cos, x1 * sin + x2 * cos], axis=-1)
            S = A - jnp.swapaxes(A, -1, -2)

            def wedge(a):
                return a + jnp.einsum('bhtd,hde->bhte', a, S)
            Qg, Kg = (wedge(rope(Qn)), wedge(rope(Kn)))
            attn = jnp.einsum('bhtd,bhsd->bhts', Qg, Kg) * scale
            causal = jnp.tril(jnp.ones((t, t), bool))
            attn = jnp.where(causal, attn, -jnp.inf)
            sink_col = jnp.broadcast_to(sink, (b, 1, t, 1))
            probs = jax.nn.softmax(jnp.concatenate([attn, sink_col], axis=-1), axis=-1)
            out = probs[..., :t] @ v + probs[..., t:] * v_null
            return out.transpose(0, 2, 1, 3).reshape(b, t, c)
        key = jax.random.key(seed)
        ks = jax.random.split(key, 9)
        x = jax.random.normal(ks[0], (B, T, C), jnp.float32)
        Wq = jax.random.normal(ks[1], (DH, C), jnp.float32) * 0.02
        Wk = jax.random.normal(ks[2], (DH, C), jnp.float32) * 0.02
        Wv = jax.random.normal(ks[3], (DH, C), jnp.float32) * 0.02
        Wg = jax.random.normal(ks[4], (DH, C), jnp.float32) * 0.02
        bg = jax.random.normal(ks[5], (DH,), jnp.float32) * 0.02
        A = jax.random.normal(ks[6], (1, DH, DH), jnp.float32) * 0.02
        sink = jnp.float32(0.0)
        v_null = jax.random.normal(ks[7], (1, 1, 1, DH), jnp.float32) * 0.02
        return dict(x=x, Wq=Wq, Wk=Wk, Wv=Wv, Wg=Wg, bg=bg, A=A, sink=sink, v_null=v_null)
    _L1_attn_all = _L1_attn_setup()
    _L1_attn_in = {k: v for k, v in _L1_attn_all.items() if k in ('Wq', 'Wk', 'Wv', 'Wg', 'bg', 'A', 'sink', 'v_null')}
    del _L1_attn_all

    def _L1_ffn_setup():
        import jax, jax.numpy as jnp
        import numpy as np
        from jax import lax
        N_EXPERTS = 16
        TOP_K = 2
        D_MODEL = 128
        D_FF = 512
        key = jax.random.key(seed)
        ks = jax.random.split(key, 7)
        s_in = 1.0 / np.sqrt(D_MODEL)
        s_ff = 1.0 / np.sqrt(D_FF)
        x = jax.random.normal(ks[0], (2, 512, D_MODEL), dtype=jnp.float32)
        router_w = jax.random.uniform(ks[1], (N_EXPERTS, D_MODEL), jnp.float32, -s_in, s_in)
        router_b = jax.random.uniform(ks[2], (N_EXPERTS,), jnp.float32, -s_in, s_in)
        w1 = jax.random.uniform(ks[3], (N_EXPERTS, D_FF, D_MODEL), jnp.float32, -s_in, s_in)
        b1 = jax.random.uniform(ks[4], (N_EXPERTS, D_FF), jnp.float32, -s_in, s_in)
        w2 = jax.random.uniform(ks[5], (N_EXPERTS, D_MODEL, D_FF), jnp.float32, -s_ff, s_ff)
        b2 = jax.random.uniform(ks[6], (N_EXPERTS, D_MODEL), jnp.float32, -s_ff, s_ff)
        return {'x': x, 'router_w': router_w, 'router_b': router_b, 'w1': w1, 'b1': b1, 'w2': w2, 'b2': b2}
    _L1_ffn_all = _L1_ffn_setup()
    _L1_ffn_in = {k: v for k, v in _L1_ffn_all.items() if k in ('router_w', 'router_b', 'w1', 'b1', 'w2', 'b2')}
    del _L1_ffn_all
    return {'x': x, 'L0_tok_emb_table': _L0_tok_in['emb_table'], 'L0_tok_proj_w': _L0_tok_in['proj_w'], 'L0_tok_proj_b': _L0_tok_in['proj_b'], 'L0_attn_q_w': _L0_attn_in['q_w'], 'L0_attn_kv_w': _L0_attn_in['kv_w'], 'L0_ffn_input_patterns': _L0_ffn_in['input_patterns'], 'L0_ffn_process_input_weights': _L0_ffn_in['process_input_weights'], 'L0_ffn_process_values': _L0_ffn_in['process_values'], 'L0_ffn_output_input_weights': _L0_ffn_in['output_input_weights'], 'L0_ffn_output_patterns': _L0_ffn_in['output_patterns'], 'L1_attn_Wq': _L1_attn_in['Wq'], 'L1_attn_Wk': _L1_attn_in['Wk'], 'L1_attn_Wv': _L1_attn_in['Wv'], 'L1_attn_Wg': _L1_attn_in['Wg'], 'L1_attn_bg': _L1_attn_in['bg'], 'L1_attn_A': _L1_attn_in['A'], 'L1_attn_sink': _L1_attn_in['sink'], 'L1_attn_v_null': _L1_attn_in['v_null'], 'L1_ffn_router_w': _L1_ffn_in['router_w'], 'L1_ffn_router_b': _L1_ffn_in['router_b'], 'L1_ffn_w1': _L1_ffn_in['w1'], 'L1_ffn_b1': _L1_ffn_in['b1'], 'L1_ffn_w2': _L1_ffn_in['w2'], 'L1_ffn_b2': _L1_ffn_in['b2']}

def reference(x, L0_tok_emb_table, L0_tok_proj_w, L0_tok_proj_b, L0_attn_q_w, L0_attn_kv_w, L0_ffn_input_patterns, L0_ffn_process_input_weights, L0_ffn_process_values, L0_ffn_output_input_weights, L0_ffn_output_patterns, L1_attn_Wq, L1_attn_Wk, L1_attn_Wv, L1_attn_Wg, L1_attn_bg, L1_attn_A, L1_attn_sink, L1_attn_v_null, L1_ffn_router_w, L1_ffn_router_b, L1_ffn_w1, L1_ffn_b1, L1_ffn_w2, L1_ffn_b2):
    import jax
    import jax.numpy as jnp

    def _L0_tok_ref(input_ids, emb_table, proj_w, proj_b):
        import jax, jax.numpy as jnp
        import numpy as np
        VOCAB = 16
        D_MODEL = 128
        D_EMB = int(D_MODEL * 0.7)
        D_STFT = D_MODEL - D_EMB
        N_FFT = 64
        HOP = 64
        N_FREQ = N_FFT // 2 + 1
        B, L = (4, 2048)

        def _stft_mag(signal):
            pad = N_FFT // 2
            padded = jnp.pad(signal, ((0, 0), (pad, pad)), mode='reflect')
            n_frames = signal.shape[1] // HOP + 1
            idx = jnp.arange(n_frames)[:, None] * HOP + jnp.arange(N_FFT)[None, :]
            window = 0.5 - 0.5 * jnp.cos(2.0 * jnp.pi * jnp.arange(N_FFT) / N_FFT)
            frames = padded[:, idx] * window.astype(signal.dtype)
            return jnp.abs(jnp.fft.rfft(frames, axis=-1))
        b, seq_len = input_ids.shape
        word_embeds = emb_table[input_ids]
        onehot = jax.nn.one_hot(input_ids, VOCAB, dtype=jnp.float32)
        signal = onehot.transpose(0, 2, 1).reshape(b * VOCAB, seq_len)
        spec = _stft_mag(signal)
        n_frames = spec.shape[1]
        stft_mag = spec.reshape(b, VOCAB, n_frames, N_FREQ).transpose(0, 1, 3, 2)
        stft_to_up = stft_mag.transpose(0, 2, 1, 3).reshape(b, N_FREQ * VOCAB, n_frames)
        up_idx = jnp.arange(seq_len) * n_frames // seq_len
        stft_up = stft_to_up[:, :, up_idx]
        feats = stft_up.transpose(0, 2, 1)
        stft_enc = jnp.einsum('bli,io->blo', feats, proj_w) + proj_b
        return jnp.concatenate([word_embeds, stft_enc], axis=-1)

    def _L0_attn_ref(x, q_w, kv_w):
        import jax, jax.numpy as jnp
        import numpy as np
        NUM_HEADS = 8
        B, N, C = x.shape
        H = NUM_HEADS
        D = C // H
        halfB = B // 2
        q = (x @ q_w.T).reshape(B, N, H, D)
        kv = (x @ kv_w.T).reshape(B, N, 2, H, D)
        k, v = (kv[:, :, 0], kv[:, :, 1])
        k = jnp.concatenate([k[halfB:], k[:halfB]], axis=0)
        v = jnp.concatenate([v[halfB:], v[:halfB]], axis=0)
        scores = jnp.einsum('bnhd,bmhd->bhnm', q, k) / jnp.sqrt(jnp.float32(C))
        prob = jax.nn.softmax(scores, axis=-1)
        out = jnp.einsum('bhnm,bmhd->bndh', prob, v).reshape(B, N, C)
        return out

    def _L0_ffn_ref(x, input_patterns, process_input_weights, process_values, output_input_weights, output_patterns):
        import jax, jax.numpy as jnp
        import numpy as np
        K_INPUT, K_PROCESS, K_OUTPUT = (64, 128, 64)

        def _gelu(x):
            return jax.nn.gelu(x, approximate=False)
        B, S, d_model = x.shape
        n_in = input_patterns.shape[0]
        input_acts = _gelu(jnp.einsum('bsd,nd->bsn', x, input_patterns))
        top_in_acts, top_in_idx = jax.lax.top_k(input_acts, K_INPUT)
        bi = jnp.arange(B)[:, None, None]
        si = jnp.arange(S)[None, :, None]
        input_repr = jnp.zeros((B, S, n_in), dtype=x.dtype).at[bi, si, top_in_idx].set(top_in_acts)
        process_acts = _gelu(jnp.einsum('bsn,pn->bsp', input_repr, process_input_weights))
        top_p_acts, top_p_idx = jax.lax.top_k(process_acts, K_PROCESS)
        sel_values = process_values[top_p_idx]
        p_weights = jax.nn.softmax(top_p_acts, axis=-1)
        agg_value = jnp.einsum('bsk,bskd->bsd', p_weights, sel_values)
        output_acts = _gelu(jnp.einsum('bsd,od->bso', agg_value, output_input_weights))
        top_o_acts, top_o_idx = jax.lax.top_k(output_acts, K_OUTPUT)
        sel_patterns = output_patterns[top_o_idx]
        out = jnp.einsum('bsk,bskm->bsm', top_o_acts, sel_patterns)
        return out

    def _L1_attn_ref(x, Wq, Wk, Wv, Wg, bg, A, sink, v_null):
        import jax, jax.numpy as jnp
        import numpy as np
        B, T, C, DH, CS = (8, 512, 128, 128, 64)

        def _forward(x, Wq, Wk, Wv, Wg, bg, A, sink, v_null):
            b, t, c = x.shape
            dh = Wq.shape[0]
            nc = t // CS
            scale = dh ** (-0.5)
            q = (x @ Wq.T)[:, None]
            k = (x @ Wk.T)[:, None]
            v = (x @ Wv.T)[:, None]
            g = jax.nn.sigmoid(x @ Wg.T + bg)[:, None]

            def to_chunks(a):
                return a.reshape(b, 1, nc, CS, dh).transpose(2, 0, 1, 3, 4)
            qc, kc, gc = (to_chunks(q), to_chunks(k), to_chunks(g))
            hist0 = jnp.zeros((b, 1, nc, dh), x.dtype)
            last0 = jnp.zeros((b, 1, dh), x.dtype)
            chunk_ids = jnp.arange(nc)

            def step(carry, inp):
                hist, last = carry
                i, qi, ki, gi = inp
                scores = jnp.einsum('bhcd,bhnd->bhcn', ki, hist) * scale
                valid = jnp.arange(nc) < i
                w = jax.nn.softmax(jnp.where(valid, scores, -1e+30), axis=-1)
                q_retr = jnp.einsum('bhcn,bhnd->bhcd', w, hist)
                q_init = jnp.where(i > 0, last[:, :, None, :] + q_retr, 0.0)
                q_out = jnp.cumsum(gi * qi, axis=2) + q_init
                final = q_out[:, :, -1, :]
                hist = hist.at[:, :, i, :].set(final)
                return ((hist, final), q_out)
            _, q_chunks = jax.lax.scan(step, (hist0, last0), (chunk_ids, qc, kc, gc))
            Qc = q_chunks.transpose(1, 2, 0, 3, 4).reshape(b, 1, t, dh)
            mean_s = 0.5 * (Qc.mean(-1, keepdims=True) + k.mean(-1, keepdims=True))
            std_s = 0.5 * (jnp.std(Qc, -1, keepdims=True, ddof=1) + jnp.std(k, -1, keepdims=True, ddof=1))
            Qn = (Qc - mean_s) / (std_s + 1e-06)
            Kn = (k - mean_s) / (std_s + 1e-06)
            inv_freq = 1.0 / 10000.0 ** (jnp.arange(0, dh, 2, dtype=jnp.float32) / dh)
            freqs = jnp.arange(t, dtype=jnp.float32)[:, None] * inv_freq[None, :]
            cos, sin = (jnp.cos(freqs), jnp.sin(freqs))

            def rope(a):
                x1, x2 = (a[..., 0::2], a[..., 1::2])
                return jnp.concatenate([-x2 * sin + x1 * cos, x1 * sin + x2 * cos], axis=-1)
            S = A - jnp.swapaxes(A, -1, -2)

            def wedge(a):
                return a + jnp.einsum('bhtd,hde->bhte', a, S)
            Qg, Kg = (wedge(rope(Qn)), wedge(rope(Kn)))
            attn = jnp.einsum('bhtd,bhsd->bhts', Qg, Kg) * scale
            causal = jnp.tril(jnp.ones((t, t), bool))
            attn = jnp.where(causal, attn, -jnp.inf)
            sink_col = jnp.broadcast_to(sink, (b, 1, t, 1))
            probs = jax.nn.softmax(jnp.concatenate([attn, sink_col], axis=-1), axis=-1)
            out = probs[..., :t] @ v + probs[..., t:] * v_null
            return out.transpose(0, 2, 1, 3).reshape(b, t, c)
        return _forward(x, Wq, Wk, Wv, Wg, bg, A, sink, v_null)

    def _L1_ffn_ref(x, router_w, router_b, w1, b1, w2, b2):
        import jax, jax.numpy as jnp
        import numpy as np
        from jax import lax
        N_EXPERTS = 16
        TOP_K = 2
        D_MODEL = 128
        D_FF = 512
        B, S, D = x.shape
        xt = x.reshape(-1, D)
        logits = xt @ router_w.T + router_b
        probs = jax.nn.softmax(logits, axis=-1)
        topk_p, topk_i = lax.top_k(probs, TOP_K)
        onehot = jax.nn.one_hot(topk_i, N_EXPERTS, dtype=probs.dtype)
        gates = jnp.sum(onehot * topk_p[..., None], axis=1)

        def expert_step(acc, packed):
            w1e, b1e, w2e, b2e, ge = packed
            h = jax.nn.gelu(xt @ w1e.T + b1e, approximate=False)
            y = h @ w2e.T + b2e
            return (acc + y * ge[:, None], None)
        out, _ = lax.scan(expert_step, jnp.zeros_like(xt), (w1, b1, w2, b2, gates.T))
        return out.reshape(B, S, D)
    h = _L0_tok_ref(x, L0_tok_emb_table, L0_tok_proj_w, L0_tok_proj_b)
    h = h + _L0_attn_ref(_layernorm(h, axis=-1), L0_attn_q_w, L0_attn_kv_w)
    h = h + _L0_ffn_ref(_layernorm(h, axis=-1), L0_ffn_input_patterns, L0_ffn_process_input_weights, L0_ffn_process_values, L0_ffn_output_input_weights, L0_ffn_output_patterns)
    h = h + _L1_attn_ref(_layernorm(h, axis=-1), L1_attn_Wq, L1_attn_Wk, L1_attn_Wv, L1_attn_Wg, L1_attn_bg, L1_attn_A, L1_attn_sink, L1_attn_v_null)
    h = h + _L1_ffn_ref(_layernorm(h, axis=-1), L1_ffn_router_w, L1_ffn_router_b, L1_ffn_w1, L1_ffn_b1, L1_ffn_w2, L1_ffn_b2)
    return h

_drawn_inputs = setup_inputs


def setup_inputs(seed=0):
    import zlib

    import numpy as np

    out = dict(_drawn_inputs(seed))
    spreads = {'L0_tok_proj_b': (0.0, 0.1)}
    factors = {'L0_attn_q_w': 8.0,
     'L0_ffn_input_patterns': 8.0,
     'L0_ffn_process_input_weights': 8.0,
     'L0_ffn_process_values': 8.0,
     'L0_ffn_output_input_weights': 8.0,
     'L0_ffn_output_patterns': 8.0,
     'L1_attn_Wg': 63.4,
     'L1_attn_bg': 64.0,
     'L1_attn_A': 60.928,
     'L1_attn_v_null': 64.0,
     'L1_ffn_router_b': 21.736,
     'L1_ffn_b1': 56.384,
     'L1_ffn_b2': 39.696,
     'L1_attn_Wq': 6.818,
     'L1_attn_Wk': 6.84,
     'L1_attn_Wv': 3.708,
     'L1_ffn_router_w': 8.0,
     'L1_ffn_w1': 8.0,
     'L1_ffn_w2': 8.0}
    for name, (base, spread) in spreads.items():
        noise = np.random.default_rng([zlib.crc32(name.encode()), seed]).standard_normal(out[name].shape)
        drawn = base * np.exp(spread * noise) if base else spread * noise
        out[name] = jnp.asarray(drawn.astype(out[name].dtype))
    for name, factor in factors.items():
        out[name] = (out[name] * factor).astype(out[name].dtype)
    return out
```

```python
import numpy as np
import concourse.bass as bass
from concourse import mybir
from contextlib import ExitStack

P = 128
B = 32
C = 128
V = 16
D_EMB, D_STFT = 89, 39
NFREQ, NFRAME = 33, 3
H, DH = 8, 16
HG = 4
N_IN, N_PROC, N_OUT, D_PV = 512, 256, 512, 64
K_IN, K_PROC, K_OUT = 64, 128, 64
E, FF, TOPK = 16, 512, 2
NC1 = FF // P
SLOTS = (B * P * TOPK + E * (P - 1)) // P + 1
SLOTS += SLOTS % 2
LN_EPS = 1e-5
GONE = -1e30
BIG = 1e30
PAIRS = B // 2


def take(eng, sem, n=1):
    eng.wait_ge(sem, n)
    eng.sem_inc(sem, -n)


def build(nc, a, out):
    f32, i32 = mybir.dt.float32, mybir.dt.int32
    ALU, ACT, AX = mybir.AluOpType, mybir.ActivationFunctionType, mybir.AxisListType
    xs_dram = nc.dram_tensor("xs_rows", (SLOTS * P, C), f32, kind="Internal").ap()
    ys_dram = nc.dram_tensor("ys_rows", (SLOTS * P, C), f32, kind="Internal").ap()

    with ExitStack() as ctx:
        def sb(name, shape, dt=f32, stack=ctx):
            return stack.enter_context(nc.sbuf_tensor(name, shape, dt))

        def sem(name):
            return ctx.enter_context(nc.semaphore(name))

        pbank = [ctx.enter_context(nc.psum_tensor(f"bank{i}", [P, 512], f32)) for i in range(4)]
        quad = ctx.enter_context(nc.psum_tensor("quad", [P, 4, 512], f32))
        bank = pbank + [quad[:, i, :] for i in range(4)]

        h = sb("h", [P, B, C])
        ident = sb("ident", [P, P])
        w_q = sb("w_q", [P, 2, HG, 32])
        w_k = sb("w_k", [P, 2, HG, 32])
        w_v = sb("w_v", [P, C])
        in_pat = sb("in_pat", [P, N_IN])
        proc_w = sb("proc_w", [P, N_IN // P, N_PROC])
        proc_v = sb("proc_v", [P, N_PROC // P, D_PV])
        out_w = sb("out_w", [D_PV, N_OUT])
        out_pat = sb("out_pat", [P, N_OUT // P, C])
        w_qkvg = sb("w_qkvg", [P, 4 * C])
        bg_rows = sb("bg_rows", [P, C])
        a_m = sb("a_m", [P, C])
        a_t = sb("a_t", [P, C])
        sink_c = sb("sink_c", [P, 1])
        vnull_rows = sb("vnull_rows", [P, C])
        cos_t = sb("cos_t", [P, 64])
        sin_t = sb("sin_t", [P, 64])
        run_sum = sb("run_sum", [P, P])
        causal = sb("causal", [P, P])
        w2_all = sb("w2_all", [P, E, NC1, C])
        r_w = sb("r_w", [P, E])
        rb_rows = sb("rb_rows", [P, E])
        b2_blocks = sb("b2_blocks", [P, 8, C])
        tri = sb("tri", [P, P])
        ones = sb("ones", [P, P])
        eid = sb("eid", [P, E])
        jid = sb("jid", [P, SLOTS])
        cst = sb("cst", [P, 4])

        stats = sb("stats", [P, 2, 6])
        mv = sb("mv", [P, 2, 2])
        rstd = sb("rstd", [P, 2, 1])
        xn = sb("xn", [P, 2, C])
        xT = sb("xT", [P, 2, C])

        load_names = ["w", "pad", "ids"]
        s_load = {n: sem("loaded_" + n) for n in load_names}
        s_chain = sem("dve_done")
        s_pchain = sem("pool_done")
        s_achain = sem("act_done")

        def link(eng, chain, ins):
            ins.then_inc(chain, 1)
            take(eng, chain)

        with ExitStack() as ph:
            ids_c = sb("ids_c", [P, B], i32, ph)
            ids_r = sb("ids_r", [V, B * P], i32, ph)
            hot = sb("hot", [P, B, V], f32, ph)
            hotT = sb("hotT", [V, B * P], f32, ph)
            emb = sb("emb", [V, D_EMB], f32, ph)
            dft = sb("dft", [P, 2 * NFRAME, NFREQ], f32, ph)
            sq = sb("sq", [NFREQ, 2, NFRAME, B * V], f32, ph)
            mag = sb("mag", [NFREQ, NFRAME, B, V], f32, ph)
            pw = sb("pw", [NFREQ, V, D_STFT], f32, ph)
            pb = sb("pb", [NFRAME * B, D_STFT], f32, ph)
            enc = sb("enc", [NFRAME * B, D_STFT], f32, ph)
            encF = sb("encF", [NFRAME, B, D_STFT], f32, ph)
            up = sb("up", [NFRAME, P], f32, ph)
            s_zeroed, s_hot, s_spec, s_sq, s_sum, s_mag, s_enc, s_encs, s_encf = (sem(n) for n in (
                "zeroed", "hot_ready", "spectra_ready", "squares_ready", "power_ready", "mag_ready",
                "enc_ready", "enc_rows_ready", "enc_frames_ready"))
            s_emb, s_embc, s_ide = sem("emb_ready"), sem("emb_copied"), sem("stft_ready")
            s_fill = sem("rows_cleared")
            zrow = sb("zrow", [P, SLOTS * C // 8], f32, ph)
            with nc.Block() as block:
                @block.sync
                def _(sp):
                    loads = [(ids_c[:, :], a["idsT"]), (ids_r[:, :], a["ids"].partition_broadcast(V)),
                             (emb[:, :], a["emb"]), (dft[:, :, :], a["dft"]), (pw[:, :, :], a["pw"]),
                             (pb[:, :], a["pb"].partition_broadcast(NFRAME * B)), (up[:, :], a["up"]),
                             (eid[:, :], a["eid"].partition_broadcast(P)), (cst[:, :], a["cst"]),
                             (ident[:, :], a["ident"])]
                    for dst, src in loads:
                        sp.dma_start(dst, src).then_inc(s_load["ids"], 16)
                    rest = [(in_pat[:, :], a["in_pat"]), (proc_w[:, :, :], a["proc_w"]), (proc_v[:, :, :], a["proc_v"]),
                            (w_v[:, :], a["w_v"]), (out_w[:, :], a["out_w"]), (out_pat[:, :, :], a["out_pat"]),
                            (w_qkvg[:, :], a["w_qkvg"]), (bg_rows[:, :], a["bg"].partition_broadcast(P)),
                            (a_m[:, :], a["A"]), (a_t[:, :], a["AT"]), (sink_c[:, :], a["sink"].partition_broadcast(P)),
                            (vnull_rows[:, :], a["v_null"].partition_broadcast(P)), (cos_t[:, :], a["cos"]),
                            (sin_t[:, :], a["sin"]), (run_sum[:, :], a["run_sum"]), (causal[:, :], a["causal"]),
                            (r_w[:, :], a["r_w"]), (rb_rows[:, :], a["r_b"].partition_broadcast(P)),
                            (tri[:, :], a["tri"]), (jid[:, :], a["jid"].partition_broadcast(P)),
                            (w2_all[:, :, :, :], a["w2"])]
                    sp.wait_ge(s_zeroed, 5)
                    for g in range(2):
                        for w, src in ((w_q, a["w_q"]), (w_k, a["w_k"])):
                            rest.append((w[:, g, :, 0:DH], src[:, g, :, :]))
                    for t in range(8):
                        rest.append((b2_blocks[E * t:E * t + E, t, :], a["b2"]))
                    for dst, src in rest:
                        sp.dma_start(dst, src).then_inc(s_load["w"], 16)
                    for q in range(8):
                        sp.dma_start(xs_dram.rearrange("(q p r) c -> q p (r c)", q=8, p=P)[q], zrow[:, :]).then_inc(s_fill, 16)
                    take(sp, s_encs)
                    for f in range(NFRAME):
                        sp.dma_start(encF[f:f + 1, :, :].rearrange("f b e -> (f b) e") if False else encF[f:f + 1, :, :], enc[B * f:B * f + B, :]).then_inc(s_encf, 16)
                    sp.wait_ge(s_load["w"], 16 * len(rest))
                    sp.wait_ge(s_fill, 16 * 8)

                @block.gpsimd
                def _(pool):
                    nc.gpsimd.memset(w_q[:, :, :, :], 0.0).then_inc(s_zeroed, 1)
                    nc.gpsimd.memset(w_k[:, :, :, :], 0.0).then_inc(s_zeroed, 1)
                    nc.gpsimd.memset(b2_blocks[:, :, :], 0.0).then_inc(s_zeroed, 1)
                    nc.gpsimd.memset(ones[:, :], 1.0).then_inc(s_zeroed, 1)
                    nc.gpsimd.memset(zrow[:, :], 0.0).then_inc(s_zeroed, 1)

                @block.vector
                def _(dve):
                    dve.wait_ge(s_load["ids"], 16 * 10)
                    nc.vector.tensor_tensor(hot[:, :, :], ids_c[:, :].unsqueeze(2).to_broadcast([P, B, V]),
                                            eid[:, :].unsqueeze(1).to_broadcast([P, B, V]), ALU.is_equal).then_inc(s_hot, 1)
                    nc.vector.tensor_scalar(hotT[:, :], ids_r[:, :], cst[0:V, 3:4], None, ALU.is_equal).then_inc(s_hot, 1)
                    dve.wait_ge(s_sq, 6)
                    nc.vector.tensor_tensor(mag[:, :, :, :].rearrange("f a b v -> f a (b v)"), sq[:, 0, :, :], sq[:, 1, :, :], ALU.add).then_inc(s_sum, 1)
                    take(dve, s_enc)
                    nc.vector.tensor_tensor(enc[:, :], bank[6][0:NFRAME * B, 0:D_STFT], pb[:, :], ALU.add).then_inc(s_encs, 1)
                    for g in range(B // 4):
                        take(dve, s_emb)
                        nc.vector.tensor_copy(h[:, 4 * g:4 * g + 4, 0:D_EMB],
                                              bank[g % 2][:, 0:4 * D_EMB].rearrange("p (b e) -> p b e", b=4)).then_inc(s_embc, 1)

                @block.scalar
                def _(act):
                    for f in range(2 * NFRAME):
                        take(act, s_spec)
                        nc.scalar.activation(sq[:, f // NFRAME, f % NFRAME, :], bank[2 + f % 4][0:NFREQ, :], ACT.Square).then_inc(s_sq, 1)
                    take(act, s_sum)
                    nc.scalar.activation(mag[:, :, :, :], mag[:, :, :, :], ACT.Sqrt).then_inc(s_mag, 1)
                    for g in range(4):
                        take(act, s_ide)
                        nc.scalar.activation(h[:, 8 * g:8 * g + 8, D_EMB:C],
                                             bank[2 + g][:, 0:8 * D_STFT].rearrange("p (b e) -> p b e", b=8), ACT.Copy).then_inc(s_achain, 1)
                    take(act, s_achain, 4)

                @block.tensor
                def _(pe):
                    pe.wait_ge(s_load["ids"], 16 * 10)
                    pe.wait_ge(s_hot, 2)
                    for f in range(2 * NFRAME):
                        if f >= 4:
                            pe.wait_ge(s_sq, f - 3)
                        nc.tensor.matmul(bank[2 + f % 4][0:NFREQ, :], dft[:, f, :], hot[:, :, :], start=True, stop=True).then_inc(s_spec, 1)
                    take(pe, s_mag)
                    for v in range(V):
                        m = nc.tensor.matmul(bank[6][0:NFRAME * B, 0:D_STFT], mag[:, :, :, v], pw[:, v, :], start=(v == 0), stop=(v == V - 1))
                    m.then_inc(s_enc, 1)
                    for g in range(B // 4):
                        if g >= 2:
                            pe.wait_ge(s_embc, g - 1)
                        for b in range(4):
                            t = 4 * g + b
                            m = nc.tensor.matmul(bank[g % 2][:, b * D_EMB:(b + 1) * D_EMB], hotT[:, t * P:(t + 1) * P], emb[:, :], start=True, stop=True)
                        m.then_inc(s_emb, 1)
                    pe.wait_ge(s_encf, 16 * NFRAME)
                    for g in range(4):
                        nc.tensor.matmul(bank[2 + g][:, 0:8 * D_STFT], up[:, :], encF[:, 8 * g:8 * g + 8, :], start=True, stop=True).then_inc(s_ide, 1)

        s_ve, s_rstd, s_xn, s_xTp, s_xT = sem("variance_ready"), sem("rstd_ready"), sem("xn_ready"), sem("xT_in_psum"), sem("xT_ready")

        def norm_stats(dve, s, rows):
            link(dve, s_chain, nc.vector.bn_stats(stats[:, s, :], rows))
            link(dve, s_chain, nc.vector.bn_aggr(mv[:, s, :], stats[:, s, :]))
            nc.vector.tensor_scalar(mv[:, s, 1:2], mv[:, s, 1:2], LN_EPS, None, ALU.add).then_inc(s_ve, 1)

        def norm_rows(dve, s, rows, dst):
            take(dve, s_rstd)
            nc.vector.tensor_scalar(dst, rows, mv[:, s, 0:1], rstd[:, s, :], ALU.subtract, ALU.mult).then_inc(s_xn, 1)

        def norm_power(pool, s):
            take(pool, s_ve)
            nc.gpsimd.tensor_tensor(rstd[:, s, :], mv[:, s, 1:2], cst[:, 0:1], ALU.pow).then_inc(s_rstd, 1)

        with ExitStack() as ph:
            qk = sb("qk", [P, 4, 2, P], f32, ph)
            va = sb("va", [P, 2, H, DH + 1], f32, ph)
            pr = sb("pr", [P, 2, H, P], f32, ph)
            prT = sb("prT", [P, 2, H, P], f32, ph)
            mx = sb("mx", [P, 2, H], f32, ph)
            rd = sb("rd", [P, 2, H], f32, ph)
            ao = sb("ao", [P, 2, DH, H], f32, ph)
            s_qk, s_qkc, s_vp, s_vc, s_sc, s_sub, s_ex, s_tp, s_tc, s_o = (sem(n) for n in (
                "qk_in_psum", "qk_ready", "v_in_psum", "v_ready", "scores_ready", "shifted_ready", "exp_ready",
                "probsT_in_psum", "probsT_ready", "attn_ready"))
            s_scf = sem("scores_read")
            with nc.Block() as block:
                @block.vector
                def _(dve):
                    link(dve, s_chain, nc.vector.memset(va[:, :, :, :], 1.0))
                    with dve.Fori(0, PAIRS) as i:
                        ti = [i, i + PAIRS]
                        for s in range(2):
                            norm_stats(dve, s, h[:, bass.ds(ti[s], 1), :])
                        for s in range(2):
                            norm_rows(dve, s, h[:, bass.ds(ti[s], 1), :], xn[:, s, :])
                        take(dve, s_vp)
                        nc.vector.tensor_copy(va[:, :, :, 0:DH], bank[2][:, 256:512].rearrange("p (s h d) -> p s h d", s=2, h=H)).then_inc(s_vc, 1)
                        for s in range(2):
                            take(dve, s_sc)
                            sc = quad[:, :, 0:256].rearrange("p r (g m) -> p r g m", g=2)
                            link(dve, s_chain, nc.vector.tensor_reduce(mx[:, s, :].rearrange("p (r g) -> p r g", r=HG), sc, AX.X, ALU.max))
                            nc.vector.tensor_tensor(pr[:, s, :, :].rearrange("p (r g) m -> p r g m", r=HG), sc,
                                                    mx[:, s, :].rearrange("p (r g) -> p r g", r=HG).unsqueeze(3).to_broadcast([P, HG, 2, P]),
                                                    ALU.subtract).then_inc(s_sub, 1)
                        for s in range(2):
                            take(dve, s_o)
                            o = bank[2 + s][:, 0:136].rearrange("p (h e) -> p h e", h=H)
                            link(dve, s_chain, nc.vector.reciprocal(rd[:, s, :], o[:, :, DH]))
                            link(dve, s_chain, nc.vector.tensor_tensor(ao[:, s, :, :].rearrange("p d h -> p h d"), o[:, :, 0:DH],
                                                                       rd[:, s, :].unsqueeze(2).to_broadcast([P, H, DH]), ALU.mult))
                            hr = h[:, bass.ds(ti[s], 1), :]
                            link(dve, s_chain, nc.vector.tensor_tensor(hr, hr, ao[:, s:s + 1, :, :].rearrange("p s d h -> p s (d h)"), ALU.add))

                @block.gpsimd
                def _(pool):
                    with pool.Fori(0, PAIRS) as i:
                        for s in range(2):
                            norm_power(pool, s)

                @block.scalar
                def _(act):
                    with act.Fori(0, PAIRS) as i:
                        take(act, s_xTp)
                        nc.scalar.activation(xT[:, :, :], bank[2][:, 0:256].rearrange("p (s t) -> p s t", s=2), ACT.Copy).then_inc(s_xT, 1)
                        for n in range(2):
                            take(act, s_qk)
                            nc.scalar.activation(qk[:, 2 * n:2 * n + 2, :, :], bank[n][:, :].rearrange("p (g s t) -> p g s t", g=2, s=2), ACT.Copy).then_inc(s_qkc, 1)
                        for s in range(2):
                            take(act, s_sub)
                            nc.scalar.activation(pr[:, s, :, :], pr[:, s, :, :], ACT.Exp, scale=float(C) ** -0.5).then_inc(s_ex, 1)
                            for n in range(2):
                                take(act, s_tp)
                                nc.scalar.activation(prT[:, s, 4 * n:4 * n + 4, :], bank[n][:, :].rearrange("p (h t) -> p h t", h=4), ACT.Copy).then_inc(s_tc, 1)

                def attend(pe, s):
                    for n in range(2):
                        for x in range(4):
                            m = nc.tensor.transpose(bank[n][:, x * P:(x + 1) * P], pr[:, s, 4 * n + x, :], ident[:, :])
                        m.then_inc(s_tp, 1)
                    if s == 0:
                        take(pe, s_vc)
                    take(pe, s_tc, 2)
                    for x in range(H):
                        r, g = x // 2, x % 2
                        hd = g * HG + r
                        m = nc.tensor.matmul(bank[2 + s][:, hd * 17:hd * 17 + 17], prT[:, s, x, :], va[:, 1 - s, hd, :], start=True, stop=True)
                    m.then_inc(s_o, 1)

                @block.tensor
                def _(pe):
                    with pe.Fori(0, PAIRS) as i:
                        for s in range(2):
                            take(pe, s_xn)
                            m = nc.tensor.transpose(bank[2][:, s * P:(s + 1) * P], xn[:, s, :], ident[:, :])
                        m.then_inc(s_xTp, 1)
                        take(pe, s_xT)
                        for n, w in enumerate((w_q, w_k)):
                            for g in range(2):
                                m = nc.tensor.matmul(bank[n][:, g * 256:(g + 1) * 256], w[:, g, :, :], xT[:, :, :], start=True, stop=True)
                            m.then_inc(s_qk, 1)
                        for s in range(2):
                            m = nc.tensor.matmul(bank[2][:, 256 + s * P:256 + (s + 1) * P], xT[:, s, :], w_v[:, :], start=True, stop=True)
                        m.then_inc(s_vp, 1)
                        take(pe, s_qkc, 2)
                        for s in range(2):
                            if s:
                                take(pe, s_ex)
                            for g in range(2):
                                for r in range(HG):
                                    m = nc.tensor.matmul(quad[:, r, g * P:(g + 1) * P], qk[32 * r:32 * r + 32, g, s, :],
                                                         qk[32 * r:32 * r + 32, 2 + g, 1 - s, :], start=True, stop=True)
                            m.then_inc(s_sc, 1)
                            if s:
                                attend(pe, 0)
                        take(pe, s_ex)
                        attend(pe, 1)

        with ExitStack() as ph:
            act1 = sb("act1", [P, 2, N_IN], f32, ph)
            act2 = sb("act2", [P, 2, N_PROC], f32, ph)
            ex2 = sb("ex2", [P, 2, N_PROC], f32, ph)
            left = sb("left", [P, 2, N_IN], f32, ph)
            kept = sb("kept", [P, 2, N_IN], f32, ph)
            keptT = sb("keptT", [P, 2, N_IN // P, P], f32, ph)
            aggT = sb("aggT", [D_PV, 2, P], f32, ph)
            top8 = sb("top8", [P, 2, 8], f32, ph)
            nmax = sb("nmax", [P, 2, 1], f32, ph)
            psumr = sb("psumr", [P, 2, 1], f32, ph)
            rden = sb("rden", [P, 2, 1], f32, ph)
            s_a1p, s_a1, s_kept, s_ktp, s_kt, s_prp, s_a2, s_nm, s_ex2, s_agp, s_ag, s_a3p, s_a3, s_op = (sem(n) for n in (
                "in_acts_psum", "acts_ready", "kept_ready", "keptT_psum", "keptT_ready", "proc_psum", "proc_ready", "proc_max",
                "proc_exp", "agg_psum", "agg_ready", "out_acts_psum", "out_acts_ready", "ffn_psum"))

            def topk(dve, s, k, acts, n):
                src = acts
                for r in range(k // 8):
                    link(dve, s_chain, nc.vector.max(top8[:, s, :], src))
                    if r == 0 and n == N_PROC:
                        nc.vector.tensor_scalar(nmax[:, s, :], top8[:, s, 0:1], -1.0, None, ALU.mult).then_inc(s_nm, 1)
                    link(dve, s_chain, nc.vector.match_replace(left[:, s, 0:n], top8[:, s, :], src, GONE))
                    src = left[:, s, 0:n]

            with nc.Block() as block:
                @block.vector
                def _(dve):
                    with dve.Fori(0, PAIRS) as i:
                        for s in range(2):
                            norm_stats(dve, s, h[:, bass.ds(2 * i + s, 1), :])
                        for s in range(2):
                            norm_rows(dve, s, h[:, bass.ds(2 * i + s, 1), :], xn[:, s, :])
                        for s in range(2):
                            take(dve, s_a1)
                            topk(dve, s, K_IN, act1[:, s, :], N_IN)
                            nc.vector.scalar_tensor_tensor(kept[:, s, :], left[:, s, :], GONE, act1[:, s, :], ALU.is_equal, ALU.mult).then_inc(s_kept, 1)
                        for s in range(2):
                            take(dve, s_a2)
                            topk(dve, s, K_PROC, act2[:, s, :], N_PROC)
                            take(dve, s_ex2)
                            link(dve, s_chain, nc.vector.scalar_tensor_tensor(kept[:, s, 0:N_PROC], left[:, s, 0:N_PROC], GONE, ex2[:, s, :],
                                                                              ALU.is_equal, ALU.mult, accum_out=psumr[:, s, :]))
                            nc.vector.reciprocal(rden[:, s, :], psumr[:, s, :]).then_inc(s_kept, 1)
                        for s in range(2):
                            take(dve, s_a3)
                            topk(dve, s, K_OUT, act1[:, s, :], N_OUT)
                            nc.vector.scalar_tensor_tensor(kept[:, s, :], left[:, s, :], GONE, act1[:, s, :], ALU.is_equal, ALU.mult).then_inc(s_kept, 1)
                        for s in range(2):
                            take(dve, s_op)
                            hr = h[:, bass.ds(2 * i + s, 1), :]
                            link(dve, s_chain, nc.vector.tensor_tensor(hr, hr, bank[3 * s + 2][:, 0:P].unsqueeze(1), ALU.add))

                @block.gpsimd
                def _(pool):
                    with pool.Fori(0, PAIRS) as i:
                        for s in range(2):
                            norm_power(pool, s)

                @block.scalar
                def _(act):
                    with act.Fori(0, PAIRS) as i:
                        for s in range(2):
                            take(act, s_xTp)
                            nc.scalar.activation(xT[:, s, :], bank[3 * s + 2][:, 0:P], ACT.Copy).then_inc(s_xT, 1)
                        for s in range(2):
                            take(act, s_a1p)
                            nc.scalar.activation(act1[:, s, :], bank[3 * s][:, :], ACT.Gelu).then_inc(s_a1, 1)
                        for s in range(2):
                            take(act, s_ktp)
                            nc.scalar.activation(keptT[:, s, :, :], bank[3 * s + 1][:, :].rearrange("p (c t) -> p c t", c=4), ACT.Copy).then_inc(s_kt, 1)
                            take(act, s_prp)
                            nc.scalar.activation(act2[:, s, :], bank[3 * s + 2][:, P:P + N_PROC], ACT.Gelu).then_inc(s_a2, 1)
                        for s in range(2):
                            take(act, s_nm)
                            nc.scalar.activation(ex2[:, s, :], act2[:, s, :], ACT.Exp, bias=nmax[:, s, :]).then_inc(s_ex2, 1)
                            take(act, s_ktp)
                            nc.scalar.activation(keptT[:, s, 0:2, :], bank[3 * s + 1][:, 0:256].rearrange("p (c t) -> p c t", c=2), ACT.Copy).then_inc(s_kt, 1)
                            take(act, s_agp)
                            nc.scalar.activation(aggT[:, s, :], bank[3 * s + 2][0:D_PV, 384:512], ACT.Copy).then_inc(s_ag, 1)
                            take(act, s_a3p)
                            nc.scalar.activation(act1[:, s, :], bank[3 * s][:, :], ACT.Gelu, scale=rden[:, s, :]).then_inc(s_a3, 1)
                        for s in range(2):
                            take(act, s_ktp)
                            nc.scalar.activation(keptT[:, s, :, :], bank[3 * s + 1][:, :].rearrange("p (c t) -> p c t", c=4), ACT.Copy).then_inc(s_kt, 1)

                @block.tensor
                def _(pe):
                    def flip(s, n):
                        take(pe, s_kept)
                        for c in range(n):
                            m = nc.tensor.transpose(bank[3 * s + 1][:, c * P:(c + 1) * P], kept[:, s, c * P:(c + 1) * P], ident[:, :])
                        m.then_inc(s_ktp, 1)
                        take(pe, s_kt)

                    with pe.Fori(0, PAIRS) as i:
                        for s in range(2):
                            take(pe, s_xn)
                            nc.tensor.transpose(bank[3 * s + 2][:, 0:P], xn[:, s, :], ident[:, :]).then_inc(s_xTp, 1)
                        for s in range(2):
                            take(pe, s_xT)
                            nc.tensor.matmul(bank[3 * s][:, :], xT[:, s, :], in_pat[:, :], start=True, stop=True).then_inc(s_a1p, 1)
                        for s in range(2):
                            flip(s, 4)
                            for c in range(4):
                                m = nc.tensor.matmul(bank[3 * s + 2][:, P:P + N_PROC], keptT[:, s, c, :], proc_w[:, c, :], start=(c == 0), stop=(c == 3))
                            m.then_inc(s_prp, 1)
                        for s in range(2):
                            flip(s, 2)
                            for c in range(2):
                                m = nc.tensor.matmul(bank[3 * s + 2][0:D_PV, 384:512], proc_v[:, c, :], keptT[:, s, c, :], start=(c == 0), stop=(c == 1))
                            m.then_inc(s_agp, 1)
                            take(pe, s_ag)
                            nc.tensor.matmul(bank[3 * s][:, :], aggT[:, s, :], out_w[:, :], start=True, stop=True).then_inc(s_a3p, 1)
                        for s in range(2):
                            flip(s, 4)
                            for c in range(4):
                                m = nc.tensor.matmul(bank[3 * s + 2][:, 0:P], keptT[:, s, c, :], out_pat[:, c, :], start=(c == 0), stop=(c == 3))
                            m.then_inc(s_op, 1)

        with ExitStack() as ph:
            wedge = sb("wedge", [P, C], f32, ph)
            gram = sb("gram", [P, C], f32, ph)
            wedgeT = sb("wedgeT", [P, C], f32, ph)
            gate = sb("gate", [P, 2, C], f32, ph)
            kv = sb("kv", [P, 2, 2, C], f32, ph)
            gq = sb("gq", [P, 2, C], f32, ph)
            st2 = sb("st2", [P, 2, 2, 6], f32, ph)
            mv2 = sb("mv2", [P, 2, 2, 2], f32, ph)
            shift = sb("shift", [P, 2, 1], f32, ph)
            spread = sb("spread", [P, 2, 2], f32, ph)
            unit = sb("unit", [P, 2, 1], f32, ph)
            qkn = sb("qkn", [P, 2, 2, 2, 64], f32, ph)
            tc = sb("tc", [P, 2, 2, 2, 64], f32, ph)
            ts_ = sb("ts_", [P, 2, 2, 2, 64], f32, ph)
            rot = sb("rot", [P, 2, 2, C], f32, ph)
            rotT = sb("rotT", [P, 2, 2, C], f32, ph)
            zT = sb("zT", [P, 2, C], f32, ph)
            sm = sb("sm", [P, 2, P], f32, ph)
            mx1 = sb("mx1", [P, 2, 1], f32, ph)
            nmx1 = sb("nmx1", [P, 2, 1], f32, ph)
            rsum = sb("rsum", [P, 2, 1], f32, ph)
            esink = sb("esink", [P, 2, 1], f32, ph)
            den = sb("den", [P, 2, 2], f32, ph)
            pT = sb("pT", [P, 2, P], f32, ph)
            o1 = sb("o1", [P, 2, C], f32, ph)
            s_pj, s_gb, s_ge, s_kv, s_gq, s_qc, s_mv, s_un, s_rot, s_rtp, s_rt, s_zp, s_z, s_s, s_mx, s_p, s_pr1, s_pp, s_pt, s_o1 = (sem(n) for n in (
                "proj_psum", "gate_logits", "gate_exp", "kv_ready", "gated_q", "state_psum", "moments", "unit_scale", "rotated",
                "rotT_psum", "rotT_ready", "z_psum", "z_ready", "l1_scores", "l1_max", "l1_row_sums", "l1_probs", "l1_probsT_psum", "l1_probsT", "l1_out_psum"))
            s_wd, s_wdt, s_wdc, s_gr = sem("wedge_ready"), sem("wedgeT_psum"), sem("wedgeT_ready"), sem("gram_psum")
            with nc.Block() as block:
                @block.vector
                def _(dve):
                    link(dve, s_chain, nc.vector.tensor_tensor(wedge[:, :], a_m[:, :], a_t[:, :], ALU.subtract))
                    nc.vector.tensor_tensor(wedge[:, :], wedge[:, :], ident[:, :], ALU.add).then_inc(s_wd, 1)
                    take(dve, s_wdt)
                    nc.vector.tensor_copy(wedgeT[:, :], bank[6][:, 0:P]).then_inc(s_wdc, 1)
                    take(dve, s_gr)
                    nc.vector.tensor_copy(gram[:, :], bank[6][:, P:2 * P]).then_inc(s_wdc, 1)
                    with dve.Fori(0, PAIRS) as i:
                        for s in range(2):
                            norm_stats(dve, s, h[:, bass.ds(2 * i + s, 1), :])
                        for s in range(2):
                            norm_rows(dve, s, h[:, bass.ds(2 * i + s, 1), :], xn[:, s, :])
                        for s in range(2):
                            take(dve, s_pj)
                            nc.vector.tensor_tensor(gate[:, s, :], bank[3 * s][:, 3 * C:4 * C], bg_rows[:, :], ALU.add).then_inc(s_gb, 1)
                        for s in range(2):
                            take(dve, s_ge)
                            link(dve, s_chain, nc.vector.tensor_scalar(gate[:, s, :], gate[:, s, :], 1.0, None, ALU.add))
                            link(dve, s_chain, nc.vector.reciprocal(gate[:, s, :], gate[:, s, :]))
                            nc.vector.tensor_tensor(gq[:, s, :], bank[3 * s][:, 0:C], gate[:, s, :], ALU.mult).then_inc(s_gq, 1)
                        for s in range(2):
                            link(dve, s_chain, nc.vector.bn_stats(st2[:, s, 1, :], kv[:, s, 0, :]))
                            take(dve, s_qc)
                            link(dve, s_chain, nc.vector.bn_stats(st2[:, s, 0, :], bank[3 * s + 1][:, 0:C]))
                            link(dve, s_chain, nc.vector.bn_aggr(mv2[:, s, 0, :], st2[:, s, 0, :]))
                            nc.vector.bn_aggr(mv2[:, s, 1, :], st2[:, s, 1, :]).then_inc(s_mv, 1)
                        for s in range(2):
                            take(dve, s_un)
                            link(dve, s_chain, nc.vector.tensor_scalar(qkn[:, s, 0, :, :].rearrange("p a b -> p (a b)"), bank[3 * s + 1][:, 0:C],
                                                                       shift[:, s, :], unit[:, s, :], ALU.subtract, ALU.mult))
                            link(dve, s_chain, nc.vector.tensor_scalar(qkn[:, s, 1, :, :].rearrange("p a b -> p (a b)"), kv[:, s, 0, :],
                                                                       shift[:, s, :], unit[:, s, :], ALU.subtract, ALU.mult))
                            v4 = qkn[:, s, :, :, :].rearrange("p q x j -> p (q x) j")
                            link(dve, s_chain, nc.vector.tensor_tensor(tc[:, s, :, :, :].rearrange("p q x j -> p (q x) j"), v4,
                                                                       cos_t[:, :].unsqueeze(1).to_broadcast([P, 4, 64]), ALU.mult))
                            link(dve, s_chain, nc.vector.tensor_tensor(ts_[:, s, :, :, :].rearrange("p q x j -> p (q x) j"), v4,
                                                                       sin_t[:, :].unsqueeze(1).to_broadcast([P, 4, 64]), ALU.mult))
                            link(dve, s_chain, nc.vector.tensor_tensor(rot[:, s, :, 0:64], tc[:, s, :, 0, :], ts_[:, s, :, 1, :], ALU.subtract))
                            nc.vector.tensor_tensor(rot[:, s, :, 64:128], ts_[:, s, :, 0, :], tc[:, s, :, 1, :], ALU.add).then_inc(s_rot, 1)
                        for s in range(2):
                            take(dve, s_s)
                            link(dve, s_chain, nc.vector.tensor_tensor(sm[:, s, :], bank[3 * s + 2][:, 3 * P:4 * P], causal[:, :], ALU.add))
                            link(dve, s_chain, nc.vector.tensor_reduce(mx1[:, s, :], sm[:, s, :], AX.X, ALU.max))
                            nc.vector.tensor_scalar(nmx1[:, s, :], mx1[:, s, :], sink_c[:, :], -1.0, ALU.max, ALU.mult).then_inc(s_mx, 1)
                        for s in range(2):
                            take(dve, s_p)
                            link(dve, s_chain, nc.vector.tensor_tensor(den[:, s, 0:1], rsum[:, s, :], esink[:, s, :], ALU.add))
                            link(dve, s_chain, nc.vector.reciprocal(den[:, s, 1:2], den[:, s, 0:1]))
                            take(dve, s_o1)
                            link(dve, s_chain, nc.vector.scalar_tensor_tensor(o1[:, s, :], vnull_rows[:, :], esink[:, s, :], bank[3 * s + 1][:, P:2 * P], ALU.mult, ALU.add))
                            hr = h[:, bass.ds(2 * i + s, 1), :]
                            link(dve, s_chain, nc.vector.scalar_tensor_tensor(hr, o1[:, s:s + 1, :], den[:, s, 1:2], hr, ALU.mult, ALU.add))

                @block.gpsimd
                def _(pool):
                    with pool.Fori(0, PAIRS) as i:
                        for s in range(2):
                            norm_power(pool, s)
                        for s in range(2):
                            take(pool, s_mv)
                            link(pool, s_pchain, nc.gpsimd.tensor_tensor(shift[:, s, :], mv2[:, s, 0, 0:1], mv2[:, s, 1, 0:1], ALU.add))
                            link(pool, s_pchain, nc.gpsimd.tensor_scalar(shift[:, s, :], shift[:, s, :], 0.5, 0.0, ALU.mult, ALU.add))
                            link(pool, s_pchain, nc.gpsimd.tensor_scalar(spread[:, s, :], mv2[:, s, :, 1], C / (C - 1.0), 0.0, ALU.mult, ALU.add))
                            link(pool, s_pchain, nc.gpsimd.tensor_tensor(spread[:, s, :], spread[:, s, :], cst[:, 1:2].to_broadcast([P, 2]), ALU.pow))
                            link(pool, s_pchain, nc.gpsimd.tensor_tensor(unit[:, s, :], spread[:, s, 0:1], spread[:, s, 1:2], ALU.add))
                            link(pool, s_pchain, nc.gpsimd.tensor_scalar(unit[:, s, :], unit[:, s, :], 0.5, 1e-6, ALU.mult, ALU.add))
                            nc.gpsimd.tensor_tensor(unit[:, s, :], unit[:, s, :], cst[:, 2:3], ALU.pow).then_inc(s_un, 1)

                @block.scalar
                def _(act):
                    with act.Fori(0, PAIRS) as i:
                        for s in range(2):
                            take(act, s_xTp)
                            nc.scalar.activation(xT[:, s, :], bank[3 * s + 2][:, 0:P], ACT.Copy).then_inc(s_xT, 1)
                        for s in range(2):
                            take(act, s_gb)
                            nc.scalar.activation(kv[:, s, :, :], bank[3 * s][:, C:3 * C].rearrange("p (a c) -> p a c", a=2), ACT.Copy).then_inc(s_kv, 1)
                            take(act, s_kv)
                            nc.scalar.activation(gate[:, s, :], gate[:, s, :], ACT.Exp, scale=-1.0).then_inc(s_ge, 1)
                        for s in range(2):
                            take(act, s_rtp)
                            nc.scalar.activation(rotT[:, s, :, :], bank[3 * s + 2][:, P:3 * P].rearrange("p (a c) -> p a c", a=2), ACT.Copy).then_inc(s_rt, 1)
                        for s in range(2):
                            take(act, s_zp)
                            nc.scalar.activation(zT[:, s, :], bank[3 * s + 2][:, 0:P], ACT.Copy, scale=float(C) ** -0.5).then_inc(s_z, 1)
                        for s in range(2):
                            take(act, s_mx)
                            nc.scalar.activation(sm[:, s, :], sm[:, s, :], ACT.Exp, bias=nmx1[:, s, :], accum_out=rsum[:, s, :]).then_inc(s_pr1, 1)
                            nc.scalar.activation(esink[:, s, :], sink_c[:, :], ACT.Exp, bias=nmx1[:, s, :]).then_inc(s_p, 1)
                            take(act, s_pp)
                            nc.scalar.activation(pT[:, s, :], bank[3 * s + 1][:, 2 * P:3 * P], ACT.Copy).then_inc(s_pt, 1)

                @block.tensor
                def _(pe):
                    take(pe, s_wd)
                    nc.tensor.transpose(bank[6][:, 0:P], wedge[:, :], ident[:, :]).then_inc(s_wdt, 1)
                    take(pe, s_wdc)
                    nc.tensor.matmul(bank[6][:, P:2 * P], wedgeT[:, :], wedgeT[:, :], start=True, stop=True).then_inc(s_gr, 1)
                    take(pe, s_wdc)
                    with pe.Fori(0, PAIRS) as i:
                        for s in range(2):
                            take(pe, s_xn)
                            nc.tensor.transpose(bank[3 * s + 2][:, 0:P], xn[:, s, :], ident[:, :]).then_inc(s_xTp, 1)
                        for s in range(2):
                            take(pe, s_xT)
                            nc.tensor.matmul(bank[3 * s][:, :], xT[:, s, :], w_qkvg[:, :], start=True, stop=True).then_inc(s_pj, 1)
                        for s in range(2):
                            take(pe, s_gq)
                            nc.tensor.matmul(bank[3 * s + 1][:, 0:C], run_sum[:, :], gq[:, s, :], start=True, stop=True).then_inc(s_qc, 1)
                        for s in range(2):
                            take(pe, s_rot)
                            for x in range(2):
                                m = nc.tensor.transpose(bank[3 * s + 2][:, (1 + x) * P:(2 + x) * P], rot[:, s, x, :], ident[:, :])
                            m.then_inc(s_rtp, 1)
                        for s in range(2):
                            take(pe, s_rt)
                            nc.tensor.matmul(bank[3 * s + 2][:, 0:P], gram[:, :], rotT[:, s, 0, :], start=True, stop=True).then_inc(s_zp, 1)
                        for s in range(2):
                            take(pe, s_z)
                            nc.tensor.matmul(bank[3 * s + 2][:, 3 * P:4 * P], zT[:, s, :], rotT[:, s, 1, :], start=True, stop=True).then_inc(s_s, 1)
                        for s in range(2):
                            take(pe, s_pr1)
                            nc.tensor.transpose(bank[3 * s + 1][:, 2 * P:3 * P], sm[:, s, :], ident[:, :]).then_inc(s_pp, 1)
                            take(pe, s_pt)
                            nc.tensor.matmul(bank[3 * s + 1][:, P:2 * P], pT[:, s, :], kv[:, s, 1, :], start=True, stop=True).then_inc(s_o1, 1)

        s_xs = sem("x_rows_scattered")
        with ExitStack() as ph:
            xn_all = sb("xn_all", [P, B, C], f32, ph)
            logit = sb("logit", [P, B, E], f32, ph)
            prob = sb("prob", [P, B, E], f32, ph)
            hot1 = sb("hot1", [P, B, E], f32, ph)
            hot2 = sb("hot2", [P, B, E], f32, ph)
            both = sb("both", [P, B, E], f32, ph)
            gates = sb("gates", [P, B, E], f32, ph)
            gatesT = sb("gatesT", [P, 4, P], f32, ph)
            wk1 = sb("wk1", [P, B, E], f32, ph)
            wk2 = sb("wk2", [P, B, E], f32, ph)
            tot = sb("tot", [P, B, E], f32, ph)
            red = sb("red", [P, B], f32, ph)
            g12 = sb("g12", [P, 2, B], f32, ph)
            pos = sb("pos", [P, 2, B], f32, ph)
            posi = sb("posi", [P, 2, B], i32, ph)
            ntile = sb("ntile", [P, E], f32, ph)
            ntile_i = sb("ntile_i", [P, E], i32, ph)
            last1 = sb("last1", [P, E], f32, ph)
            last2 = sb("last2", [P, E], f32, ph)
            ej = sb("ej", [P, SLOTS, E], f32, ph)
            ejr = sb("ejr", [P, SLOTS], f32, ph)
            eji = sb("eji", [1, SLOTS], i32, ph)
            xg = sb("xg", [P, 2, C], f32, ph)
            xgT = sb("xgT", [P, 2, C], f32, ph)
            w1b = sb("w1b", [P, 2, FF + NC1], f32, ph)
            hid = sb("hid", [P, 2, NC1, P], f32, ph)
            yo = sb("yo", [P, 2, C], f32, ph)
            yg = sb("yg", [P, 2, B, C], f32, ph)
            s_rl, s_tab, s_pre, s_prec, s_pos, s_gt, s_gtc, s_ej = (sem(n) for n in (
                "router_logits", "gates_ready", "ranks_psum", "ranks_read", "positions_ready", "gatesT_psum", "gatesT_ready", "expert_table"))
            s_xl, s_wl, s_xgp, s_xg, s_hp, s_hid, s_yp, s_y, s_yst = (sem(n) for n in (
                "x_rows_loaded", "w1_loaded", "xgT_psum", "xgT_ready", "hidden_psum", "hidden_ready", "y_psum", "y_ready", "y_stored"))
            s_yst2, s_w1g, s_w1f, s_wl2 = sem("y_stored_b"), sem("w1_used_b"), sem("w1_used"), sem("w1_loaded_b")
            s_tab2, s_fill2 = sem("choice_ready"), sem("all_y_stored")
            s_yg, s_b2p, s_out, s_fin = [sem(f"y_rows_gathered_{g}") for g in range(8)], sem("b2_psum"), sem("out_stored"), sem("out_ready")
            with nc.Block() as block:
                @block.vector
                def _(dve):
                    with dve.Fori(0, PAIRS) as i:
                        for s in range(2):
                            norm_stats(dve, s, h[:, bass.ds(2 * i + s, 1), :])
                        for s in range(2):
                            take(dve, s_rstd)
                            link(dve, s_chain, nc.vector.tensor_scalar(xn[:, s, :], h[:, bass.ds(2 * i + s, 1), :].rearrange("p a c -> p (a c)"), mv[:, s, 0:1], rstd[:, s, :], ALU.subtract, ALU.mult))
                            nc.vector.tensor_copy(xn_all[:, bass.ds(2 * i + s, 1), :], xn[:, s:s + 1, :]).then_inc(s_xn, 1)
                        for s in range(2):
                            take(dve, s_rl)
                            link(dve, s_chain, nc.vector.tensor_tensor(logit[:, bass.ds(2 * i + s, 1), :], bank[2 * s + 1][:, 0:E].unsqueeze(1), rb_rows[:, :].unsqueeze(1), ALU.add))

                    def wide(x):
                        return x.unsqueeze(2).to_broadcast([P, B, E])

                    def L(ins):
                        link(dve, s_chain, ins)
                    v = nc.vector
                    eid_b = eid[:, :].unsqueeze(1).to_broadcast([P, B, E])
                    L(v.tensor_reduce(red[:, :], logit[:, :, :], AX.X, ALU.max))
                    v.tensor_tensor(logit[:, :, :], logit[:, :, :], wide(red[:, :]), ALU.subtract).then_inc(s_tab, 1)
                    take(dve, s_pos)
                    L(v.tensor_reduce(red[:, :], prob[:, :, :], AX.X, ALU.add))
                    L(v.reciprocal(red[:, :], red[:, :]))
                    L(v.tensor_tensor(prob[:, :, :], prob[:, :, :], wide(red[:, :]), ALU.mult))
                    cur = prob
                    for n, hotn in enumerate((hot1, hot2)):
                        L(v.tensor_reduce(g12[:, n, :], cur[:, :, :], AX.X, ALU.max))
                        L(v.tensor_tensor(wk1[:, :, :], cur[:, :, :], wide(g12[:, n, :]), ALU.is_equal))
                        L(v.scalar_tensor_tensor(wk1[:, :, :], eid_b, -float(E), wk1[:, :, :], ALU.add, ALU.mult))
                        L(v.tensor_reduce(red[:, :], wk1[:, :, :], AX.X, ALU.min))
                        L(v.tensor_scalar(red[:, :], red[:, :], float(E), None, ALU.add))
                        L(v.tensor_tensor(hotn[:, :, :], eid_b, wide(red[:, :]), ALU.is_equal))
                        if n == 0:
                            L(v.scalar_tensor_tensor(wk2[:, :, :], hot1[:, :, :], -2.0, prob[:, :, :], ALU.mult, ALU.add))
                            cur = wk2
                    L(v.tensor_tensor(both[:, :, :], hot1[:, :, :], hot2[:, :, :], ALU.add))
                    v.tensor_tensor(gates[:, :, :], both[:, :, :], prob[:, :, :], ALU.mult).then_inc(s_tab2, 1)
                    take(dve, s_pre)
                    L(v.tensor_copy(tot[:, :, :], bank[1][:, :].rearrange("p (t e) -> p t e", e=E)))
                    src, dst = tot, wk1
                    step = 1
                    while step < B:
                        L(v.tensor_copy(dst[:, 0:step, :], src[:, 0:step, :]))
                        L(v.tensor_tensor(dst[:, step:B, :], src[:, step:B, :], src[:, 0:B - step, :], ALU.add))
                        src, dst = dst, (wk2 if dst is wk1 else wk1)
                        step *= 2
                    incl, ex = src, dst
                    L(v.tensor_scalar(ntile_i[:, :], incl[:, B - 1, :], P - 1.0, None, ALU.add))
                    L(v.tensor_scalar(ntile_i[:, :], ntile_i[:, :], 7, None, ALU.logical_shift_right))
                    L(v.tensor_copy(ntile[:, :], ntile_i[:, :]))
                    L(v.tensor_tensor(ex[:, :, :], incl[:, :, :], tot[:, :, :], ALU.subtract))
                    s2, d2 = ntile, last1
                    step = 1
                    while step < E:
                        L(v.tensor_copy(d2[:, 0:step], s2[:, 0:step]))
                        L(v.tensor_tensor(d2[:, step:E], s2[:, step:E], s2[:, 0:E - step], ALU.add))
                        s2, d2 = d2, (last2 if d2 is last1 else last1)
                        step *= 2
                    ends, base = s2, d2
                    L(v.tensor_tensor(base[:, :], ends[:, :], ntile[:, :], ALU.subtract))
                    L(v.tensor_scalar(base[:, :], base[:, :], float(P), None, ALU.mult))
                    L(v.tensor_tensor(ex[:, :, :], ex[:, :, :], base[:, :].unsqueeze(1).to_broadcast([P, B, E]), ALU.add))
                    L(v.tensor_tensor(ex[:, :, :], ex[:, :, :], bank[0][:, :].rearrange("p (t e) -> p t e", e=E), ALU.add))
                    for n, hotn in enumerate((hot1, hot2)):
                        L(v.tensor_tensor(tot[:, :, :], hotn[:, :, :], ex[:, :, :], ALU.mult))
                        L(v.tensor_reduce(pos[:, n, :], tot[:, :, :], AX.X, ALU.add))
                    v.tensor_copy(posi[:, :, :], pos[:, :, :]).then_inc(s_prec, 1)
                    L(v.tensor_tensor(ej[:, :, :], ends[:, :].unsqueeze(1).to_broadcast([P, SLOTS, E]), jid[:, :].unsqueeze(2).to_broadcast([P, SLOTS, E]), ALU.is_le))
                    L(v.tensor_reduce(ejr[:, :], ej[:, :, :], AX.X, ALU.add))
                    v.tensor_scalar(eji[:, :], ejr[0:1, :], E - 1.0, None, ALU.min).then_inc(s_ej, 1)
                    take(dve, s_gt)
                    v.tensor_copy(gatesT[:, :, :], bank[2][:, :].rearrange("p (g t) -> p g t", g=4)).then_inc(s_gtc, 1)
                    with dve.Fori(0, SLOTS // 2) as j:
                        for s in range(2):
                            take(dve, s_xgp)
                            v.tensor_copy(xgT[:, s, :], bank[4 + s][:, 0:P]).then_inc(s_xg, 1)
                        for s in range(2):
                            take(dve, s_yp)
                            take(dve, s_yst if s == 0 else s_yst2, 16)
                            v.tensor_copy(yo[:, s, :], bank[6 + s][:, 0:P]).then_inc(s_y, 1)
                    for g in range(8):
                        take(dve, s_b2p)
                        L(v.tensor_tensor(h[:, 4 * g:4 * g + 4, :], h[:, 4 * g:4 * g + 4, :], bank[g % 4][:, :].rearrange("p (t c) -> p t c", t=4), ALU.add))
                        dve.wait_ge(s_yg[g], 16 * 8)
                        for n in range(2):
                            for t in range(4 * g, 4 * g + 4):
                                last = v.scalar_tensor_tensor(h[:, t, :], yg[:, n, t, :], g12[:, n, t:t + 1], h[:, t, :], ALU.mult, ALU.add)
                                last.then_inc(s_fin if n else s_chain, 1)
                            if n == 0:
                                take(dve, s_chain, 4)

                @block.gpsimd
                def _(pool):
                    with pool.Fori(0, PAIRS) as i:
                        for s in range(2):
                            norm_power(pool, s)
                    take(pool, s_prec)
                    for t in range(B):
                        for n in range(2):
                            nc.gpsimd.indirect_dma_start(xs_dram[:, :], bass.IndirectOffsetOnAxis(posi[:, n, t:t + 1], 0), xn_all[:, t, :], None).then_inc(s_xs, 16)
                    take(pool, s_fill2)
                    for t in range(B):
                        for n in range(2):
                            nc.gpsimd.indirect_dma_start(yg[:, n, t, :], None, ys_dram[:, :], bass.IndirectOffsetOnAxis(posi[:, n, t:t + 1], 0)).then_inc(s_yg[t // 4], 16)

                @block.sync
                def _(sp):
                    sp.wait_ge(s_ej, 1)
                    sp.wait_ge(s_xs, 16 * 2 * B)
                    with sp.Fori(0, SLOTS // 2) as j:
                        for s in range(2):
                            take(sp, s_w1f if s == 0 else s_w1g)
                            ex = sp.value_load(eji[0:1, bass.ds(2 * j + s, 1)], min_val=0, max_val=E - 1)
                            sp.dma_start(xg[:, s, :], xs_dram[bass.ds((2 * j + s) * P, P), :]).then_inc(s_wl if s == 0 else s_wl2, 16)
                            sp.dma_start(w1b[:, s, :], a["w1b"][bass.ds(ex, 1), :, :].rearrange("a p f -> (a p) f")).then_inc(s_wl if s == 0 else s_wl2, 16)
                    for g in range(8):
                        sp.wait_ge(s_fin, 4 * (g + 1))
                        sp.dma_start(out[4 * g:4 * g + 4, :, :].rearrange("b p c -> p b c"), h[:, 4 * g:4 * g + 4, :]).then_inc(s_out, 16)
                    sp.wait_ge(s_out, 16 * 8)

                @block.scalar
                def _(act):
                    with act.Fori(0, PAIRS) as i:
                        for s in range(2):
                            take(act, s_xTp)
                            nc.scalar.activation(xT[:, s, :], bank[2 * s][:, 0:P], ACT.Copy).then_inc(s_xT, 1)
                    take(act, s_tab)
                    nc.scalar.activation(prob[:, :, :], logit[:, :, :], ACT.Exp).then_inc(s_pos, 1)
                    act.sem_inc(s_yst, 16)
                    act.sem_inc(s_yst2, 16)
                    with act.Fori(0, SLOTS // 2) as j:
                        for s in range(2):
                            take(act, s_hp)
                            for c in range(NC1):
                                m = nc.scalar.activation(hid[:, s, c, :], bank[2 + s][:, c * P:(c + 1) * P], ACT.Gelu, bias=w1b[:, s, FF + c:FF + c + 1])
                            m.then_inc(s_hid, 1)
                        for s in range(2):
                            take(act, s_y)
                            act.dma_start(ys_dram[bass.ds((2 * j + s) * P, P), :], yo[:, s, :]).then_inc(s_yst if s == 0 else s_yst2, 16)
                    act.wait_ge(s_yst, 16)
                    act.wait_ge(s_yst2, 16)
                    act.sem_inc(s_fill2, 1)

                @block.tensor
                def _(pe):
                    with pe.Fori(0, PAIRS) as i:
                        for s in range(2):
                            take(pe, s_xn)
                            nc.tensor.transpose(bank[2 * s][:, 0:P], xn[:, s, :], ident[:, :]).then_inc(s_xTp, 1)
                        for s in range(2):
                            take(pe, s_xT)
                            nc.tensor.matmul(bank[2 * s + 1][:, 0:E], xT[:, s, :], r_w[:, :], start=True, stop=True).then_inc(s_rl, 1)
                    take(pe, s_tab2)
                    nc.tensor.matmul(bank[0][:, :], tri[:, :], both[:, :, :], start=True, stop=True)
                    nc.tensor.matmul(bank[1][:, :], ones[:, :], both[:, :, :], start=True, stop=True).then_inc(s_pre, 1)
                    for g in range(4):
                        m = nc.tensor.transpose(bank[2][:, g * P:(g + 1) * P], gates[:, 8 * g:8 * g + 8, :], ident[:, :])
                    m.then_inc(s_gt, 1)
                    take(pe, s_gtc)
                    pe.wait_ge(s_ej, 1)
                    pe.sem_inc(s_w1f, 1)
                    pe.sem_inc(s_w1g, 1)
                    with pe.Fori(0, SLOTS // 2) as j:
                        for s in range(2):
                            take(pe, s_wl if s == 0 else s_wl2, 32)
                            nc.tensor.transpose(bank[4 + s][:, 0:P], xg[:, s, :], ident[:, :]).then_inc(s_xgp, 1)
                        for s in range(2):
                            take(pe, s_xg)
                            for c in range(NC1):
                                m = nc.tensor.matmul(bank[2 + s][:, c * P:(c + 1) * P], w1b[:, s, c * P:(c + 1) * P], xgT[:, s, :], start=True, stop=True)
                            m.then_inc(s_hp, 1)
                        for s in range(2):
                            ex = pe.value_load(eji[0:1, bass.ds(2 * j + s, 1)], min_val=0, max_val=E - 1)
                            take(pe, s_hid)
                            pe.sem_inc(s_w1f if s == 0 else s_w1g, 1)
                            for c in range(NC1):
                                m = nc.tensor.matmul(bank[6 + s][:, 0:P], hid[:, s, c, :], w2_all[:, bass.ds(ex, 1), c, :].rearrange("p a c -> p (a c)"), start=(c == 0), stop=(c == NC1 - 1))
                            m.then_inc(s_yp, 1)
                    for g in range(8):
                        if g >= 4:
                            pe.wait_ge(s_fin, 4 * (g - 3))
                        nc.tensor.matmul(bank[g % 4][:, :], gatesT[:, g // 2, :], b2_blocks[:, 4 * (g % 2):4 * (g % 2) + 4, :], start=True, stop=True).then_inc(s_b2p, 1)


_EMB_OUT = (B, P, C)


def kernel(**inputs):
    import concourse.bacc as _bacc
    from concourse.bass_utils import run_bass_kernel_spmd as _run

    x = {k: np.asarray(v) for k, v in inputs.items()}
    f = np.float32
    n = np.arange(64)
    win = 0.5 - 0.5 * np.cos(2.0 * np.pi * n / 64)
    dft = np.zeros((P, 2, NFRAME, NFREQ), np.float64)
    for fr in range(NFRAME):
        at = fr * 64 + n - 32
        at = np.where(at < 0, -at, at)
        at = np.where(at > P - 1, 2 * (P - 1) - at, at)
        for k in range(NFREQ):
            np.add.at(dft[:, 0, fr, k], at, win * np.cos(2 * np.pi * k * n / 64))
            np.add.at(dft[:, 1, fr, k], at, -win * np.sin(2 * np.pi * k * n / 64))
    l = np.arange(P)
    inv = (1.0 / 10000.0 ** (np.arange(0, C, 2, dtype=f) / f(C))).astype(f)
    fr = l[:, None].astype(f) * inv[None, :]
    same = (l[:, None] // 64) == (l[None, :] // 64)
    run = (same & (l[:, None] <= l[None, :])) + 2.0 * ((l[:, None] < 64) & (l[None, :] >= 64))
    cst = np.tile(np.array([-0.5, 0.5, -1.0, 0.0], f), (P, 1))
    cst[:, 3] = l
    tok = x["x"].astype(np.int32)
    proj = x["L0_tok_proj_w"].reshape(NFREQ, V, D_STFT)
    eo = np.concatenate([np.arange(0, C, 2), np.arange(1, C, 2)])
    w1 = x["L1_ffn_w1"].transpose(0, 2, 1)
    b1 = x["L1_ffn_b1"].reshape(E, NC1, P).transpose(0, 2, 1)
    A = x["L1_attn_A"][0]
    arrays = {
        "idsT": tok.T, "ids": tok.reshape(-1), "emb": x["L0_tok_emb_table"], "dft": dft.reshape(P, 2 * NFRAME, NFREQ).astype(f),
        "pw": proj, "pb": x["L0_tok_proj_b"], "up": ((l[None, :] * 3 // P) == np.arange(3)[:, None]).astype(f),
        "eid": np.arange(E).astype(f), "jid": np.arange(SLOTS).astype(f), "cst": cst, "ident": np.eye(P, dtype=f),
        "w_q": x["L0_attn_q_w"].T.reshape(C, 2, HG, DH), "w_k": x["L0_attn_kv_w"][:C].T.reshape(C, 2, HG, DH),
        "w_v": x["L0_attn_kv_w"][C:].T, "in_pat": x["L0_ffn_input_patterns"].T,
        "proc_w": x["L0_ffn_process_input_weights"].T.reshape(4, P, N_PROC).transpose(1, 0, 2),
        "proc_v": x["L0_ffn_process_values"].reshape(2, P, D_PV).transpose(1, 0, 2),
        "out_w": x["L0_ffn_output_input_weights"].T,
        "out_pat": x["L0_ffn_output_patterns"].reshape(4, P, C).transpose(1, 0, 2),
        "w_qkvg": np.concatenate([x["L1_attn_Wq"][eo], x["L1_attn_Wk"][eo], x["L1_attn_Wv"], x["L1_attn_Wg"][eo]]).T,
        "bg": x["L1_attn_bg"][eo], "A": A, "AT": A.T, "sink": x["L1_attn_sink"].reshape(1), "v_null": x["L1_attn_v_null"].reshape(C),
        "cos": np.cos(fr).astype(f), "sin": np.sin(fr).astype(f), "run_sum": run.astype(f),
        "causal": np.where(l[:, None] >= l[None, :], 0.0, -BIG).astype(f),
        "r_w": x["L1_ffn_router_w"].T, "r_b": x["L1_ffn_router_b"], "tri": (l[:, None] < l[None, :]).astype(f),
        "w2": x["L1_ffn_w2"].reshape(E, C, NC1, P).transpose(3, 0, 2, 1), "b2": x["L1_ffn_b2"],
        "w1b": np.concatenate([w1, b1], axis=2),
    }
    nc = _bacc.Bacc("TRN2", target_bir_lowering=False, num_devices=1)
    args, ins = {}, {}
    for k, v in arrays.items():
        v = np.ascontiguousarray(v)
        ins["in_" + k] = v
        args[k] = nc.dram_tensor("in_" + k, v.shape, mybir.dt.from_np(v.dtype), kind="ExternalInput").ap()
    out = nc.dram_tensor("out_0", (B, P, C), mybir.dt.float32, kind="ExternalOutput").ap()
    build(nc, args, out)
    r = _run(nc, [ins], core_ids=[0])
    return r.results[0]["out_0"]
```

```python
import numpy as np
import concourse.bass as bass
from concourse import mybir
from contextlib import ExitStack

P = 128
B = 32
C = 128
V = 16
D_EMB, D_STFT = 89, 39
NFREQ, NFRAME = 33, 3
H, DH = 8, 16
HG = 4
N_IN, N_PROC, N_OUT, D_PV = 512, 256, 512, 64
K_IN, K_PROC, K_OUT = 64, 128, 64
E, FF, TOPK = 16, 512, 2
NC1 = FF // P
NSLOT = 8
SLOTS = -(-((B * P * TOPK + E * (P - 1)) // P) // NSLOT) * NSLOT
REGION = B * P + P
XW = C + 4
SKIP = 2.0 ** 20
LN_EPS = 1e-5
GONE = -1e30
BIG = 1e30
PAIRS = B // 2




def build(nc, a, out):
    f32, i32 = mybir.dt.float32, mybir.dt.int32
    ALU, ACT, AX = mybir.AluOpType, mybir.ActivationFunctionType, mybir.AxisListType
    xs_dram = nc.dram_tensor("xs_rows", (E * REGION + P, XW), f32, kind="Internal").ap()
    ys_dram = nc.dram_tensor("ys_rows", (TOPK * B * P, C), f32, kind="Internal").ap()

    with ExitStack() as ctx:
        def sb(name, shape, dt=f32, stack=ctx):
            return stack.enter_context(nc.sbuf_tensor(name, shape, dt))

        def sem(name):
            return ctx.enter_context(nc.semaphore(name))

        acc = ctx.enter_context(nc.psum_tensor("acc", [P, 8, 512], f32))
        bank = [acc[:, i, :] for i in range(8)]

        h = sb("h", [P, B, C])
        ident = sb("ident", [P, P])
        w_q = sb("w_q", [P, 2, HG, 32])
        w_k = sb("w_k", [P, 2, HG, 32])
        w_v = sb("w_v", [P, C])
        in_pat = sb("in_pat", [P, N_IN])
        proc_w = sb("proc_w", [P, N_IN // P, N_PROC])
        proc_v = sb("proc_v", [P, N_PROC // P, D_PV])
        out_w = sb("out_w", [D_PV, N_OUT])
        out_pat = sb("out_pat", [P, N_OUT // P, C])
        w_qkvg = sb("w_qkvg", [P, 4 * C])
        bg_rows = sb("bg_rows", [P, C])
        a_m = sb("a_m", [P, C])
        a_t = sb("a_t", [P, C])
        sink_c = sb("sink_c", [P, 1])
        vnull_rows = sb("vnull_rows", [P, C])
        cos_t = sb("cos_t", [P, 64])
        sin_t = sb("sin_t", [P, 64])
        run_sum = sb("run_sum", [P, P])
        causal = sb("causal", [P, P])
        r_w = sb("r_w", [P, E])
        rb_rows = sb("rb_rows", [P, E])
        b2_blocks = sb("b2_blocks", [P, 8, C])
        tri = sb("tri", [P, P])
        ones = sb("ones", [P, P])
        eid = sb("eid", [P, E])
        region = sb("region", [P, E])
        pad_rows = sb("pad_rows", [P, XW])
        cst = sb("cst", [P, 4])

        stats = sb("stats", [P, NSLOT, 6])
        mv = sb("mv", [P, NSLOT, 2])
        rstd = sb("rstd", [P, NSLOT])
        xn = sb("xn", [P, NSLOT, C])
        xT = sb("xT", [P, NSLOT, C])

        load_names = ["w", "pad", "ids"]
        s_load = {n: sem("loaded_" + n) for n in load_names}
        s_chain = sem("dve_done")
        s_pchain = sem("pool_done")
        s_achain = sem("act_done")

        def link(eng, chain, ins):
            ins.then_inc(chain, 1)
            eng.wait_ge(chain, 1)
            eng.sem_inc(chain, -1)

        with ExitStack() as ph:
            ids_c = sb("ids_c", [P, B], i32, ph)
            ids_r = sb("ids_r", [V, B * P], i32, ph)
            hot = sb("hot", [P, B, V], f32, ph)
            hotT = sb("hotT", [V, B * P], f32, ph)
            emb = sb("emb", [V, D_EMB], f32, ph)
            dft = sb("dft", [P, 2 * NFRAME, NFREQ], f32, ph)
            sq = sb("sq", [NFREQ, 2, NFRAME, B * V], f32, ph)
            mag = sb("mag", [NFREQ, NFRAME, B, V], f32, ph)
            pw = sb("pw", [NFREQ, V, D_STFT], f32, ph)
            pb = sb("pb", [NFRAME * B, D_STFT], f32, ph)
            enc = sb("enc", [NFRAME * B, D_STFT], f32, ph)
            encF = sb("encF", [NFRAME, B, D_STFT], f32, ph)
            up = sb("up", [NFRAME, P], f32, ph)
            s_zeroed, s_hot, s_spec, s_sq, s_sum, s_mag, s_enc, s_encs, s_encf = (sem(n) for n in (
                "zeroed", "hot_ready", "spectra_ready", "squares_ready", "power_ready", "mag_ready",
                "enc_ready", "enc_rows_ready", "enc_frames_ready"))
            s_emb, s_embc, s_ide = sem("emb_ready"), sem("emb_copied"), sem("stft_ready")
            with nc.Block() as block:
                @block.sync
                def _(sp):
                    loads = [(ids_c[:, :], a["idsT"]), (ids_r[:, :], a["ids"].partition_broadcast(V)),
                             (emb[:, :], a["emb"]), (dft[:, :, :], a["dft"]), (pw[:, :, :], a["pw"]),
                             (pb[:, :], a["pb"].partition_broadcast(NFRAME * B)), (up[:, :], a["up"]),
                             (eid[:, :], a["eid"].partition_broadcast(P)), (cst[:, :], a["cst"]),
                             (ident[:, :], a["ident"])]
                    for dst, src in loads:
                        sp.dma_start(dst, src).then_inc(s_load["ids"], 16)
                    rest = [(in_pat[:, :], a["in_pat"]), (proc_w[:, :, :], a["proc_w"]), (proc_v[:, :, :], a["proc_v"]),
                            (w_v[:, :], a["w_v"]), (out_w[:, :], a["out_w"]), (out_pat[:, :, :], a["out_pat"]),
                            (w_qkvg[:, :], a["w_qkvg"]), (bg_rows[:, :], a["bg"].partition_broadcast(P)),
                            (a_m[:, :], a["A"]), (a_t[:, :], a["AT"]), (sink_c[:, :], a["sink"].partition_broadcast(P)),
                            (vnull_rows[:, :], a["v_null"].partition_broadcast(P)), (cos_t[:, :], a["cos"]),
                            (sin_t[:, :], a["sin"]), (run_sum[:, :], a["run_sum"]), (causal[:, :], a["causal"]),
                            (r_w[:, :], a["r_w"]), (rb_rows[:, :], a["r_b"].partition_broadcast(P)),
                            (tri[:, :], a["tri"]), (region[:, :], a["region"].partition_broadcast(P)),
                            (pad_rows[:, :], a["pad_rows"])]
                    sp.wait_ge(s_zeroed, 4)
                    for g in range(2):
                        for w, src in ((w_q, a["w_q"]), (w_k, a["w_k"])):
                            rest.append((w[:, g, :, 0:DH], src[:, g, :, :]))
                    for t in range(8):
                        rest.append((b2_blocks[E * t:E * t + E, t, :], a["b2"]))
                    for dst, src in rest:
                        sp.dma_start(dst, src).then_inc(s_load["w"], 16)
                    sp.wait_ge(s_encs, 1)
                    sp.sem_inc(s_encs, -1)
                    for f in range(NFRAME):
                        sp.dma_start(encF[f:f + 1, :, :], enc[B * f:B * f + B, :]).then_inc(s_encf, 16)
                    sp.wait_ge(s_load["w"], 16 * len(rest))

                @block.gpsimd
                def _(pool):
                    nc.gpsimd.memset(w_q[:, :, :, :], 0.0).then_inc(s_zeroed, 1)
                    nc.gpsimd.memset(w_k[:, :, :, :], 0.0).then_inc(s_zeroed, 1)
                    nc.gpsimd.memset(b2_blocks[:, :, :], 0.0).then_inc(s_zeroed, 1)
                    nc.gpsimd.memset(ones[:, :], 1.0).then_inc(s_zeroed, 1)

                @block.vector
                def _(dve):
                    dve.wait_ge(s_load["ids"], 16 * 10)
                    nc.vector.tensor_tensor(hot[:, :, :], ids_c[:, :].unsqueeze(2).to_broadcast([P, B, V]),
                                            eid[:, :].unsqueeze(1).to_broadcast([P, B, V]), ALU.is_equal).then_inc(s_hot, 1)
                    nc.vector.tensor_scalar(hotT[:, :], ids_r[:, :], cst[0:V, 3:4], None, ALU.is_equal).then_inc(s_hot, 1)
                    dve.wait_ge(s_sq, 6)
                    nc.vector.tensor_tensor(mag[:, :, :, :].rearrange("f a b v -> f a (b v)"), sq[:, 0, :, :], sq[:, 1, :, :], ALU.add).then_inc(s_sum, 1)
                    dve.wait_ge(s_enc, 1)
                    dve.sem_inc(s_enc, -1)
                    nc.vector.tensor_tensor(enc[:, :], bank[6][0:NFRAME * B, 0:D_STFT], pb[:, :], ALU.add).then_inc(s_encs, 1)
                    for g in range(B // 4):
                        dve.wait_ge(s_emb, 1)
                        dve.sem_inc(s_emb, -1)
                        nc.vector.tensor_copy(h[:, 4 * g:4 * g + 4, 0:D_EMB],
                                              bank[g % 2][:, 0:4 * D_EMB].rearrange("p (b e) -> p b e", b=4)).then_inc(s_embc, 1)

                @block.scalar
                def _(act):
                    for f in range(2 * NFRAME):
                        act.wait_ge(s_spec, 1)
                        act.sem_inc(s_spec, -1)
                        nc.scalar.activation(sq[:, f // NFRAME, f % NFRAME, :], bank[2 + f % 4][0:NFREQ, :], ACT.Square).then_inc(s_sq, 1)
                    act.wait_ge(s_sum, 1)
                    act.sem_inc(s_sum, -1)
                    nc.scalar.activation(mag[:, :, :, :], mag[:, :, :, :], ACT.Sqrt).then_inc(s_mag, 1)
                    for g in range(4):
                        act.wait_ge(s_ide, 1)
                        act.sem_inc(s_ide, -1)
                        nc.scalar.activation(h[:, 8 * g:8 * g + 8, D_EMB:C],
                                             bank[2 + g][:, 0:8 * D_STFT].rearrange("p (b e) -> p b e", b=8), ACT.Copy).then_inc(s_achain, 1)
                    act.wait_ge(s_achain, 4)
                    act.sem_inc(s_achain, -4)

                @block.tensor
                def _(pe):
                    pe.wait_ge(s_load["ids"], 16 * 10)
                    pe.wait_ge(s_hot, 2)
                    for f in range(2 * NFRAME):
                        if f >= 4:
                            pe.wait_ge(s_sq, f - 3)
                        nc.tensor.matmul(bank[2 + f % 4][0:NFREQ, :], dft[:, f, :], hot[:, :, :], start=True, stop=True).then_inc(s_spec, 1)
                    pe.wait_ge(s_mag, 1)
                    pe.sem_inc(s_mag, -1)
                    for v in range(V):
                        m = nc.tensor.matmul(bank[6][0:NFRAME * B, 0:D_STFT], mag[:, :, :, v], pw[:, v, :], start=(v == 0), stop=(v == V - 1))
                    m.then_inc(s_enc, 1)
                    for g in range(B // 4):
                        if g >= 2:
                            pe.wait_ge(s_embc, g - 1)
                        for b in range(4):
                            t = 4 * g + b
                            m = nc.tensor.matmul(bank[g % 2][:, b * D_EMB:(b + 1) * D_EMB], hotT[:, t * P:(t + 1) * P], emb[:, :], start=True, stop=True)
                        m.then_inc(s_emb, 1)
                    pe.wait_ge(s_encf, 16 * NFRAME)
                    for g in range(4):
                        nc.tensor.matmul(bank[2 + g][:, 0:8 * D_STFT], up[:, :], encF[:, 8 * g:8 * g + 8, :], start=True, stop=True).then_inc(s_ide, 1)

        s_ve, s_rstd, s_xn, s_xTp, s_xT = sem("variance_ready"), sem("rstd_ready"), sem("xn_ready"), sem("xT_in_psum"), sem("xT_ready")

        def norm_stats(dve, at, rows):
            for s, x in enumerate(rows):
                nc.vector.bn_stats(stats[:, at + s, :], x).then_inc(s_chain, 1)
            for s in range(len(rows)):
                dve.wait_ge(s_chain, 1)
                dve.sem_inc(s_chain, -1)
                nc.vector.bn_aggr(mv[:, at + s, :], stats[:, at + s, :]).then_inc(s_chain, 1)
            dve.wait_ge(s_chain, len(rows))
            dve.sem_inc(s_chain, -len(rows))
            v = mv[:, at:at + len(rows), 1]
            nc.vector.tensor_scalar(v, v, LN_EPS, None, ALU.add).then_inc(s_ve, 1)

        def norm_power(pool, at, n):
            pool.wait_ge(s_ve, 1)
            pool.sem_inc(s_ve, -1)
            nc.gpsimd.tensor_tensor(rstd[:, at:at + n], mv[:, at:at + n, 1], cst[:, 0:1].to_broadcast([P, n]), ALU.pow).then_inc(s_rstd, 1)

        def norm_rows(dve, at, rows, dsts):
            dve.wait_ge(s_rstd, 1)
            dve.sem_inc(s_rstd, -1)
            for s, (x, dst) in enumerate(zip(rows, dsts)):
                nc.vector.tensor_scalar(dst, x, mv[:, at + s, 0:1], rstd[:, at + s:at + s + 1], ALU.subtract, ALU.mult).then_inc(s_xn, 1)

        def tile_of(t):
            return h[:, bass.ds(t, 1), :].rearrange("p a c -> p (a c)")

        with ExitStack() as ph:
            qk = sb("qk", [P, 4, 2, P], f32, ph)
            va = sb("va", [P, B, H, DH + 1], f32, ph)
            sh = sb("sh", [P, HG, 2, 2, P], f32, ph)
            pr = sb("pr", [P, HG, 2, 2, P], f32, ph)
            prT = sb("prT", [P, 4, HG, P], f32, ph)
            mx = sb("mx", [P, HG * 4], f32, ph)
            rd = sb("rd", [P, 2, H], f32, ph)
            ao = sb("ao", [P, 2, DH, H], f32, ph)
            scores = acc[:, 0:4, :].rearrange("p r (x m) -> p r x m", m=P)
            BT, BU0, BU1 = (4, 5), 6, 7
            s_qk, s_qkc, s_vp, s_vc, s_sc, s_sub, s_ex, s_tp, s_tc, s_o, s_free = (sem(n) for n in (
                "qk_in_psum", "qk_ready", "v_in_psum", "v_ready", "scores_ready", "shifted_ready", "exp_ready",
                "probsT_in_psum", "probsT_ready", "attn_ready", "outputs_out_of_psum"))

            with nc.Block() as block:
                @block.vector
                def _(dve):
                    def rows(i):
                        return [tile_of(i), tile_of(i + PAIRS)]

                    def normalize(i):
                        norm_stats(dve, 0, rows(i))
                        norm_rows(dve, 0, rows(i), [xn[:, 0, :], xn[:, 1, :]])

                    def keep_values(i):
                        dve.wait_ge(s_vp, 1)
                        dve.sem_inc(s_vp, -1)
                        for s in range(2):
                            m = nc.vector.tensor_copy(va[:, bass.ds(i + s * PAIRS, 1), :, 0:DH].rearrange("p a h e -> p (a h) e"),
                                                      bank[BU1][:, 256 + s * P:256 + (s + 1) * P].rearrange("p (h d) -> p h d", h=H))
                            m.then_inc(s_vc if s else s_chain, 1)
                        dve.wait_ge(s_chain, 1)
                        dve.sem_inc(s_chain, -1)

                    def shifted(i):
                        dve.wait_ge(s_sc, 1)
                        dve.sem_inc(s_sc, -1)
                        link(dve, s_chain, nc.vector.tensor_reduce(mx[:, :].rearrange("p (r x) -> p r x", r=HG), scores, AX.X, ALU.max))
                        nc.vector.tensor_tensor(sh[:, :, :, :, :].rearrange("p r s g m -> p r (s g) m"), scores,
                                                mx[:, :].rearrange("p (r x) -> p r x", r=HG).unsqueeze(3).to_broadcast([P, HG, 4, P]),
                                                ALU.subtract).then_inc(s_sub, 1)

                    def finish(i):
                        dve.wait_ge(s_o, 1)
                        dve.sem_inc(s_o, -1)
                        o = bank[BU1][:, 0:272].rearrange("p (s h e) -> p s h e", s=2, h=H)
                        link(dve, s_chain, nc.vector.reciprocal(rd[:, :, :], o[:, :, :, DH]))
                        for s in range(2):
                            nc.vector.tensor_tensor(ao[:, s, :, :].rearrange("p d h -> p h d"), o[:, s, :, 0:DH],
                                                    rd[:, s, :].unsqueeze(2).to_broadcast([P, H, DH]), ALU.mult).then_inc(s_chain, 1)
                        dve.wait_ge(s_chain, 2)
                        dve.sem_inc(s_chain, -2)
                        dve.sem_inc(s_free, 1)
                        for s in range(2):
                            hr = tile_of(i + s * PAIRS)
                            nc.vector.tensor_tensor(hr, hr, ao[:, s, :, :].rearrange("p d h -> p (d h)"), ALU.add).then_inc(s_chain, 1)
                        dve.wait_ge(s_chain, 2)
                        dve.sem_inc(s_chain, -2)

                    def step(i, after=True, later=True, before=True):
                        shifted(i)
                        if after:
                            keep_values(i + 1)
                        if before:
                            finish(i - 1)
                        if later:
                            normalize(i + 2)

                    link(dve, s_chain, nc.vector.memset(va[:, :, :, :], 1.0))
                    dve.sem_inc(s_free, 1)
                    normalize(0)
                    keep_values(0)
                    normalize(1)
                    step(0, before=False)
                    with dve.Fori(1, PAIRS - 2) as i:
                        step(i)
                    step(PAIRS - 2, later=False)
                    step(PAIRS - 1, after=False, later=False)
                    finish(PAIRS - 1)

                @block.gpsimd
                def _(pool):
                    with pool.Fori(0, PAIRS) as i:
                        norm_power(pool, 0, 2)

                @block.scalar
                def _(act):
                    def project():
                        act.wait_ge(s_xTp, 1)
                        act.sem_inc(s_xTp, -1)
                        nc.scalar.activation(xT[:, 0:2, :], bank[BU1][:, 0:256].rearrange("p (s t) -> p s t", s=2), ACT.Copy).then_inc(s_xT, 1)
                        for n in range(2):
                            act.wait_ge(s_qk, 1)
                            act.sem_inc(s_qk, -1)
                            nc.scalar.activation(qk[:, 2 * n:2 * n + 2, :, :], bank[BU0][:, :].rearrange("p (g s t) -> p g s t", g=2, s=2), ACT.Copy).then_inc(s_qkc, 1)

                    def attend():
                        for u in range(4):
                            act.wait_ge(s_tp, 1)
                            act.sem_inc(s_tp, -1)
                            nc.scalar.activation(prT[:, u, :, :], bank[BT[u % 2]][:, :].rearrange("p (h t) -> p h t", h=4), ACT.Copy).then_inc(s_tc, 1)

                    def step(after=True, before=True):
                        if after:
                            project()
                        if before:
                            attend()
                        act.wait_ge(s_sub, 1)
                        act.sem_inc(s_sub, -1)
                        nc.scalar.activation(pr[:, :, :, :, :], sh[:, :, :, :, :], ACT.Exp, scale=float(C) ** -0.5).then_inc(s_ex, 1)

                    project()
                    step(before=False)
                    with act.Fori(1, PAIRS - 1) as i:
                        step()
                    step(after=False)
                    attend()

                @block.tensor
                def _(pe):
                    def project():
                        for s in range(2):
                            pe.wait_ge(s_xn, 1)
                            pe.sem_inc(s_xn, -1)
                            m = nc.tensor.transpose(bank[BU1][:, s * P:(s + 1) * P], xn[:, s, :], ident[:, :])
                        m.then_inc(s_xTp, 1)
                        pe.wait_ge(s_xT, 1)
                        pe.sem_inc(s_xT, -1)
                        for n, w in enumerate((w_q, w_k)):
                            if n:
                                pe.wait_ge(s_qkc, 1)
                                pe.sem_inc(s_qkc, -1)
                            for g in range(2):
                                m = nc.tensor.matmul(bank[BU0][:, g * 256:(g + 1) * 256], w[:, g, :, :], xT[:, 0:2, :], start=True, stop=True)
                            m.then_inc(s_qk, 1)
                            if n == 0:
                                for s in range(2):
                                    m = nc.tensor.matmul(bank[BU1][:, 256 + s * P:256 + (s + 1) * P], xT[:, s, :], w_v[:, :], start=True, stop=True)
                                m.then_inc(s_vp, 1)

                    def score():
                        pe.wait_ge(s_qkc, 1)
                        pe.sem_inc(s_qkc, -1)
                        for s in range(2):
                            for g in range(2):
                                for r in range(HG):
                                    m = nc.tensor.matmul(scores[:, r, 2 * s + g, :], qk[32 * r:32 * r + 32, g, s, :],
                                                         qk[32 * r:32 * r + 32, 2 + g, 1 - s, :], start=True, stop=True)
                        m.then_inc(s_sc, 1)

                    def attend(i):
                        def flip(u):
                            s, half = u // 2, u % 2
                            for x in range(4):
                                r, g = 2 * half + x // 2, x % 2
                                m = nc.tensor.transpose(bank[BT[u % 2]][:, x * P:(x + 1) * P], pr[:, r, s, g, :], ident[:, :])
                            m.then_inc(s_tp, 1)

                        def weigh(s):
                            for u in (2 * s, 2 * s + 1):
                                for x in range(4):
                                    r, g = 2 * (u % 2) + x // 2, x % 2
                                    hd = g * HG + r
                                    v_of = va[:, bass.ds(i + (1 - s) * PAIRS, 1), hd, :].rearrange("p a e -> p (a e)")
                                    m = nc.tensor.matmul(bank[BU1][:, s * 136 + hd * 17:s * 136 + hd * 17 + 17], prT[:, u, x, :], v_of, start=True, stop=True)
                            return m

                        flip(0)
                        flip(1)
                        pe.wait_ge(s_tc, 1)
                        pe.sem_inc(s_tc, -1)
                        flip(2)
                        pe.wait_ge(s_tc, 1)
                        pe.sem_inc(s_tc, -1)
                        flip(3)
                        pe.wait_ge(s_free, 1)
                        pe.sem_inc(s_free, -1)
                        weigh(0)
                        pe.wait_ge(s_tc, 2)
                        pe.sem_inc(s_tc, -2)
                        weigh(1).then_inc(s_o, 1)

                    def step(i, after=True, before=True):
                        if before:
                            pe.wait_ge(s_ex, 1)
                            pe.sem_inc(s_ex, -1)
                        score()
                        if after:
                            project()
                            pe.wait_ge(s_vc, 1)
                            pe.sem_inc(s_vc, -1)
                        if before:
                            attend(i - 1)

                    project()
                    pe.wait_ge(s_vc, 1)
                    pe.sem_inc(s_vc, -1)
                    step(0, before=False)
                    with pe.Fori(1, PAIRS - 1) as i:
                        step(i)
                    step(PAIRS - 1, after=False)
                    pe.wait_ge(s_ex, 1)
                    pe.sem_inc(s_ex, -1)
                    attend(PAIRS - 1)

        with ExitStack() as ph:
            act1 = sb("act1", [P, 2, 2, N_IN], f32, ph)
            act2 = sb("act2", [P, 2, 2, N_PROC], f32, ph)
            ex2 = sb("ex2", [P, 2, 2, N_PROC], f32, ph)
            left = sb("left", [P, 2, 2, N_IN], f32, ph)
            kept = sb("kept", [P, 2, 2, N_IN], f32, ph)
            keptT = sb("keptT", [P, 2, 2, N_IN // P, P], f32, ph)
            aggT = sb("aggT", [D_PV, 2, 2, P], f32, ph)
            top8 = sb("top8", [P, 2, 2, 8], f32, ph)
            nmax = sb("nmax", [P, 2, 2, 1], f32, ph)
            psumr = sb("psumr", [P, 2, 2, 1], f32, ph)
            rden = sb("rden", [P, 2, 2, 1], f32, ph)
            s_a1p, s_a1, s_kept, s_ktp, s_kt, s_prp, s_a2, s_nm, s_ex2, s_agp, s_ag, s_a3p, s_a3, s_op = (sem(n) for n in (
                "in_acts_psum", "acts_ready", "kept_ready", "keptT_psum", "keptT_ready", "proc_psum", "proc_ready", "proc_max",
                "proc_exp", "agg_psum", "agg_ready", "out_acts_psum", "out_acts_ready", "ffn_psum"))
            STEPS = B // 4

            def wide(g):
                return acc[:, 2 * g:2 * g + 2, :]

            def narrow(g):
                return acc[:, 4 + 2 * g:6 + 2 * g, :]

            with nc.Block() as block:
                @block.vector
                def _(dve):
                    def rows(i, g):
                        return [tile_of(4 * i + 2 * g + s) for s in range(2)]

                    def topk(g, k, acts, n):
                        for r in range(k // 8):
                            src = left[:, g, :, 0:n] if r else acts[:, g, :, :]
                            for s in range(2):
                                if r:
                                    dve.wait_ge(s_chain, 1)
                                    dve.sem_inc(s_chain, -1)
                                nc.vector.max(top8[:, g, s, :], src[:, s, :]).then_inc(s_chain, 1)
                            for s in range(2):
                                dve.wait_ge(s_chain, 1)
                                dve.sem_inc(s_chain, -1)
                                if r == 0 and n == N_PROC:
                                    nc.vector.tensor_scalar(nmax[:, g, s, :], top8[:, g, s, 0:1], -1.0, None, ALU.mult).then_inc(s_nm, 1)
                                nc.vector.match_replace(left[:, g, s, 0:n], top8[:, g, s, :], src[:, s, :], GONE).then_inc(s_chain, 1)

                    def keep_largest(g, k, ready, signals):
                        dve.wait_ge(ready, signals)
                        dve.sem_inc(ready, -signals)
                        topk(g, k, act1, N_IN)
                        for s in range(2):
                            dve.wait_ge(s_chain, 1)
                            dve.sem_inc(s_chain, -1)
                            nc.vector.scalar_tensor_tensor(kept[:, g, s, :], left[:, g, s, :], GONE, act1[:, g, s, :], ALU.is_equal, ALU.mult).then_inc(s_kept, 1)

                    def keep_process(g):
                        dve.wait_ge(s_a2, 1)
                        dve.sem_inc(s_a2, -1)
                        topk(g, K_PROC, act2, N_PROC)
                        for s in range(2):
                            dve.wait_ge(s_chain, 1)
                            dve.sem_inc(s_chain, -1)
                            dve.wait_ge(s_ex2, 1)
                            dve.sem_inc(s_ex2, -1)
                            nc.vector.scalar_tensor_tensor(kept[:, g, s, 0:N_PROC], left[:, g, s, 0:N_PROC], GONE, ex2[:, g, s, :],
                                                           ALU.is_equal, ALU.mult, accum_out=psumr[:, g, s, :]).then_inc(s_chain, 1)
                        dve.wait_ge(s_chain, 2)
                        dve.sem_inc(s_chain, -2)
                        nc.vector.reciprocal(rden[:, g, :, :], psumr[:, g, :, :]).then_inc(s_kept, 2)

                    def add_out(i, g):
                        dve.wait_ge(s_op, 1)
                        dve.sem_inc(s_op, -1)
                        hr = h[:, bass.ds(4 * i + 2 * g, 2), :]
                        link(dve, s_chain, nc.vector.tensor_tensor(hr, hr, narrow(g)[:, :, 0:P], ALU.add))

                    def step(i, after=True):
                        for g in range(2):
                            keep_process(g)
                        for g in range(2):
                            if after:
                                norm_stats(dve, 2 * g, rows(i + 1, g))
                            keep_largest(g, K_OUT, s_a3, 2)
                            if after:
                                norm_rows(dve, 2 * g, rows(i + 1, g), [xn[:, 2 * g + s, :] for s in range(2)])
                        for g in range(2):
                            add_out(i, g)
                            if after:
                                keep_largest(g, K_IN, s_a1, 1)

                    for g in range(2):
                        norm_stats(dve, 2 * g, rows(0, g))
                        norm_rows(dve, 2 * g, rows(0, g), [xn[:, 2 * g + s, :] for s in range(2)])
                    for g in range(2):
                        keep_largest(g, K_IN, s_a1, 1)
                    with dve.Fori(0, STEPS - 1) as i:
                        step(i)
                    step(STEPS - 1, after=False)

                @block.gpsimd
                def _(pool):
                    with pool.Fori(0, STEPS) as i:
                        for g in range(2):
                            norm_power(pool, 2 * g, 2)

                @block.scalar
                def _(act):
                    def in_acts(g):
                        act.wait_ge(s_xTp, 1)
                        act.sem_inc(s_xTp, -1)
                        nc.scalar.activation(xT[:, 2 * g:2 * g + 2, :], wide(g)[:, :, 0:P], ACT.Copy).then_inc(s_xT, 1)
                        act.wait_ge(s_a1p, 1)
                        act.sem_inc(s_a1p, -1)
                        nc.scalar.activation(act1[:, g, :, :], wide(g), ACT.Gelu).then_inc(s_a1, 1)

                    def copy_flipped(g, n):
                        act.wait_ge(s_ktp, 1)
                        act.sem_inc(s_ktp, -1)
                        nc.scalar.activation(keptT[:, g, :, 0:n, :], narrow(g)[:, :, 0:n * P].rearrange("p s (c t) -> p s c t", c=n), ACT.Copy).then_inc(s_kt, 1)

                    def step(after=True):
                        for g in range(2):
                            copy_flipped(g, 4)
                            act.wait_ge(s_prp, 1)
                            act.sem_inc(s_prp, -1)
                            nc.scalar.activation(act2[:, g, :, :], narrow(g)[:, :, 0:N_PROC], ACT.Gelu).then_inc(s_a2, 1)
                        for g in range(2):
                            for s in range(2):
                                act.wait_ge(s_nm, 1)
                                act.sem_inc(s_nm, -1)
                                nc.scalar.activation(ex2[:, g, s, :], act2[:, g, s, :], ACT.Exp, bias=nmax[:, g, s, :]).then_inc(s_ex2, 1)
                            copy_flipped(g, 2)
                            act.wait_ge(s_agp, 1)
                            act.sem_inc(s_agp, -1)
                            nc.scalar.activation(aggT[:, g, :, :], narrow(g)[0:D_PV, :, 384:512], ACT.Copy).then_inc(s_ag, 1)
                            act.wait_ge(s_a3p, 1)
                            act.sem_inc(s_a3p, -1)
                            for s in range(2):
                                nc.scalar.activation(act1[:, g, s, :], wide(g)[:, s, :], ACT.Gelu, scale=rden[:, g, s, :]).then_inc(s_a3, 1)
                        for g in range(2):
                            copy_flipped(g, 4)
                            if after:
                                in_acts(g)

                    for g in range(2):
                        in_acts(g)
                    with act.Fori(0, STEPS - 1) as i:
                        step()
                    step(after=False)

                @block.tensor
                def _(pe):
                    def in_acts(g):
                        for s in range(2):
                            pe.wait_ge(s_xn, 1)
                            pe.sem_inc(s_xn, -1)
                            m = nc.tensor.transpose(wide(g)[:, s, 0:P], xn[:, 2 * g + s, :], ident[:, :])
                        m.then_inc(s_xTp, 1)
                        pe.wait_ge(s_xT, 1)
                        pe.sem_inc(s_xT, -1)
                        for s in range(2):
                            m = nc.tensor.matmul(wide(g)[:, s, :], xT[:, 2 * g + s, :], in_pat[:, :], start=True, stop=True)
                        m.then_inc(s_a1p, 1)

                    def flip(g, n):
                        for s in range(2):
                            pe.wait_ge(s_kept, 1)
                            pe.sem_inc(s_kept, -1)
                            for c in range(n):
                                m = nc.tensor.transpose(narrow(g)[:, s, c * P:(c + 1) * P], kept[:, g, s, c * P:(c + 1) * P], ident[:, :])
                        m.then_inc(s_ktp, 1)
                        pe.wait_ge(s_kt, 1)
                        pe.sem_inc(s_kt, -1)

                    def step(after=True):
                        for g in range(2):
                            flip(g, 4)
                            for s in range(2):
                                for c in range(4):
                                    m = nc.tensor.matmul(narrow(g)[:, s, 0:N_PROC], keptT[:, g, s, c, :], proc_w[:, c, :], start=(c == 0), stop=(c == 3))
                            m.then_inc(s_prp, 1)
                        for g in range(2):
                            flip(g, 2)
                            for s in range(2):
                                for c in range(2):
                                    m = nc.tensor.matmul(narrow(g)[0:D_PV, s, 384:512], proc_v[:, c, :], keptT[:, g, s, c, :], start=(c == 0), stop=(c == 1))
                            m.then_inc(s_agp, 1)
                            pe.wait_ge(s_ag, 1)
                            pe.sem_inc(s_ag, -1)
                            for s in range(2):
                                m = nc.tensor.matmul(wide(g)[:, s, :], aggT[:, g, s, :], out_w[:, :], start=True, stop=True)
                            m.then_inc(s_a3p, 1)
                        for g in range(2):
                            flip(g, 4)
                            for s in range(2):
                                for c in range(4):
                                    m = nc.tensor.matmul(narrow(g)[:, s, 0:P], keptT[:, g, s, c, :], out_pat[:, c, :], start=(c == 0), stop=(c == 3))
                            m.then_inc(s_op, 1)
                            if after:
                                in_acts(g)

                    for g in range(2):
                        in_acts(g)
                    with pe.Fori(0, STEPS - 1) as i:
                        step()
                    step(after=False)

        tok_id = sb("tok_id", [P, B])
        top_p = sb("top_p", [P, TOPK, B])
        gates = sb("gates", [P, B, E])
        filled = sb("filled", [P, E])
        w2_all = sb("w2_all", [P, E, NC1, C])
        s_xs = [sem("rows_scattered_a"), sem("rows_scattered_b")]
        s_xf = sem("rows_buffer_free")
        s_w2, s_ids = sem("w2_loaded"), sem("token_numbers_loaded")

        with ExitStack() as ph:
            G = 4
            wedge = sb("wedge", [P, C], f32, ph)
            gram = sb("gram", [P, C], f32, ph)
            wedgeT = sb("wedgeT", [P, C], f32, ph)
            gate = sb("gate", [P, 2, G, C], f32, ph)
            kv = sb("kv", [P, 2, G, 2, C], f32, ph)
            gq = sb("gq", [P, 2, G, C], f32, ph)
            st2 = sb("st2", [P, 2, 2, G, 6], f32, ph)
            mv2 = sb("mv2", [P, 2, 2, G, 2], f32, ph)
            shift = sb("shift", [P, 2, G], f32, ph)
            spread = sb("spread", [P, 2, 2, G], f32, ph)
            unit = sb("unit", [P, 2, G], f32, ph)
            qkn = sb("qkn", [P, G, 2, 2, 64], f32, ph)
            tc = sb("tc", [P, G, 2, 2, 64], f32, ph)
            ts_ = sb("ts_", [P, G, 2, 2, 64], f32, ph)
            rot = sb("rot", [P, 2, G, 2, C], f32, ph)
            rotT = sb("rotT", [P, 2, G, 2, C], f32, ph)
            zT = sb("zT", [P, 2, G, C], f32, ph)
            sm = sb("sm", [P, 2, G, P], f32, ph)
            mx1 = sb("mx1", [P, 2, G], f32, ph)
            nmx1 = sb("nmx1", [P, 2, G], f32, ph)
            rsum = sb("rsum", [P, 2, G], f32, ph)
            esink = sb("esink", [P, 2, G], f32, ph)
            den = sb("den", [P, 2, G], f32, ph)
            rden1 = sb("rden1", [P, 2, G], f32, ph)
            pT = sb("pT", [P, 2, G, P], f32, ph)
            o1 = sb("o1", [P, 2, G, C], f32, ph)
            xr = sb("xr", [P, 2, G, XW], f32, ph)
            lg = sb("lg", [P, 2, G, E], f32, ph)
            pe_ = sb("pe_", [P, 2, G, E], f32, ph)
            wk = sb("wk", [P, 2, G, E], f32, ph)
            pm = sb("pm", [P, 2, G, E], f32, ph)
            red = sb("red", [P, 2, G], f32, ph)
            hot2 = sb("hot2", [P, 2, TOPK, G, E], f32, ph)
            both = sb("both", [P, 2, G, E], f32, ph)
            place = sb("place", [P, 2, G, E], f32, ph)
            hp = sb("hp", [P, 2, TOPK, G, E], f32, ph)
            posf = sb("posf", [P, 2, TOPK, G], f32, ph)
            posi = sb("posi", [P, 2, TOPK, G], i32, ph)
            s_pj, s_gb, s_kvc, s_ge, s_gq, s_qc, s_mv, s_un, s_rot, s_rtp, s_rt, s_zp, s_z, s_s, s_mx, s_p, s_pr1, s_pp, s_pt, s_o1 = (sem(n) for n in (
                "proj_psum", "gate_logits", "kv_ready", "gate_tanh", "gated_q", "state_psum", "moments", "unit_scale", "rotated",
                "rotT_psum", "rotT_ready", "z_psum", "z_ready", "l1_scores", "l1_max", "l1_row_sums", "l1_probs", "l1_probsT_psum", "l1_probsT", "l1_out_psum"))
            s_wd, s_wdt, s_wdc, s_gr = sem("wedge_ready"), sem("wedgeT_psum"), sem("wedgeT_ready"), sem("gram_psum")
            s_lgp, s_lg, s_le, s_both, s_rank, s_pos = (sem(n) for n in (
                "router_logits", "logits_shifted", "router_exp", "choice_ready", "ranks_psum", "positions_ready"))
            STEPS1 = B // (2 * G)

            def banks(g):
                return acc[:, G * g:G * g + G, :]

            with nc.Block() as block:
                @block.sync
                def _(sp):
                    sp.dma_start(tok_id[:, :], a["tok_id"]).then_inc(s_ids, 16)
                    sp.dma_start(w2_all[:, :, :, :], a["w2"]).then_inc(s_w2, 16)

                @block.vector
                def _(dve):
                    v = nc.vector

                    def L(ins):
                        link(dve, s_chain, ins)

                    L(v.tensor_tensor(wedge[:, :], a_m[:, :], a_t[:, :], ALU.subtract))
                    v.tensor_tensor(wedge[:, :], wedge[:, :], ident[:, :], ALU.add).then_inc(s_wd, 1)
                    dve.wait_ge(s_wdt, 1)
                    dve.sem_inc(s_wdt, -1)
                    v.tensor_copy(wedgeT[:, :], bank[6][:, 0:P]).then_inc(s_wdc, 1)
                    dve.wait_ge(s_gr, 1)
                    dve.sem_inc(s_gr, -1)
                    v.tensor_copy(gram[:, :], bank[6][:, P:2 * P]).then_inc(s_wdc, 1)
                    L(v.tensor_copy(filled[:, :], region[:, :]))
                    L(v.memset(xr[:, :, :, :], 0.0))
                    dve.wait_ge(s_ids, 16)
                    with dve.Fori(0, STEPS1) as i:
                        def rows(g):
                            return [tile_of(2 * G * i + G * g + s) for s in range(G)]

                        for g in range(2):
                            norm_stats(dve, G * g, rows(g))
                        for g in range(2):
                            norm_rows(dve, G * g, rows(g), [xn[:, G * g + s, :] for s in range(G)])
                        for g in range(2):
                            dve.wait_ge(s_pj, 1)
                            dve.sem_inc(s_pj, -1)
                            v.tensor_tensor(gate[:, g, :, :], banks(g)[:, :, 3 * C:4 * C], bg_rows[:, :].unsqueeze(1).to_broadcast([P, G, C]), ALU.add).then_inc(s_gb, 1)
                        for g in range(2):
                            dve.wait_ge(s_ge, 1)
                            dve.sem_inc(s_ge, -1)
                            v.scalar_tensor_tensor(gq[:, g, :, :], gate[:, g, :, :], 1.0, banks(g)[:, :, 0:C], ALU.add, ALU.mult).then_inc(s_gq, 1)
                        for g in range(2):
                            for s in range(G):
                                v.bn_stats(st2[:, g, 1, s, :], kv[:, g, s, 0, :]).then_inc(s_chain, 1)
                            dve.wait_ge(s_qc, 1)
                            dve.sem_inc(s_qc, -1)
                            for s in range(G):
                                v.bn_stats(st2[:, g, 0, s, :], banks(g)[:, s, 0:C]).then_inc(s_chain, 1)
                            for x in (1, 0):
                                for s in range(G):
                                    dve.wait_ge(s_chain, 1)
                                    dve.sem_inc(s_chain, -1)
                                    v.bn_aggr(mv2[:, g, x, s, :], st2[:, g, x, s, :]).then_inc(s_mv, 1)
                        for g in range(2):
                            dve.wait_ge(s_un, 1)
                            dve.sem_inc(s_un, -1)
                            for s in range(G):
                                v.tensor_scalar(qkn[:, s, 0, :, :].rearrange("p a b -> p (a b)"), banks(g)[:, s, 0:C],
                                                shift[:, g, s:s + 1], unit[:, g, s:s + 1], ALU.subtract, ALU.mult).then_inc(s_chain, 1)
                                v.tensor_scalar(qkn[:, s, 1, :, :].rearrange("p a b -> p (a b)"), kv[:, g, s, 0, :],
                                                shift[:, g, s:s + 1], unit[:, g, s:s + 1], ALU.subtract, ALU.mult).then_inc(s_chain, 1)
                            dve.wait_ge(s_chain, 2 * G)
                            dve.sem_inc(s_chain, -2 * G)
                            v4 = qkn[:, :, :, :, :].rearrange("p s q x j -> p (s q x) j")
                            v.tensor_tensor(tc[:, :, :, :, :].rearrange("p s q x j -> p (s q x) j"), v4,
                                            cos_t[:, :].unsqueeze(1).to_broadcast([P, 4 * G, 64]), ALU.mult).then_inc(s_chain, 1)
                            L(v.tensor_tensor(ts_[:, :, :, :, :].rearrange("p s q x j -> p (s q x) j"), v4,
                                              sin_t[:, :].unsqueeze(1).to_broadcast([P, 4 * G, 64]), ALU.mult))
                            dve.wait_ge(s_chain, 1)
                            dve.sem_inc(s_chain, -1)
                            r4 = rot[:, g, :, :, :].rearrange("p s q c -> p (s q) c")
                            c4 = tc[:, :, :, :, :].rearrange("p s q x j -> p (s q) x j")
                            n4 = ts_[:, :, :, :, :].rearrange("p s q x j -> p (s q) x j")
                            v.tensor_tensor(r4[:, :, 0:64], c4[:, :, 0, :], n4[:, :, 1, :], ALU.subtract).then_inc(s_chain, 1)
                            v.tensor_tensor(r4[:, :, 64:128], n4[:, :, 0, :], c4[:, :, 1, :], ALU.add).then_inc(s_rot, 1)
                            dve.wait_ge(s_chain, 1)
                            dve.sem_inc(s_chain, -1)
                        for g in range(2):
                            dve.wait_ge(s_s, 1)
                            dve.sem_inc(s_s, -1)
                            v.tensor_tensor(sm[:, g, :, :], banks(g)[:, :, P:2 * P], causal[:, :].unsqueeze(1).to_broadcast([P, G, P]), ALU.add).then_inc(s_chain, 1)
                        for g in range(2):
                            dve.wait_ge(s_chain, 1)
                            dve.sem_inc(s_chain, -1)
                            v.tensor_reduce(mx1[:, g, :], sm[:, g, :, :], AX.X, ALU.max).then_inc(s_chain, 1)
                        for g in range(2):
                            dve.wait_ge(s_chain, 1)
                            dve.sem_inc(s_chain, -1)
                            v.tensor_scalar(nmx1[:, g, :], mx1[:, g, :], sink_c[:, :], -1.0, ALU.max, ALU.mult).then_inc(s_mx, 1)
                        for g in range(2):
                            dve.wait_ge(s_p, 1)
                            dve.sem_inc(s_p, -1)
                            v.tensor_tensor(den[:, g, :], rsum[:, g, :], esink[:, g, :], ALU.add).then_inc(s_chain, 1)
                        for g in range(2):
                            dve.wait_ge(s_chain, 1)
                            dve.sem_inc(s_chain, -1)
                            v.reciprocal(rden1[:, g, :], den[:, g, :]).then_inc(s_chain, 1)
                        dve.wait_ge(s_chain, 2)
                        dve.sem_inc(s_chain, -2)
                        for g in range(2):
                            dve.wait_ge(s_o1, 1)
                            dve.sem_inc(s_o1, -1)
                            for s in range(G):
                                v.scalar_tensor_tensor(o1[:, g, s, :], vnull_rows[:, :], esink[:, g, s:s + 1], banks(g)[:, s, 3 * P:4 * P], ALU.mult, ALU.add).then_inc(s_chain, 1)
                            for s in range(G):
                                dve.wait_ge(s_chain, 1)
                                dve.sem_inc(s_chain, -1)
                                hr = rows(g)[s]
                                v.scalar_tensor_tensor(hr, o1[:, g, s, :], rden1[:, g, s:s + 1], hr, ALU.mult, ALU.add).then_inc(s_chain, 1)
                            dve.wait_ge(s_chain, G)
                            dve.sem_inc(s_chain, -G)
                            norm_stats(dve, G * g, rows(g))
                        for g in range(2):
                            dve.wait_ge(s_xf, 1)
                            dve.sem_inc(s_xf, -1)
                            norm_rows(dve, G * g, rows(g), [xr[:, g, s, 0:C] for s in range(G)])
                            L(v.tensor_copy(xr[:, g, :, C], tok_id[:, bass.ds(2 * G * i + G * g, G)]))
                        for g in range(2):
                            dve.wait_ge(s_lgp, 1)
                            dve.sem_inc(s_lgp, -1)
                            v.tensor_tensor(lg[:, g, :, :], banks(g)[:, :, P:P + E], rb_rows[:, :].unsqueeze(1).to_broadcast([P, G, E]), ALU.add).then_inc(s_chain, 1)
                        dve.wait_ge(s_chain, 2)
                        dve.sem_inc(s_chain, -2)

                        def flat(x):
                            return x[:, :, :, :].rearrange("p g s e -> p (g s) e")

                        def over(x):
                            return x.rearrange("p g s -> p (g s)").unsqueeze(2).to_broadcast([P, 2 * G, E])

                        e_b = eid[:, :].unsqueeze(1).to_broadcast([P, 2 * G, E])
                        redf = red[:, :, :].rearrange("p g s -> p (g s)")
                        L(v.tensor_reduce(redf, flat(lg), AX.X, ALU.max))
                        v.tensor_tensor(flat(lg), flat(lg), over(red[:, :, :]), ALU.subtract).then_inc(s_lg, 1)
                        dve.wait_ge(s_le, 1)
                        dve.sem_inc(s_le, -1)
                        L(v.tensor_reduce(redf, flat(pe_), AX.X, ALU.add))
                        L(v.reciprocal(redf, redf))
                        L(v.tensor_tensor(flat(pe_), flat(pe_), over(red[:, :, :]), ALU.mult))
                        cur = pe_
                        for k in range(TOPK):
                            topk_k = top_p[:, k, bass.ds(2 * G * i, 2 * G)]
                            hot_k = hot2[:, :, k, :, :]
                            L(v.tensor_reduce(redf, flat(cur), AX.X, ALU.max))
                            v.tensor_copy(topk_k, redf).then_inc(s_chain, 1)
                            v.tensor_tensor(flat(wk), flat(cur), over(red[:, :, :]), ALU.is_equal).then_inc(s_chain, 1)
                            dve.wait_ge(s_chain, 2)
                            dve.sem_inc(s_chain, -2)
                            L(v.scalar_tensor_tensor(flat(wk), e_b, -float(E), flat(wk), ALU.add, ALU.mult))
                            L(v.tensor_reduce(redf, flat(wk), AX.X, ALU.min))
                            L(v.tensor_scalar(redf, redf, float(E), None, ALU.add))
                            for g in range(2):
                                if k == 0:
                                    v.tensor_copy(xr[:, g, :, C + 1], red[:, g, :]).then_inc(s_chain, 1)
                                v.tensor_tensor(hot2[:, g, k, :, :], eid[:, :].unsqueeze(1).to_broadcast([P, G, E]),
                                                red[:, g, :].unsqueeze(2).to_broadcast([P, G, E]), ALU.is_equal).then_inc(s_chain, 1)
                            dve.wait_ge(s_chain, 4 - 2 * k)
                            dve.sem_inc(s_chain, -(4 - 2 * k))
                            if k == 0:
                                L(v.scalar_tensor_tensor(pm[:, :, :, :], hot2[:, :, 0, :, :], -2.0, pe_[:, :, :, :], ALU.mult, ALU.add))
                                cur = pm
                        v.tensor_tensor(both[:, :, :, :], hot2[:, :, 0, :, :], hot2[:, :, 1, :, :], ALU.add).then_inc(s_both, 1)
                        dve.wait_ge(s_rank, 1)
                        dve.sem_inc(s_rank, -1)
                        L(v.tensor_tensor(gates[:, bass.ds(2 * G * i, 2 * G), :], flat(both), flat(pe_), ALU.mult))
                        L(v.tensor_tensor(flat(place), bank[0][:, 2 * P:3 * P].rearrange("p (t e) -> p t e", e=E),
                                          filled[:, :].unsqueeze(1).to_broadcast([P, 2 * G, E]), ALU.add))
                        v.tensor_tensor(filled[:, :], filled[:, :], bank[0][:, 3 * P:3 * P + E], ALU.add).then_inc(s_chain, 1)
                        for k in range(TOPK):
                            v.tensor_tensor(hp[:, :, k, :, :], hot2[:, :, k, :, :], place[:, :, :, :], ALU.mult).then_inc(s_chain, 1)
                        dve.wait_ge(s_chain, 3)
                        dve.sem_inc(s_chain, -3)
                        for g in range(2):
                            L(v.tensor_reduce(posf[:, g, :, :], hp[:, g, :, :, :], AX.X, ALU.add))
                            v.tensor_copy(posi[:, g, :, :], posf[:, g, :, :]).then_inc(s_pos, 1)

                @block.gpsimd
                def _(pool):
                    def L(ins):
                        link(pool, s_pchain, ins)

                    g_ = nc.gpsimd
                    pool.sem_inc(s_xf, 2)
                    with pool.Fori(0, STEPS1) as i:
                        for g in range(2):
                            norm_power(pool, G * g, G)
                        for g in range(2):
                            pool.wait_ge(s_mv, 2 * G)
                            pool.sem_inc(s_mv, -2 * G)
                            L(g_.tensor_tensor(shift[:, g, :], mv2[:, g, 0, :, 0], mv2[:, g, 1, :, 0], ALU.add))
                            L(g_.tensor_scalar(shift[:, g, :], shift[:, g, :], 0.5, 0.0, ALU.mult, ALU.add))
                            L(g_.tensor_scalar(spread[:, g, :, :], mv2[:, g, :, :, 1], C / (C - 1.0), 0.0, ALU.mult, ALU.add))
                            sp2 = spread[:, g, :, :].rearrange("p q s -> p (q s)")
                            L(g_.tensor_tensor(sp2, sp2, cst[:, 1:2].to_broadcast([P, 2 * G]), ALU.pow))
                            L(g_.tensor_tensor(unit[:, g, :], spread[:, g, 0, :], spread[:, g, 1, :], ALU.add))
                            L(g_.tensor_scalar(unit[:, g, :], unit[:, g, :], 0.5, 1e-6, ALU.mult, ALU.add))
                            g_.tensor_tensor(unit[:, g, :], unit[:, g, :], cst[:, 2:3].to_broadcast([P, G]), ALU.pow).then_inc(s_un, 1)
                        for g in range(2):
                            norm_power(pool, G * g, G)
                        for g in range(2):
                            pool.wait_ge(s_pos, 1)
                            pool.sem_inc(s_pos, -1)
                            for s in range(G):
                                for k in range(TOPK):
                                    g_.indirect_dma_start(xs_dram[:, :], bass.IndirectOffsetOnAxis(posi[:, g, k, s:s + 1], 0), xr[:, g, s, :], None).then_inc(s_xs[g], 16)
                        for g in range(2):
                            pool.wait_ge(s_xs[g], i * (16 * TOPK * G) + 16 * TOPK * G)
                            pool.sem_inc(s_xf, 1)

                @block.scalar
                def _(act):
                    with act.Fori(0, STEPS1) as i:
                        for g in range(2):
                            act.wait_ge(s_xTp, 1)
                            act.sem_inc(s_xTp, -1)
                            nc.scalar.activation(xT[:, G * g:G * g + G, :], banks(g)[:, :, 0:P], ACT.Copy).then_inc(s_xT, 1)
                        for g in range(2):
                            act.wait_ge(s_gb, 1)
                            act.sem_inc(s_gb, -1)
                            nc.scalar.activation(kv[:, g, :, :, :], banks(g)[:, :, C:3 * C].rearrange("p s (a c) -> p s a c", a=2), ACT.Copy).then_inc(s_kvc, 1)
                            act.wait_ge(s_kvc, 1)
                            act.sem_inc(s_kvc, -1)
                            nc.scalar.activation(gate[:, g, :, :], gate[:, g, :, :], ACT.Tanh, scale=0.5).then_inc(s_ge, 1)
                        for g in range(2):
                            act.wait_ge(s_rtp, 1)
                            act.sem_inc(s_rtp, -1)
                            nc.scalar.activation(rotT[:, g, :, :, :], banks(g)[:, :, P:3 * P].rearrange("p s (a c) -> p s a c", a=2), ACT.Copy).then_inc(s_rt, 1)
                        for g in range(2):
                            act.wait_ge(s_zp, 1)
                            act.sem_inc(s_zp, -1)
                            nc.scalar.activation(zT[:, g, :, :], banks(g)[:, :, 0:P], ACT.Copy, scale=float(C) ** -0.5).then_inc(s_z, 1)
                        for g in range(2):
                            act.wait_ge(s_mx, 1)
                            act.sem_inc(s_mx, -1)
                            for s in range(G):
                                m = nc.scalar.activation(sm[:, g, s, :], sm[:, g, s, :], ACT.Exp, bias=nmx1[:, g, s:s + 1], accum_out=rsum[:, g, s:s + 1])
                            m.then_inc(s_pr1, 1)
                            nc.scalar.activation(esink[:, g, :], nmx1[:, g, :], ACT.Exp, bias=sink_c[:, :]).then_inc(s_p, 1)
                        for g in range(2):
                            act.wait_ge(s_pp, 1)
                            act.sem_inc(s_pp, -1)
                            nc.scalar.activation(pT[:, g, :, :], banks(g)[:, :, 2 * P:3 * P], ACT.Copy).then_inc(s_pt, 1)
                        for g in range(2):
                            act.wait_ge(s_xTp, 1)
                            act.sem_inc(s_xTp, -1)
                            nc.scalar.activation(xT[:, G * g:G * g + G, :], banks(g)[:, :, 0:P], ACT.Copy).then_inc(s_xT, 1)
                        act.wait_ge(s_lg, 1)
                        act.sem_inc(s_lg, -1)
                        nc.scalar.activation(pe_[:, :, :, :], lg[:, :, :, :], ACT.Exp).then_inc(s_le, 1)

                @block.tensor
                def _(pe):
                    pe.wait_ge(s_wd, 1)
                    pe.sem_inc(s_wd, -1)
                    nc.tensor.transpose(bank[6][:, 0:P], wedge[:, :], ident[:, :]).then_inc(s_wdt, 1)
                    pe.wait_ge(s_wdc, 1)
                    pe.sem_inc(s_wdc, -1)
                    nc.tensor.matmul(bank[6][:, P:2 * P], wedgeT[:, :], wedgeT[:, :], start=True, stop=True).then_inc(s_gr, 1)
                    pe.wait_ge(s_wdc, 1)
                    pe.sem_inc(s_wdc, -1)

                    def flip_rows(g, src):
                        pe.wait_ge(s_xn, G)
                        pe.sem_inc(s_xn, -G)
                        for s in range(G):
                            m = nc.tensor.transpose(banks(g)[:, s, 0:P], src(s), ident[:, :])
                        m.then_inc(s_xTp, 1)

                    with pe.Fori(0, STEPS1) as i:
                        for g in range(2):
                            flip_rows(g, lambda s: xn[:, G * g + s, :])
                        for g in range(2):
                            pe.wait_ge(s_xT, 1)
                            pe.sem_inc(s_xT, -1)
                            for s in range(G):
                                m = nc.tensor.matmul(banks(g)[:, s, :], xT[:, G * g + s, :], w_qkvg[:, :], start=True, stop=True)
                            m.then_inc(s_pj, 1)
                        for g in range(2):
                            pe.wait_ge(s_gq, 1)
                            pe.sem_inc(s_gq, -1)
                            for s in range(G):
                                m = nc.tensor.matmul(banks(g)[:, s, 0:C], run_sum[:, :], gq[:, g, s, :], start=True, stop=True)
                            m.then_inc(s_qc, 1)
                        for g in range(2):
                            pe.wait_ge(s_rot, 1)
                            pe.sem_inc(s_rot, -1)
                            for s in range(G):
                                for x in range(2):
                                    m = nc.tensor.transpose(banks(g)[:, s, (1 + x) * P:(2 + x) * P], rot[:, g, s, x, :], ident[:, :])
                            m.then_inc(s_rtp, 1)
                        for g in range(2):
                            pe.wait_ge(s_rt, 1)
                            pe.sem_inc(s_rt, -1)
                            for s in range(G):
                                m = nc.tensor.matmul(banks(g)[:, s, 0:P], gram[:, :], rotT[:, g, s, 0, :], start=True, stop=True)
                            m.then_inc(s_zp, 1)
                        for g in range(2):
                            pe.wait_ge(s_z, 1)
                            pe.sem_inc(s_z, -1)
                            for s in range(G):
                                m = nc.tensor.matmul(banks(g)[:, s, P:2 * P], zT[:, g, s, :], rotT[:, g, s, 1, :], start=True, stop=True)
                            m.then_inc(s_s, 1)
                        for g in range(2):
                            pe.wait_ge(s_pr1, 1)
                            pe.sem_inc(s_pr1, -1)
                            for s in range(G):
                                m = nc.tensor.transpose(banks(g)[:, s, 2 * P:3 * P], sm[:, g, s, :], ident[:, :])
                            m.then_inc(s_pp, 1)
                        for g in range(2):
                            pe.wait_ge(s_pt, 1)
                            pe.sem_inc(s_pt, -1)
                            for s in range(G):
                                m = nc.tensor.matmul(banks(g)[:, s, 3 * P:4 * P], pT[:, g, s, :], kv[:, g, s, 1, :], start=True, stop=True)
                            m.then_inc(s_o1, 1)
                        for g in range(2):
                            flip_rows(g, lambda s: xr[:, g, s, 0:C])
                        for g in range(2):
                            pe.wait_ge(s_xT, 1)
                            pe.sem_inc(s_xT, -1)
                            for s in range(G):
                                m = nc.tensor.matmul(banks(g)[:, s, P:P + E], xT[:, G * g + s, :], r_w[:, :], start=True, stop=True)
                            m.then_inc(s_lgp, 1)
                        pe.wait_ge(s_both, 1)
                        pe.sem_inc(s_both, -1)
                        rank = bank[0][:, 2 * P:3 * P]
                        bf = both[:, :, :, :].rearrange("p g s e -> p (g s e)")
                        nt = 2 * G
                        nc.tensor.matmul(rank, tri[:, :], bf, start=True, stop=False)
                        for d in range(1, nt):
                            nc.tensor.matmul(rank[:, d * E:nt * E], ones[:, :], bf[:, 0:(nt - d) * E], start=False, stop=(d == nt - 1))
                        for t in range(nt):
                            m = nc.tensor.matmul(bank[0][:, 3 * P:3 * P + E], ones[:, :], bf[:, t * E:(t + 1) * E], start=(t == 0), stop=(t == nt - 1))
                        m.then_inc(s_rank, 1)

        with ExitStack() as ph:
            G = 4
            gatesT = sb("gatesT", [P, 4, P], f32, ph)
            count = sb("count", [P, E], f32, ph)
            ntile_i = sb("ntile_i", [P, E], i32, ph)
            ntile = sb("ntile", [P, E], f32, ph)
            last1 = sb("last1", [P, E], f32, ph)
            last2 = sb("last2", [P, E], f32, ph)
            inside = sb("inside", [P, E], f32, ph)
            start_r = sb("start_r", [P, E], f32, ph)
            wkE = sb("wkE", [P, E], f32, ph)
            tab = sb("tab", [P, 4], f32, ph)
            tab_e = sb("tab_e", [P, P], f32, ph)
            tabT = sb("tabT", [2, P], i32, ph)
            pad_at = sb("pad_at", [1, E], i32, ph)
            e_of = sb("e_of", [P, SLOTS], f32, ph)
            xg = sb("xg", [P, NSLOT, XW], f32, ph)
            w1b = sb("w1b", [P, NSLOT, FF + NC1], f32, ph)
            hid = sb("hid", [P, NSLOT, NC1, P], f32, ph)
            yo = sb("yo", [P, 2, G, C], f32, ph)
            own = sb("own", [P, 2, G], f32, ph)
            dest = sb("dest", [P, 2, G], i32, ph)
            yg = sb("yg", [P, TOPK, B, C], f32, ph)
            s_gt, s_tab, s_tp2, s_ej, s_pad = (sem(n) for n in ("gatesT_psum", "table_ready", "table_psum", "expert_table", "pads_written"))
            s_pa = sem("pad_places")
            s_b2p, s_gtc = sem("b2_psum"), sem("gatesT_ready")
            s_ld = [sem(f"tile_loaded_{n}") for n in range(NSLOT)]
            s_fr, s_xgp, s_xg, s_hp, s_hid, s_yp, s_bk, s_y = (sem(n) for n in (
                "weights_free", "xgT_psum", "xgT_ready", "hidden_psum", "hidden_ready", "y_psum", "y_out_of_psum", "y_ready"))
            s_ys = [sem("y_scattered_a"), sem("y_scattered_b")]
            s_own = sem("row_numbers_read")
            s_all, s_yf = sem("all_y_scattered"), sem("y_buffer_free")
            s_yg, s_out, s_fin = [sem(f"y_rows_loaded_{g}") for g in range(8)], sem("out_stored"), sem("out_ready")
            NSTEP = SLOTS // NSLOT
            with nc.Block() as block:
                @block.vector
                def _(dve):
                    v = nc.vector

                    def L(ins):
                        link(dve, s_chain, ins)
                    dve.wait_ge(s_gt, 1)
                    dve.sem_inc(s_gt, -1)
                    v.tensor_copy(gatesT[:, :, :], bank[2][:, :].rearrange("p (g t) -> p g t", g=4)).then_inc(s_gtc, 1)
                    v.tensor_copy(pad_at[:, :], filled[0:1, :]).then_inc(s_pa, 1)
                    L(v.tensor_tensor(count[:, :], filled[:, :], region[:, :], ALU.subtract))
                    L(v.tensor_scalar(ntile_i[:, :], count[:, :], P - 1.0, None, ALU.add))
                    L(v.tensor_scalar(ntile_i[:, :], ntile_i[:, :], 7, None, ALU.logical_shift_right))
                    L(v.tensor_copy(ntile[:, :], ntile_i[:, :]))
                    s2, d2 = ntile, last1
                    step = 1
                    while step < E:
                        v.tensor_copy(d2[:, 0:step], s2[:, 0:step]).then_inc(s_chain, 1)
                        L(v.tensor_tensor(d2[:, step:E], s2[:, step:E], s2[:, 0:E - step], ALU.add))
                        dve.wait_ge(s_chain, 1)
                        dve.sem_inc(s_chain, -1)
                        s2, d2 = d2, (last2 if d2 is last1 else last1)
                        step *= 2
                    ends, base = s2, d2
                    me = cst[:, 3:4]
                    L(v.tensor_tensor(base[:, :], ends[:, :], ntile[:, :], ALU.subtract))
                    L(v.tensor_scalar(inside[:, :], ends[:, :], me, None, ALU.is_le))
                    L(v.tensor_reduce(tab[:, 0:1], inside[:, :], AX.X, ALU.add))
                    L(v.tensor_scalar(tab[:, 0:1], tab[:, 0:1], E - 1.0, None, ALU.min))
                    L(v.tensor_scalar(wkE[:, :], base[:, :], me, None, ALU.is_le))
                    L(v.tensor_tensor(inside[:, :], wkE[:, :], inside[:, :], ALU.subtract))
                    L(v.tensor_reduce(tab[:, 2:3], inside[:, :], AX.X, ALU.add))
                    L(v.tensor_scalar(start_r[:, :], base[:, :], me, -float(P), ALU.subtract, ALU.mult))
                    L(v.tensor_tensor(start_r[:, :], start_r[:, :], region[:, :], ALU.add))
                    L(v.tensor_tensor(start_r[:, :], start_r[:, :], inside[:, :], ALU.mult))
                    L(v.tensor_reduce(tab[:, 1:2], start_r[:, :], AX.X, ALU.add))
                    L(v.tensor_scalar(tab[:, 2:3], tab[:, 2:3], -float(E * REGION), float(E * REGION), ALU.mult, ALU.add))
                    L(v.tensor_tensor(tab[:, 1:2], tab[:, 1:2], tab[:, 2:3], ALU.add))
                    v.tensor_copy(tab_e[:, :], tab[:, 0:1].to_broadcast([P, P])).then_inc(s_tab, 1)
                    dve.wait_ge(s_tp2, 1)
                    dve.sem_inc(s_tp2, -1)
                    v.tensor_copy(tabT[:, :], bank[3][0:2, 0:P]).then_inc(s_ej, 1)
                    L(v.tensor_copy(e_of[:, :], bank[3][:, P:P + SLOTS]))
                    for g in range(8):
                        dve.wait_ge(s_b2p, 1)
                        dve.sem_inc(s_b2p, -1)
                        v.tensor_tensor(h[:, 4 * g:4 * g + 4, :], h[:, 4 * g:4 * g + 4, :], bank[4 + g % 2][:, :].rearrange("p (t c) -> p t c", t=4), ALU.add).then_inc(s_bk, 1)
                    dve.sem_inc(s_own, 2)
                    with dve.Fori(0, NSTEP) as j:
                        dve.wait_ge(s_own, 2)
                        dve.sem_inc(s_own, -2)
                        for g in range(2):
                            dve.wait_ge(s_xgp, 1)
                            dve.sem_inc(s_xgp, -1)
                            sl = slice(G * g, G * g + G)
                            L(v.tensor_tensor(own[:, g, :], xg[:, sl, C + 1], e_of[:, bass.ds(NSLOT * j + G * g, G)], ALU.not_equal))
                            L(v.scalar_tensor_tensor(own[:, g, :], own[:, g, :], float(B * P), xg[:, sl, C], ALU.mult, ALU.add))
                            v.tensor_copy(xT[:, sl, :], acc[:, sl, 0:P]).then_inc(s_xg, 1)
                        for g in range(2):
                            sl = slice(G * g, G * g + G)
                            dve.wait_ge(s_yp, 1)
                            dve.sem_inc(s_yp, -1)
                            dve.wait_ge(s_yf, 1)
                            dve.sem_inc(s_yf, -1)
                            v.tensor_copy(yo[:, g, :, :], acc[:, sl, 0:P]).then_inc(s_bk, 1)
                            v.tensor_copy(dest[:, g, :], own[:, g, :]).then_inc(s_y, 1)
                    for g in range(8):
                        dve.wait_ge(s_yg[g], 16 * TOPK)
                        for n in range(TOPK):
                            for t in range(4 * g, 4 * g + 4):
                                v.scalar_tensor_tensor(h[:, t, :], yg[:, n, t, :], top_p[:, n, t:t + 1], h[:, t, :], ALU.mult, ALU.add).then_inc(s_fin if n else s_chain, 1)
                            if n == 0:
                                dve.wait_ge(s_chain, 4)
                                dve.sem_inc(s_chain, -4)

                @block.gpsimd
                def _(pool):
                    pool.sem_inc(s_yf, 2)
                    with pool.Fori(0, NSTEP) as j:
                        for g in range(2):
                            pool.wait_ge(s_y, 1)
                            pool.sem_inc(s_y, -1)
                            pool.sem_inc(s_own, 1)
                            for s in range(G):
                                nc.gpsimd.indirect_dma_start(ys_dram[:, :], bass.IndirectOffsetOnAxis(dest[:, g, s:s + 1], 0), yo[:, g, s, :], None,
                                                             bounds_check=TOPK * B * P - 1, oob_is_err=False).then_inc(s_ys[g], 16)
                        for g in range(2):
                            pool.wait_ge(s_ys[g], j * (16 * G) + 16 * G)
                            pool.sem_inc(s_yf, 1)
                    pool.sem_inc(s_all, 1)

                @block.sync
                def _(sp):
                    for g in range(2):
                        sp.wait_ge(s_xs[g], 16 * TOPK * G * STEPS1)
                    sp.wait_ge(s_w2, 16)
                    sp.dma_start(xs_dram[E * REGION:E * REGION + P, :], pad_rows[:, :]).then_inc(s_pad, 16)
                    sp.wait_ge(s_pa, 1)
                    sp.sem_inc(s_pa, -1)
                    for e in range(E):
                        at = sp.value_load(pad_at[0:1, e:e + 1], min_val=e * REGION, max_val=e * REGION + B * P)
                        sp.dma_start(xs_dram[bass.ds(at, P), :], pad_rows[:, :]).then_inc(s_pad, 16)
                    sp.wait_ge(s_ej, 1)
                    sp.sem_inc(s_ej, -1)
                    sp.wait_ge(s_pad, 16 * (E + 1))
                    with sp.Fori(0, NSTEP) as j:
                        for n in range(NSLOT):
                            sp.wait_ge(s_fr, 1)
                            sp.sem_inc(s_fr, -1)
                            ex = sp.value_load(tabT[0:1, bass.ds(NSLOT * j + n, 1)], min_val=0, max_val=E - 1)
                            row = sp.value_load(tabT[1:2, bass.ds(NSLOT * j + n, 1)], min_val=0, max_val=E * REGION)
                            sp.dma_start(xg[:, n, :], xs_dram[bass.ds(row, P), :]).then_inc(s_ld[n], 16)
                            sp.dma_start(w1b[:, n, :], a["w1b"][bass.ds(ex, 1), :, :].rearrange("a p f -> (a p) f")).then_inc(s_ld[n], 16)
                    sp.wait_ge(s_all, 1)
                    sp.sem_inc(s_all, -1)
                    ysv = ys_dram.rearrange("(n b p) c -> n p b c", n=TOPK, p=P)
                    for g in range(8):
                        for n in range(TOPK):
                            sp.dma_start(yg[:, n, 4 * g:4 * g + 4, :], ysv[n, :, 4 * g:4 * g + 4, :]).then_inc(s_yg[g], 16)
                    for g in range(8):
                        sp.wait_ge(s_fin, 4 * (g + 1))
                        sp.dma_start(out[4 * g:4 * g + 4, :, :].rearrange("b p c -> p b c"), h[:, 4 * g:4 * g + 4, :]).then_inc(s_out, 16)
                    sp.wait_ge(s_out, 16 * 8)

                @block.scalar
                def _(act):
                    with act.Fori(0, NSTEP) as j:
                        for n in range(NSLOT):
                            act.wait_ge(s_hp, 1)
                            act.sem_inc(s_hp, -1)
                            for c in range(NC1):
                                m = nc.scalar.activation(hid[:, n, c, :], acc[:, n, c * P:(c + 1) * P], ACT.Gelu, bias=w1b[:, n, FF + c:FF + c + 1])
                            m.then_inc(s_hid, 1)

                @block.tensor
                def _(pe):
                    for g in range(4):
                        m = nc.tensor.transpose(bank[2][:, g * P:(g + 1) * P], gates[:, 8 * g:8 * g + 8, :], ident[:, :])
                    m.then_inc(s_gt, 1)
                    pe.wait_ge(s_tab, 1)
                    pe.sem_inc(s_tab, -1)
                    nc.tensor.matmul(bank[3][0:2, 0:P], tab[:, 0:2], ident[:, :], start=True, stop=True)
                    nc.tensor.matmul(bank[3][:, P:P + SLOTS], tab_e[:, :], ident[:, 0:SLOTS], start=True, stop=True).then_inc(s_tp2, 1)
                    pe.wait_ge(s_gtc, 1)
                    pe.sem_inc(s_gtc, -1)
                    for g in range(8):
                        if g >= 2:
                            pe.wait_ge(s_bk, 1)
                            pe.sem_inc(s_bk, -1)
                        nc.tensor.matmul(bank[4 + g % 2][:, :], gatesT[:, g // 2, :], b2_blocks[:, 4 * (g % 2):4 * (g % 2) + 4, :], start=True, stop=True).then_inc(s_b2p, 1)
                    pe.sem_inc(s_fr, NSLOT)
                    with pe.Fori(0, NSTEP) as j:
                        ex = [pe.value_load(tabT[0:1, bass.ds(NSLOT * j + n, 1)], min_val=0, max_val=E - 1) for n in range(NSLOT)]
                        for g in range(2):
                            pe.wait_ge(s_bk, 1)
                            pe.sem_inc(s_bk, -1)
                            for s in range(G):
                                n = G * g + s
                                pe.wait_ge(s_ld[n], 32)
                                pe.sem_inc(s_ld[n], -32)
                                m = nc.tensor.transpose(acc[:, n, 0:P], xg[:, n, 0:C], ident[:, :])
                            m.then_inc(s_xgp, 1)
                        for g in range(2):
                            pe.wait_ge(s_xg, 1)
                            pe.sem_inc(s_xg, -1)
                            for s in range(G):
                                n = G * g + s
                                for c in range(NC1):
                                    m = nc.tensor.matmul(acc[:, n, c * P:(c + 1) * P], w1b[:, n, c * P:(c + 1) * P], xT[:, n, :], start=True, stop=True)
                                m.then_inc(s_hp, 1)
                        for g in range(2):
                            for s in range(G):
                                n = G * g + s
                                pe.wait_ge(s_hid, 1)
                                pe.sem_inc(s_hid, -1)
                                pe.sem_inc(s_fr, 1)
                                for c in range(NC1):
                                    m = nc.tensor.matmul(acc[:, n, 0:P], hid[:, n, c, :], w2_all[:, bass.ds(ex[n], 1), c, :].rearrange("p a c -> p (a c)"), start=(c == 0), stop=(c == NC1 - 1))
                            m.then_inc(s_yp, 1)


def kernel(**inputs):
    import concourse.bacc as _bacc
    from concourse.bass_utils import run_bass_kernel_spmd as _run

    x = {k: np.asarray(v) for k, v in inputs.items()}
    f = np.float32
    n = np.arange(64)
    win = 0.5 - 0.5 * np.cos(2.0 * np.pi * n / 64)
    dft = np.zeros((P, 2, NFRAME, NFREQ), np.float64)
    for fr in range(NFRAME):
        at = fr * 64 + n - 32
        at = np.where(at < 0, -at, at)
        at = np.where(at > P - 1, 2 * (P - 1) - at, at)
        for k in range(NFREQ):
            np.add.at(dft[:, 0, fr, k], at, win * np.cos(2 * np.pi * k * n / 64))
            np.add.at(dft[:, 1, fr, k], at, -win * np.sin(2 * np.pi * k * n / 64))
    l = np.arange(P)
    inv = (1.0 / 10000.0 ** (np.arange(0, C, 2, dtype=f) / f(C))).astype(f)
    fr = l[:, None].astype(f) * inv[None, :]
    same = (l[:, None] // 64) == (l[None, :] // 64)
    run = (same & (l[:, None] <= l[None, :])) + 2.0 * ((l[:, None] < 64) & (l[None, :] >= 64))
    cst = np.tile(np.array([-0.5, 0.5, -1.0, 0.0], f), (P, 1))
    cst[:, 3] = l
    pad = np.zeros((P, XW), f)
    pad[:, C], pad[:, C + 1] = SKIP, -1.0
    tok = x["x"].astype(np.int32)
    proj = x["L0_tok_proj_w"].reshape(NFREQ, V, D_STFT)
    eo = np.concatenate([np.arange(0, C, 2), np.arange(1, C, 2)])
    w1 = x["L1_ffn_w1"].transpose(0, 2, 1)
    b1 = x["L1_ffn_b1"].reshape(E, NC1, P).transpose(0, 2, 1)
    A = x["L1_attn_A"][0]
    arrays = {
        "idsT": tok.T, "ids": tok.reshape(-1), "emb": x["L0_tok_emb_table"], "dft": dft.reshape(P, 2 * NFRAME, NFREQ).astype(f),
        "pw": proj, "pb": x["L0_tok_proj_b"], "up": ((l[None, :] * 3 // P) == np.arange(3)[:, None]).astype(f),
        "eid": np.arange(E).astype(f), "region": (REGION * np.arange(E)).astype(f), "pad_rows": pad, "tok_id": (P * np.arange(B)[None, :] + l[:, None]).astype(f), "cst": cst, "ident": np.eye(P, dtype=f),
        "w_q": x["L0_attn_q_w"].T.reshape(C, 2, HG, DH), "w_k": x["L0_attn_kv_w"][:C].T.reshape(C, 2, HG, DH),
        "w_v": x["L0_attn_kv_w"][C:].T, "in_pat": x["L0_ffn_input_patterns"].T,
        "proc_w": x["L0_ffn_process_input_weights"].T.reshape(4, P, N_PROC).transpose(1, 0, 2),
        "proc_v": x["L0_ffn_process_values"].reshape(2, P, D_PV).transpose(1, 0, 2),
        "out_w": x["L0_ffn_output_input_weights"].T,
        "out_pat": x["L0_ffn_output_patterns"].reshape(4, P, C).transpose(1, 0, 2),
        "w_qkvg": np.concatenate([x["L1_attn_Wq"][eo], x["L1_attn_Wk"][eo], x["L1_attn_Wv"], x["L1_attn_Wg"][eo]]).T,
        "bg": x["L1_attn_bg"][eo], "A": A, "AT": A.T, "sink": x["L1_attn_sink"].reshape(1), "v_null": x["L1_attn_v_null"].reshape(C),
        "cos": np.cos(fr).astype(f), "sin": np.sin(fr).astype(f), "run_sum": (0.5 * run).astype(f),
        "causal": np.where(l[:, None] >= l[None, :], 0.0, -BIG).astype(f),
        "r_w": x["L1_ffn_router_w"].T, "r_b": x["L1_ffn_router_b"], "tri": (l[:, None] < l[None, :]).astype(f),
        "w2": x["L1_ffn_w2"].reshape(E, C, NC1, P).transpose(3, 0, 2, 1), "b2": x["L1_ffn_b2"],
        "w1b": np.concatenate([w1, b1], axis=2),
    }
    nc = _bacc.Bacc("TRN2", target_bir_lowering=False, num_devices=1)
    args, ins = {}, {}
    for k, v in arrays.items():
        v = np.ascontiguousarray(v)
        ins["in_" + k] = v
        args[k] = nc.dram_tensor("in_" + k, v.shape, mybir.dt.from_np(v.dtype), kind="ExternalInput").ap()
    out = nc.dram_tensor("out_0", (B, P, C), mybir.dt.float32, kind="ExternalOutput").ap()
    build(nc, args, out)
    r = _run(nc, [ins], core_ids=[0])
    return r.results[0]["out_0"]
```

```python
import numpy as np
import concourse.bass as bass
from concourse import mybir
from contextlib import ExitStack

P = 128
B = 32
C = 128
V = 16
D_EMB, D_STFT = 89, 39
NFREQ, NFRAME = 33, 3
H, DH = 8, 16
HG = 4
N_IN, N_PROC, N_OUT, D_PV = 512, 256, 512, 64
K_IN, K_PROC, K_OUT = 64, 128, 64
E, FF, TOPK = 16, 512, 2
NC1 = FF // P
NSLOT = 8
WAYS = 12
SLOTS = -(-((B * P * TOPK + E * (P - 1)) // P) // 2) * 2
REGION = 2 * B * P
XW = C + 4
SKIP = 2.0 ** 20
LN_EPS = 1e-5
GONE = -1e30
BIG = 1e30
PAIRS = B // 2
WINDOW, WINDOW_PROC = 16, 24
WIDEST = max(WINDOW, WINDOW_PROC)
COUNTS = 3
HALF_MEAN = 0.3989
FIRST_IN, FIRST_OUT = 1.2, 1.4
RANKS_IN, RANKS_OUT = 0.29 * N_IN, 0.27 * N_OUT
RANKS_PROC = 0.55 * N_PROC
LEAST_T = 1e-30




def build(nc, a, out):
    f32, i32, bf16 = mybir.dt.float32, mybir.dt.int32, mybir.dt.bfloat16
    ALU, ACT, AX = mybir.AluOpType, mybir.ActivationFunctionType, mybir.AxisListType
    xs_dram = nc.dram_tensor("xs_rows", (E * REGION, XW), f32, kind="Internal").ap()
    ys_dram = nc.dram_tensor("ys_rows", (TOPK * B * P, C), f32, kind="Internal").ap()

    with ExitStack() as ctx:
        def sb(name, shape, dt=f32, stack=ctx):
            return stack.enter_context(nc.sbuf_tensor(name, shape, dt))

        def sem(name):
            return ctx.enter_context(nc.semaphore(name))

        acc = ctx.enter_context(nc.psum_tensor("acc", [P, 8, 512], f32))
        bank = [acc[:, i, :] for i in range(8)]

        h = sb("h", [P, B, C])
        ident = sb("ident", [P, P])
        w_q = sb("w_q", [P, 2, HG, 32])
        w_k = sb("w_k", [P, 2, HG, 32])
        w_v = sb("w_v", [P, C])
        in_pat = sb("in_pat", [P, N_IN])
        proc_w = sb("proc_w", [P, N_IN // P, N_PROC])
        proc_v = sb("proc_v", [P, N_PROC // P, D_PV])
        out_w = sb("out_w", [D_PV, N_OUT])
        out_pat = sb("out_pat", [P, N_OUT // P, C])
        w_qkvg = sb("w_qkvg", [P, 4 * C])
        bg_rows = sb("bg_rows", [P, C])
        a_m = sb("a_m", [P, C])
        a_t = sb("a_t", [P, C])
        sink_c = sb("sink_c", [P, 1])
        vnull_rows = sb("vnull_rows", [P, C])
        cos_t = sb("cos_t", [P, 64])
        sin_t = sb("sin_t", [P, 64])
        run_sum = sb("run_sum", [P, P])
        causal = sb("causal", [P, P])
        r_w = sb("r_w", [P, E])
        rb_rows = sb("rb_rows", [P, E])
        b2_blocks = sb("b2_blocks", [P, 8, C])
        tri = sb("tri", [P, P])
        ones = sb("ones", [P, P])
        eid = sb("eid", [P, E])
        region = sb("region", [P, E])
        pad_rows = sb("pad_rows", [P, XW])
        rank_no = sb("rank_no", [P, WIDEST])
        cst = sb("cst", [P, 4])

        stats = sb("stats", [P, 2 * NSLOT, 6])
        mv = sb("mv", [P, 2 * NSLOT, 2])
        rstd = sb("rstd", [P, 2 * NSLOT])
        xn = sb("xn", [P, NSLOT, C])
        xT = sb("xT", [P, NSLOT, C])

        load_names = ["ids", "spectra", "weights"]
        s_load = {n: sem("loaded_" + n) for n in load_names}
        s_chain = sem("dve_done")
        s_pchain = sem("pool_done")
        s_achain = sem("act_done")

        def link(eng, chain, ins):
            ins.then_inc(chain, 1)
            eng.wait_ge(chain, 1)
            eng.sem_inc(chain, -1)

        with ExitStack() as ph:
            ids_c = sb("ids_c", [P, B], i32, ph)
            ids_r = sb("ids_r", [V, B * P], i32, ph)
            hot = sb("hot", [P, B, V], f32, ph)
            hotT = sb("hotT", [V, B * P], f32, ph)
            emb = sb("emb", [V, D_EMB], f32, ph)
            dft = sb("dft", [P, 2 * NFRAME, NFREQ], f32, ph)
            sq = sb("sq", [NFREQ, 2, NFRAME, B * V], f32, ph)
            mag = sb("mag", [NFREQ, NFRAME, B, V], f32, ph)
            pw = sb("pw", [NFREQ, V, D_STFT], f32, ph)
            pb = sb("pb", [NFRAME * B, D_STFT], f32, ph)
            enc = sb("enc", [NFRAME * B, D_STFT], f32, ph)
            encF = sb("encF", [NFRAME, B, D_STFT], f32, ph)
            up = sb("up", [NFRAME, P], f32, ph)
            s_zeroed, s_hot, s_spec, s_sq, s_sum, s_mag, s_enc, s_encs, s_encf = (sem(n) for n in (
                "zeroed", "hot_ready", "spectra_ready", "squares_ready", "power_ready", "mag_ready",
                "enc_ready", "enc_rows_ready", "enc_frames_ready"))
            FIRST_ROWS = 4
            s_emb, s_embc, s_ide = sem("emb_ready"), sem("emb_copied"), sem("stft_ready")
            with nc.Block() as block:
                @block.sync
                def _(sp):
                    first = [(ids_c[:, :], a["idsT"]), (eid[:, :], a["eid"].partition_broadcast(P)),
                             (ids_r[:, :], a["ids"].partition_broadcast(V)), (cst[:, :], a["cst"])]
                    spectra = [(dft[:, :, :], a["dft"]), (emb[:, :], a["emb"]), (pw[:, :, :], a["pw"]),
                               (pb[:, :], a["pb"].partition_broadcast(NFRAME * B)), (up[:, :], a["up"]), (ident[:, :], a["ident"])]
                    for dst, src in first:
                        sp.dma_start(dst, src).then_inc(s_load["ids"], 16)
                    for dst, src in spectra:
                        sp.dma_start(dst, src).then_inc(s_load["spectra"], 16)
                    rest = [(in_pat[:, :], a["in_pat"]), (proc_w[:, :, :], a["proc_w"]), (proc_v[:, :, :], a["proc_v"]),
                            (w_v[:, :], a["w_v"]), (out_w[:, :], a["out_w"]), (out_pat[:, :, :], a["out_pat"]),
                            (w_qkvg[:, :], a["w_qkvg"]), (bg_rows[:, :], a["bg"].partition_broadcast(P)),
                            (a_m[:, :], a["A"]), (a_t[:, :], a["AT"]), (sink_c[:, :], a["sink"].partition_broadcast(P)),
                            (vnull_rows[:, :], a["v_null"].partition_broadcast(P)), (cos_t[:, :], a["cos"]),
                            (sin_t[:, :], a["sin"]), (run_sum[:, :], a["run_sum"]), (causal[:, :], a["causal"]),
                            (r_w[:, :], a["r_w"]), (rb_rows[:, :], a["r_b"].partition_broadcast(P)),
                            (tri[:, :], a["tri"]), (region[:, :], a["region"].partition_broadcast(P)),
                            (pad_rows[:, :], a["pad_rows"]), (rank_no[:, :], a["rank_no"].partition_broadcast(P))]
                    sp.wait_ge(s_zeroed, 4)
                    for g in range(2):
                        for w, src in ((w_q, a["w_q"]), (w_k, a["w_k"])):
                            rest.append((w[:, g, :, 0:DH], src[:, g, :, :]))
                    for t in range(8):
                        rest.append((b2_blocks[E * t:E * t + E, t, :], a["b2"]))
                    for dst, src in rest:
                        sp.dma_start(dst, src).then_inc(s_load["weights"], 16)
                    sp.wait_ge(s_encs, 1)
                    sp.sem_inc(s_encs, -1)
                    for f in range(NFRAME):
                        sp.dma_start(encF[f:f + 1, :, :], enc[B * f:B * f + B, :]).then_inc(s_encf, 16)
                    sp.wait_ge(s_load["weights"], 16 * len(rest))

                @block.gpsimd
                def _(pool):
                    nc.gpsimd.memset(w_q[:, :, :, :], 0.0).then_inc(s_zeroed, 1)
                    nc.gpsimd.memset(w_k[:, :, :, :], 0.0).then_inc(s_zeroed, 1)
                    nc.gpsimd.memset(b2_blocks[:, :, :], 0.0).then_inc(s_zeroed, 1)
                    nc.gpsimd.memset(ones[:, :], 1.0).then_inc(s_zeroed, 1)

                @block.vector
                def _(dve):
                    dve.wait_ge(s_load["ids"], 16 * 4)
                    nc.vector.tensor_tensor(hot[:, :, :], ids_c[:, :].unsqueeze(2).to_broadcast([P, B, V]),
                                            eid[:, :].unsqueeze(1).to_broadcast([P, B, V]), ALU.is_equal).then_inc(s_hot, 1)
                    nc.vector.tensor_scalar(hotT[:, :], ids_r[:, :], cst[0:V, 3:4], None, ALU.is_equal).then_inc(s_hot, 1)
                    def table_rows(g):
                        dve.wait_ge(s_emb, 1)
                        dve.sem_inc(s_emb, -1)
                        nc.vector.tensor_copy(h[:, 4 * g:4 * g + 4, 0:D_EMB],
                                              bank[g % 2][:, 0:4 * D_EMB].rearrange("p (b e) -> p b e", b=4)).then_inc(s_embc, 1)

                    table_rows(0)
                    dve.wait_ge(s_sq, 6)
                    nc.vector.tensor_tensor(mag[:, :, :, :].rearrange("f a b v -> f a (b v)"), sq[:, 0, :, :], sq[:, 1, :, :], ALU.add).then_inc(s_sum, 1)
                    for g in range(1, FIRST_ROWS):
                        table_rows(g)
                    dve.wait_ge(s_enc, 1)
                    dve.sem_inc(s_enc, -1)
                    dve.wait_ge(s_load["spectra"], 16 * 6)
                    nc.vector.tensor_tensor(enc[:, :], bank[6][0:NFRAME * B, 0:D_STFT], pb[:, :], ALU.add).then_inc(s_encs, 1)
                    for g in range(FIRST_ROWS, B // 4):
                        table_rows(g)

                @block.scalar
                def _(act):
                    for f in range(2 * NFRAME):
                        act.wait_ge(s_spec, 1)
                        act.sem_inc(s_spec, -1)
                        nc.scalar.activation(sq[:, f // NFRAME, f % NFRAME, :], bank[2 + f % 4][0:NFREQ, :], ACT.Square).then_inc(s_sq, 1)
                    act.wait_ge(s_sum, 1)
                    act.sem_inc(s_sum, -1)
                    nc.scalar.activation(mag[:, :, :, :], mag[:, :, :, :], ACT.Sqrt).then_inc(s_mag, 1)
                    for g in range(4):
                        act.wait_ge(s_ide, 1)
                        act.sem_inc(s_ide, -1)
                        nc.scalar.activation(h[:, 8 * g:8 * g + 8, D_EMB:C],
                                             bank[2 + g][:, 0:8 * D_STFT].rearrange("p (b e) -> p b e", b=8), ACT.Copy).then_inc(s_achain, 1)
                    act.wait_ge(s_achain, 4)
                    act.sem_inc(s_achain, -4)

                @block.tensor
                def _(pe):
                    pe.wait_ge(s_load["spectra"], 16 * 6)
                    pe.wait_ge(s_hot, 2)
                    for f in range(2 * NFRAME):
                        if f >= 4:
                            pe.wait_ge(s_sq, f - 3)
                        nc.tensor.matmul(bank[2 + f % 4][0:NFREQ, :], dft[:, f, :], hot[:, :, :], start=True, stop=True).then_inc(s_spec, 1)
                    def table_rows(g):
                        if g >= 2:
                            pe.wait_ge(s_embc, g - 1)
                        for b in range(4):
                            t = 4 * g + b
                            m = nc.tensor.matmul(bank[g % 2][:, b * D_EMB:(b + 1) * D_EMB], hotT[:, t * P:(t + 1) * P], emb[:, :], start=True, stop=True)
                        m.then_inc(s_emb, 1)

                    for g in range(FIRST_ROWS):
                        table_rows(g)
                    pe.wait_ge(s_mag, 1)
                    pe.sem_inc(s_mag, -1)
                    for v in range(V):
                        m = nc.tensor.matmul(bank[6][0:NFRAME * B, 0:D_STFT], mag[:, :, :, v], pw[:, v, :], start=(v == 0), stop=(v == V - 1))
                    m.then_inc(s_enc, 1)
                    for g in range(FIRST_ROWS, B // 4):
                        table_rows(g)
                    pe.wait_ge(s_encf, 16 * NFRAME)
                    for g in range(4):
                        nc.tensor.matmul(bank[2 + g][:, 0:8 * D_STFT], up[:, :], encF[:, 8 * g:8 * g + 8, :], start=True, stop=True).then_inc(s_ide, 1)

        s_ve, s_rstd, s_xn, s_xTp, s_xT = sem("variance_ready"), sem("rstd_ready"), sem("xn_ready"), sem("xT_in_psum"), sem("xT_ready")

        def norm_stats(dve, at, rows):
            for s, x in enumerate(rows):
                nc.vector.bn_stats(stats[:, at + s, :], x).then_inc(s_chain, 1)
            for s in range(len(rows)):
                dve.wait_ge(s_chain, 1)
                dve.sem_inc(s_chain, -1)
                nc.vector.bn_aggr(mv[:, at + s, :], stats[:, at + s, :]).then_inc(s_chain, 1)
            dve.wait_ge(s_chain, len(rows))
            dve.sem_inc(s_chain, -len(rows))
            v = mv[:, at:at + len(rows), 1]
            nc.vector.tensor_scalar(v, v, LN_EPS, None, ALU.add).then_inc(s_ve, 1)

        def norm_power(pool, at, n):
            pool.wait_ge(s_ve, 1)
            pool.sem_inc(s_ve, -1)
            nc.gpsimd.tensor_tensor(rstd[:, at:at + n], mv[:, at:at + n, 1], cst[:, 0:1].to_broadcast([P, n]), ALU.pow).then_inc(s_rstd, 1)

        def norm_rows(dve, at, rows, dsts):
            dve.wait_ge(s_rstd, 1)
            dve.sem_inc(s_rstd, -1)
            for s, (x, dst) in enumerate(zip(rows, dsts)):
                nc.vector.tensor_scalar(dst, x, mv[:, at + s, 0:1], rstd[:, at + s:at + s + 1], ALU.subtract, ALU.mult).then_inc(s_xn, 1)

        def tile_of(t):
            return h[:, bass.ds(t, 1), :].rearrange("p a c -> p (a c)")

        with ExitStack() as ph:
            qk = sb("qk", [P, 4, 2, P], f32, ph)
            va = sb("va", [P, B, H, DH + 1], f32, ph)
            sh = sb("sh", [P, HG, 2, 2, P], f32, ph)
            pr = sb("pr", [P, HG, 2, 2, P], f32, ph)
            prT = sb("prT", [P, 4, HG, P], f32, ph)
            mx = sb("mx", [P, HG * 4], f32, ph)
            rd = sb("rd", [P, 2, H], f32, ph)
            ao = sb("ao", [P, 2, DH, H], f32, ph)
            scores = acc[:, 0:4, :].rearrange("p r (x m) -> p r x m", m=P)
            BT, BU0, BU1 = (4, 5), 6, 7
            s_qk, s_qkc, s_vp, s_vc, s_sc, s_sub, s_ex, s_tp, s_tc, s_o, s_free = (sem(n) for n in (
                "qk_in_psum", "qk_ready", "v_in_psum", "v_ready", "scores_ready", "shifted_ready", "exp_ready",
                "probsT_in_psum", "probsT_ready", "attn_ready", "outputs_out_of_psum"))

            with nc.Block() as block:
                @block.vector
                def _(dve):
                    def rows(i):
                        return [tile_of(i), tile_of(i + PAIRS)]

                    def normalize(i):
                        norm_stats(dve, 0, rows(i))
                        norm_rows(dve, 0, rows(i), [xn[:, 0, :], xn[:, 1, :]])

                    def keep_values(i):
                        dve.wait_ge(s_vp, 1)
                        dve.sem_inc(s_vp, -1)
                        for s in range(2):
                            m = nc.vector.tensor_copy(va[:, bass.ds(i + s * PAIRS, 1), :, 0:DH].rearrange("p a h e -> p (a h) e"),
                                                      bank[BU1][:, 256 + s * P:256 + (s + 1) * P].rearrange("p (h d) -> p h d", h=H))
                            m.then_inc(s_vc if s else s_chain, 1)
                        dve.wait_ge(s_chain, 1)
                        dve.sem_inc(s_chain, -1)

                    def shifted(i):
                        dve.wait_ge(s_sc, 1)
                        dve.sem_inc(s_sc, -1)
                        link(dve, s_chain, nc.vector.tensor_reduce(mx[:, :].rearrange("p (r x) -> p r x", r=HG), scores, AX.X, ALU.max))
                        nc.vector.tensor_tensor(sh[:, :, :, :, :].rearrange("p r s g m -> p r (s g) m"), scores,
                                                mx[:, :].rearrange("p (r x) -> p r x", r=HG).unsqueeze(3).to_broadcast([P, HG, 4, P]),
                                                ALU.subtract).then_inc(s_sub, 1)

                    def finish(i):
                        dve.wait_ge(s_o, 1)
                        dve.sem_inc(s_o, -1)
                        o = bank[BU1][:, 0:272].rearrange("p (s h e) -> p s h e", s=2, h=H)
                        link(dve, s_chain, nc.vector.reciprocal(rd[:, :, :], o[:, :, :, DH]))
                        for s in range(2):
                            nc.vector.tensor_tensor(ao[:, s, :, :].rearrange("p d h -> p h d"), o[:, s, :, 0:DH],
                                                    rd[:, s, :].unsqueeze(2).to_broadcast([P, H, DH]), ALU.mult).then_inc(s_chain, 1)
                        dve.wait_ge(s_chain, 2)
                        dve.sem_inc(s_chain, -2)
                        dve.sem_inc(s_free, 1)
                        for s in range(2):
                            hr = tile_of(i + s * PAIRS)
                            nc.vector.tensor_tensor(hr, hr, ao[:, s, :, :].rearrange("p d h -> p (d h)"), ALU.add).then_inc(s_chain, 1)
                        dve.wait_ge(s_chain, 2)
                        dve.sem_inc(s_chain, -2)

                    def step(i, after=True, later=True, before=True):
                        shifted(i)
                        if after:
                            keep_values(i + 1)
                        if before:
                            finish(i - 1)
                        if later:
                            normalize(i + 2)

                    link(dve, s_chain, nc.vector.memset(va[:, :, :, DH:DH + 1], 1.0))
                    dve.sem_inc(s_free, 1)
                    normalize(0)
                    keep_values(0)
                    normalize(1)
                    step(0, before=False)
                    with dve.Fori(1, PAIRS - 2) as i:
                        step(i)
                    step(PAIRS - 2, later=False)
                    step(PAIRS - 1, after=False, later=False)
                    finish(PAIRS - 1)

                @block.gpsimd
                def _(pool):
                    with pool.Fori(0, PAIRS) as i:
                        norm_power(pool, 0, 2)

                @block.scalar
                def _(act):
                    def copy_xT():
                        act.wait_ge(s_xTp, 1)
                        act.sem_inc(s_xTp, -1)
                        nc.scalar.activation(xT[:, 0:2, :], bank[BU1][:, 0:256].rearrange("p (s t) -> p s t", s=2), ACT.Copy).then_inc(s_xT, 1)

                    def copy_qk(n):
                        act.wait_ge(s_qk, 1)
                        act.sem_inc(s_qk, -1)
                        nc.scalar.activation(qk[:, 2 * n:2 * n + 2, :, :], bank[BU0][:, :].rearrange("p (g s t) -> p g s t", g=2, s=2), ACT.Copy).then_inc(s_qkc, 1)

                    def copy_probs(u):
                        act.wait_ge(s_tp, 1)
                        act.sem_inc(s_tp, -1)
                        nc.scalar.activation(prT[:, u, :, :], bank[BT[u % 2]][:, :].rearrange("p (h t) -> p h t", h=4), ACT.Copy).then_inc(s_tc, 1)

                    def step(after=True, before=True):
                        if after:
                            copy_xT()
                        if before:
                            copy_probs(0)
                        if after:
                            copy_qk(0)
                        if before:
                            copy_probs(1)
                        if after:
                            copy_qk(1)
                        if before:
                            copy_probs(2)
                            copy_probs(3)
                        act.wait_ge(s_sub, 1)
                        act.sem_inc(s_sub, -1)
                        nc.scalar.activation(pr[:, :, :, :, :], sh[:, :, :, :, :], ACT.Exp, scale=float(C) ** -0.5).then_inc(s_ex, 1)

                    copy_xT()
                    copy_qk(0)
                    copy_qk(1)
                    step(before=False)
                    with act.Fori(1, PAIRS - 1) as i:
                        step()
                    step(after=False)
                    for u in range(4):
                        copy_probs(u)

                @block.tensor
                def _(pe):
                    def flip_rows():
                        for s in range(2):
                            pe.wait_ge(s_xn, 1)
                            pe.sem_inc(s_xn, -1)
                            m = nc.tensor.transpose(bank[BU1][:, s * P:(s + 1) * P], xn[:, s, :], ident[:, :])
                        m.then_inc(s_xTp, 1)

                    def project(w):
                        for g in range(2):
                            m = nc.tensor.matmul(bank[BU0][:, g * 256:(g + 1) * 256], w[:, g, :, :], xT[:, 0:2, :], start=True, stop=True)
                        m.then_inc(s_qk, 1)

                    def project_qv():
                        pe.wait_ge(s_xT, 1)
                        pe.sem_inc(s_xT, -1)
                        project(w_q)
                        for s in range(2):
                            m = nc.tensor.matmul(bank[BU1][:, 256 + s * P:256 + (s + 1) * P], xT[:, s, :], w_v[:, :], start=True, stop=True)
                        m.then_inc(s_vp, 1)

                    def project_k():
                        pe.wait_ge(s_qkc, 1)
                        pe.sem_inc(s_qkc, -1)
                        project(w_k)

                    def score():
                        pe.wait_ge(s_qkc, 1)
                        pe.sem_inc(s_qkc, -1)
                        for s in range(2):
                            for g in range(2):
                                for r in range(HG):
                                    m = nc.tensor.matmul(scores[:, r, 2 * s + g, :], qk[32 * r:32 * r + 32, g, s, :],
                                                         qk[32 * r:32 * r + 32, 2 + g, 1 - s, :], start=True, stop=True)
                        m.then_inc(s_sc, 1)

                    def flip(u):
                        s, half = u // 2, u % 2
                        for x in range(4):
                            r, g = 2 * half + x // 2, x % 2
                            m = nc.tensor.transpose(bank[BT[u % 2]][:, x * P:(x + 1) * P], pr[:, r, s, g, :], ident[:, :])
                        m.then_inc(s_tp, 1)

                    def weigh(i, s):
                        for u in (2 * s, 2 * s + 1):
                            for x in range(4):
                                r, g = 2 * (u % 2) + x // 2, x % 2
                                hd = g * HG + r
                                v_of = va[:, bass.ds(i + (1 - s) * PAIRS, 1), hd, :].rearrange("p a e -> p (a e)")
                                m = nc.tensor.matmul(bank[BU1][:, s * 136 + hd * 17:s * 136 + hd * 17 + 17], prT[:, u, x, :], v_of, start=True, stop=True)
                        return m

                    def attend(i):
                        pe.wait_ge(s_tc, 1)
                        pe.sem_inc(s_tc, -1)
                        flip(2)
                        pe.wait_ge(s_tc, 1)
                        pe.sem_inc(s_tc, -1)
                        flip(3)
                        pe.wait_ge(s_free, 1)
                        pe.sem_inc(s_free, -1)
                        weigh(i, 0)
                        pe.wait_ge(s_tc, 2)
                        pe.sem_inc(s_tc, -2)
                        weigh(i, 1).then_inc(s_o, 1)

                    def step(i, after=True, before=True):
                        if before:
                            pe.wait_ge(s_ex, 1)
                            pe.sem_inc(s_ex, -1)
                        score()
                        if after:
                            flip_rows()
                        if before:
                            flip(0)
                        if after:
                            project_qv()
                        if before:
                            flip(1)
                        if after:
                            project_k()
                            pe.wait_ge(s_vc, 1)
                            pe.sem_inc(s_vc, -1)
                        if before:
                            attend(i - 1)

                    flip_rows()
                    project_qv()
                    project_k()
                    pe.wait_ge(s_vc, 1)
                    pe.sem_inc(s_vc, -1)
                    step(0, before=False)
                    with pe.Fori(1, PAIRS - 1) as i:
                        step(i)
                    step(PAIRS - 1, after=False)
                    pe.wait_ge(s_ex, 1)
                    pe.sem_inc(s_ex, -1)
                    flip(0)
                    flip(1)
                    attend(PAIRS - 1)

        with ExitStack() as ph:
            G = 4
            act0 = sb("act0", [P, 2, G, N_IN], f32, ph)
            act1 = sb("act1", [P, 2, G, N_OUT], f32, ph)
            signs = sb("signs", [P, G, N_IN], bf16, ph)
            act2 = sb("act2", [P, 2, G, N_PROC], f32, ph)
            ex2 = sb("ex2", [P, 2, G, N_PROC], f32, ph)
            left = sb("left", [P, 2, G, N_IN], f32, ph)
            kept = sb("kept", [P, 2, G, N_IN], f32, ph)
            keptT = sb("keptT", [P, 2, G, N_IN // P, P], f32, ph)
            aggT = sb("aggT", [D_PV, 2, G, P], f32, ph)
            ffn_out = sb("ffn_out", [P, 2, G, C], f32, ph)
            total = sb("total", [P, 4, G], f32, ph)
            above = sb("above", [P, 4, G], f32, ph)
            neg_t = sb("neg_t", [P, 4, G], f32, ph)
            thr = sb("thr", [P, 4, G], f32, ph)
            gain = sb("gain", [P, 4, G], f32, ph)
            move = sb("move", [P, 4, G], f32, ph)
            short = sb("short", [P, 4, G], f32, ph)
            base_t = sb("base_t", [P, 4, G], f32, ph)
            rest = sb("rest", [P, 4, G], f32, ph)
            far = sb("far", [P, 4, G], f32, ph)
            spare = sb("spare", [P, 4, G, WIDEST], f32, ph)
            top = sb("top", [P, 2, G, WIDEST], f32, ph)
            found = sb("found", [P, 2, G, WIDEST], f32, ph)
            least = sb("least", [P, 2, G], f32, ph)
            missed = sb("missed", [P, 2, G], f32, ph)
            missed_i = sb("missed_i", [1, 2], i32, ph)
            top8 = sb("top8", [P, G, 8], f32, ph)
            nmax = sb("nmax", [P, 2, G], f32, ph)
            psumr = sb("psumr", [P, 2, G], f32, ph)
            rden = sb("rden", [P, 2, G], f32, ph)
            s_a1p, s_a1, s_kept, s_ktp, s_kt, s_prp, s_a2, s_nm, s_ex2, s_agp, s_ag, s_a3p, s_op, s_oc = (sem(n) for n in (
                "in_acts_psum", "acts_total", "kept_ready", "keptT_psum", "keptT_ready", "proc_psum", "proc_ready", "proc_max",
                "proc_exp", "agg_psum", "agg_ready", "out_acts_psum", "ffn_psum", "ffn_out_ready"))
            s_t0, s_spare0, s_g0, s_o3 = (sem(n) for n in (
                "last_threshold_in", "spare_ready_in", "in_acts_out_of_psum", "out_acts_out_of_psum"))
            s_oc2 = sem("ffn_out_of_psum")
            s_nt, s_cnt, s_t, s_spare, s_miss, s_flag, s_ocf = (sem(n) for n in (
                "threshold_ready", "count_ready", "last_threshold", "spare_ready", "missed_ready", "missed_sum", "ffn_out_added"))
            STEPS = B // (2 * G)

            def banks(g):
                return acc[:, G * g:G * g + G, :]

            with nc.Block() as block:
                @block.vector
                def _(dve):
                    v = nc.vector

                    def rows(i, g):
                        return [tile_of(2 * G * i + G * g + s) for s in range(G)]

                    def keep(g, acts, n, src, gone):
                        for s in range(G):
                            dve.wait_ge(s_chain, 1)
                            dve.sem_inc(s_chain, -1)
                            more = {"accum_out": psumr[:, g, s:s + 1]} if n == N_PROC else {}
                            v.scalar_tensor_tensor(kept[:, g, s, 0:n], left[:, g, s, 0:n], gone, src[:, g, s, :], ALU.is_equal, ALU.mult, **more).then_inc(s_chain, 1)

                    def mark(g, at, acts, n, gone):
                        lf = left[:, g, :, 0:n]
                        for s in range(G):
                            if gone == 0.0:
                                v.scalar_tensor_tensor(lf[:, s, :], acts[:, g, s, :], thr[:, at, s:s + 1], acts[:, g, s, :], ALU.is_le, ALU.mult).then_inc(s_chain, 1)
                            else:
                                v.tensor_scalar(lf[:, s, :], acts[:, g, s, :], thr[:, at, s:s + 1], gone, ALU.is_gt, ALU.mult).then_inc(s_chain, 1)
                        if gone != 0.0:
                            dve.wait_ge(s_chain, G)
                            dve.sem_inc(s_chain, -G)
                            link(dve, s_chain, v.tensor_tensor(lf, lf, acts[:, g, :, :], ALU.add))
                        else:
                            dve.wait_ge(s_chain, G)
                            dve.sem_inc(s_chain, -G)

                    def topk(g, slot, k, acts, n, src, gone, window, meanwhile):
                        lf = left[:, g, :, 0:n]
                        for j in range(window // 8):
                            at = slice(8 * j, 8 * j + 8)
                            for s in range(G):
                                if j:
                                    dve.wait_ge(s_chain, 1)
                                    dve.sem_inc(s_chain, -1)
                                v.max(top[:, g, s, at], lf[:, s, :]).then_inc(s_chain, 1)
                            for s in range(G):
                                dve.wait_ge(s_chain, 1)
                                dve.sem_inc(s_chain, -1)
                                v.tensor_tensor(found[:, g, s, at], top[:, g, s, at], spare[:, slot, s, at], ALU.max).then_inc(s_chain, 1)
                            for s in range(G):
                                dve.wait_ge(s_chain, 1)
                                dve.sem_inc(s_chain, -1)
                                v.match_replace(lf[:, s, :], found[:, g, s, at], lf[:, s, :], gone).then_inc(s_chain, 1)
                        dve.wait_ge(s_chain, G)
                        dve.sem_inc(s_chain, -G)
                        v.tensor_tensor(missed[:, g, :], top[:, g, :, 1], thr[:, slot, :], ALU.is_ge).then_inc(s_chain, 1)
                        v.tensor_reduce(least[:, g, :], found[:, g, :, 0:window], AX.X, ALU.min).then_inc(s_chain, 1)
                        dve.wait_ge(s_chain, 2)
                        dve.sem_inc(s_chain, -2)
                        dve.sem_inc(s_chain, G)
                        keep(g, acts, n, src, gone)
                        if gone == 0.0:
                            v.scalar_tensor_tensor(missed[:, g, :], least[:, g, :], 0.0, missed[:, g, :], ALU.is_le, ALU.add).then_inc(s_chain, 1)
                            dve.wait_ge(s_chain, G + 1)
                            dve.sem_inc(s_chain, -(G + 1))
                        else:
                            dve.wait_ge(s_chain, G)
                            dve.sem_inc(s_chain, -G)
                        v.tensor_tensor(missed[:, g, :], missed[:, g, :], far[:, slot, :], ALU.add).then_inc(s_miss, 1)
                        meanwhile()
                        dve.wait_ge(s_flag, 1)
                        dve.sem_inc(s_flag, -1)
                        link(dve, s_chain, v.tensor_copy(missed_i[:, g:g + 1], banks(g)[0:1, 0, 0:1]))
                        any_missed = dve.value_load(missed_i[0:1, g:g + 1], min_val=0, max_val=2 ** 30)
                        with dve.If_ne(dve.to_reg(any_missed), 0):
                            link(dve, s_chain, v.tensor_copy(lf, acts[:, g, :, :]))
                            with dve.Fori(0, k // 8) as r:
                                for s in range(G):
                                    v.max(top8[:, s, :], lf[:, s, :]).then_inc(s_chain, 1)
                                for s in range(G):
                                    dve.wait_ge(s_chain, 1)
                                    dve.sem_inc(s_chain, -1)
                                    v.match_replace(lf[:, s, :], top8[:, s, :], lf[:, s, :], GONE).then_inc(s_chain, 1)
                                dve.wait_ge(s_chain, G)
                                dve.sem_inc(s_chain, -G)
                            dve.sem_inc(s_chain, G)
                            keep(g, acts, n, src, GONE)
                            dve.wait_ge(s_chain, G)
                            dve.sem_inc(s_chain, -G)

                    def mark_in(g):
                        dve.wait_ge(s_t0, 1)
                        dve.sem_inc(s_t0, -1)
                        mark(g, 2 + g, act0, N_IN, 0.0)

                    def keep_in(g, meanwhile):
                        dve.wait_ge(s_spare0, 1)
                        dve.sem_inc(s_spare0, -1)
                        topk(g, 2 + g, K_IN, act0, N_IN, act0, 0.0, WINDOW, meanwhile)
                        dve.sem_inc(s_kept, 1)

                    def mark_process(g):
                        dve.wait_ge(s_a2, 1)
                        dve.sem_inc(s_a2, -1)
                        link(dve, s_chain, v.tensor_reduce(nmax[:, g, :], act2[:, g, :, :], AX.X, ALU.max))
                        v.tensor_scalar(nmax[:, g, :], nmax[:, g, :], -1.0, None, ALU.mult).then_inc(s_nm, 1)
                        dve.wait_ge(s_t, 1)
                        dve.sem_inc(s_t, -1)
                        mark(g, g, act2, N_PROC, GONE)

                    def keep_process(g, meanwhile):
                        dve.wait_ge(s_spare, 1)
                        dve.sem_inc(s_spare, -1)
                        dve.wait_ge(s_ex2, 1)
                        dve.sem_inc(s_ex2, -1)
                        topk(g, g, K_PROC, act2, N_PROC, ex2, GONE, WINDOW_PROC, meanwhile)
                        v.reciprocal(rden[:, g, :], psumr[:, g, :]).then_inc(s_kept, 1)

                    def mark_out(g):
                        dve.wait_ge(s_t, 1)
                        dve.sem_inc(s_t, -1)
                        mark(g, g, act1, N_OUT, 0.0)

                    def keep_out(g, meanwhile):
                        dve.wait_ge(s_spare, 1)
                        dve.sem_inc(s_spare, -1)
                        topk(g, g, K_OUT, act1, N_OUT, act1, 0.0, WINDOW, meanwhile)
                        dve.sem_inc(s_kept, 1)

                    def next_stats(i):
                        for g in range(2):
                            norm_stats(dve, G * g, rows(i, g))

                    def next_rows(i):
                        for g in range(2):
                            norm_rows(dve, G * g, rows(i, g), [xn[:, G * g + s, :] for s in range(G)])

                    def step(i, after=True):
                        mark_in(0)
                        keep_in(0, lambda: mark_in(1))
                        keep_in(1, lambda: mark_process(0))
                        keep_process(0, lambda: next_stats(i + 1) if after else None)
                        mark_process(1)
                        keep_process(1, lambda: next_rows(i + 1) if after else None)
                        mark_out(0)
                        keep_out(0, lambda: mark_out(1))
                        keep_out(1, lambda: None)

                    next_stats(0)
                    next_rows(0)
                    with dve.Fori(0, STEPS - 1) as i:
                        step(i)
                    step(STEPS - 1, after=False)

                @block.gpsimd
                def _(pool):
                    g_ = nc.gpsimd

                    def L(ins):
                        link(pool, s_pchain, ins)

                    def find(g, k, n, window, first, ranks, s_t, s_spare):
                        aim = k - window // 2
                        dev = 1.0 / (n * HALF_MEAN)
                        pool.wait_ge(s_a1, 1)
                        pool.sem_inc(s_a1, -1)
                        L(g_.tensor_scalar(gain[:, g, :], total[:, g, :], -0.5 * dev / ranks, 0.0, ALU.mult, ALU.add))
                        L(g_.tensor_scalar(neg_t[:, g, :], total[:, g, :], -first * dev, 0.0, ALU.mult, ALU.add))
                        L(g_.tensor_scalar(neg_t[:, g, :], neg_t[:, g, :], -LEAST_T, 1.0, ALU.min, ALU.mult))
                        pool.sem_inc(s_nt, 1)
                        L(g_.tensor_scalar(short[:, g, :], gain[:, g, :], float(n - 2 * aim), 0.0, ALU.mult, ALU.add))
                        for c in range(COUNTS - 1):
                            L(g_.tensor_tensor(base_t[:, g, :], neg_t[:, g, :], short[:, g, :], ALU.add))
                            pool.wait_ge(s_cnt, 1)
                            pool.sem_inc(s_cnt, -1)
                            L(g_.tensor_tensor(move[:, g, :], above[:, g, :], gain[:, g, :], ALU.mult))
                            if c < COUNTS - 2 and first > 0.0:
                                L(g_.tensor_tensor(neg_t[:, g, :], base_t[:, g, :], move[:, g, :], ALU.add))
                                pool.sem_inc(s_nt, 1)
                            else:
                                L(g_.tensor_tensor(neg_t[:, g, :], base_t[:, g, :], move[:, g, :], ALU.add))
                                L(g_.tensor_scalar(neg_t[:, g, :], neg_t[:, g, :], -LEAST_T, 1.0, ALU.min, ALU.mult))
                                pool.sem_inc(s_nt, 1)
                        g_.tensor_scalar(thr[:, g, :], neg_t[:, g, :], -1.0, 0.0, ALU.mult, ALU.add).then_inc(s_t, 1)
                        pool.wait_ge(s_cnt, 1)
                        pool.sem_inc(s_cnt, -1)
                        L(g_.tensor_scalar(rest[:, g, :], above[:, g, :], -0.5, k - n / 2.0, ALU.mult, ALU.add))
                        L(g_.tensor_tensor(spare[:, g, :, 0:window], rank_no[:, 0:window].unsqueeze(1).to_broadcast([P, G, window]),
                                           rest[:, g, :].unsqueeze(2).to_broadcast([P, G, window]), ALU.subtract))
                        L(g_.tensor_scalar(spare[:, g, :, 0:window], spare[:, g, :, 0:window], 0.25, BIG, ALU.add, ALU.mult))
                        L(g_.tensor_scalar(move[:, g, :], rest[:, g, :], -window / 2.0, 1.0, ALU.add, ALU.mult))
                        L(g_.tensor_tensor(move[:, g, :], move[:, g, :], move[:, g, :], ALU.mult))
                        g_.tensor_scalar(far[:, g, :], move[:, g, :], -window ** 2 / 4.0, 0.0, ALU.add, ALU.max).then_inc(s_spare, 1)

                    def find_in(g):
                        find(2 + g, K_IN, N_IN, WINDOW, FIRST_IN, RANKS_IN, s_t0, s_spare0)

                    def step(i, after=True):
                        for g in range(2):
                            find(g, K_PROC, N_PROC, WINDOW_PROC, 0.0, RANKS_PROC, s_t, s_spare)
                        if after:
                            for g in range(2):
                                norm_power(pool, G * g, G)
                        for g in range(2):
                            find(g, K_OUT, N_OUT, WINDOW, FIRST_OUT, RANKS_OUT, s_t, s_spare)
                        for g in range(2):
                            if after:
                                find_in(g)
                            pool.wait_ge(s_oc, 1)
                            pool.sem_inc(s_oc, -1)
                            pool.sem_inc(s_oc2, 1)
                            hr = h[:, bass.ds(2 * G * i + G * g, G), :]
                            L(g_.tensor_tensor(hr, hr, ffn_out[:, g, :, :], ALU.add))
                            pool.sem_inc(s_ocf, 1)

                    pool.sem_inc(s_ocf, 2)
                    pool.sem_inc(s_oc2, 2)
                    for g in range(2):
                        norm_power(pool, G * g, G)
                    for g in range(2):
                        find_in(g)
                    with pool.Fori(0, STEPS - 1) as i:
                        step(i)
                    step(STEPS - 1, after=False)

                @block.scalar
                def _(act):
                    def count(at, acts, n, between=lambda c: None):
                        for c in range(COUNTS):
                            act.wait_ge(s_nt, 1)
                            act.sem_inc(s_nt, -1)
                            for s in range(G):
                                m = nc.scalar.activation(signs[:, s, 0:n], acts[:, s, :], ACT.Sign, bias=neg_t[:, at, s:s + 1], accum_out=above[:, at, s:s + 1])
                            m.then_inc(s_cnt, 1)
                            between(c)

                    def copy_xT():
                        for g in range(2):
                            act.wait_ge(s_xTp, 1)
                            act.sem_inc(s_xTp, -1)
                            nc.scalar.activation(xT[:, G * g:G * g + G, :], banks(g)[:, :, 0:P], ACT.Copy).then_inc(s_xT, 1)

                    def in_acts():
                        for g in range(2):
                            for s in range(G):
                                act.wait_ge(s_a1p, 1)
                                act.sem_inc(s_a1p, -1)
                                m = nc.scalar.activation(act0[:, g, s, :], banks(g)[:, s, :], ACT.Gelu, accum_out=total[:, 2 + g, s:s + 1])
                            m.then_inc(s_achain, 1)
                            act.wait_ge(s_achain, 1)
                            act.sem_inc(s_achain, -1)
                            act.sem_inc(s_a1, 1)
                            act.sem_inc(s_g0, 1)

                    def copy_flipped(g, n, tiles=range(G)):
                        for s in tiles:
                            act.wait_ge(s_ktp, 1)
                            act.sem_inc(s_ktp, -1)
                            nc.scalar.activation(keptT[:, g, s, 0:n, :], banks(g)[:, s, 0:n * P].rearrange("p (c t) -> p c t", c=n), ACT.Copy).then_inc(s_kt, 1)

                    def step(after=True):
                        for g in range(2):
                            copy_flipped(g, 4)
                            for s in range(G):
                                act.wait_ge(s_prp, 1)
                                act.sem_inc(s_prp, -1)
                                m = nc.scalar.activation(act2[:, g, s, :], banks(g)[:, s, 0:N_PROC], ACT.Gelu, accum_out=total[:, g, s:s + 1])
                            m.then_inc(s_a1, 1)
                            count(g, act2[:, g, :, :], N_PROC)
                            act.sem_inc(s_a2, 1)
                            act.wait_ge(s_nm, 1)
                            act.sem_inc(s_nm, -1)
                            for s in range(G):
                                m = nc.scalar.activation(ex2[:, g, s, :], act2[:, g, s, :], ACT.Exp, bias=nmax[:, g, s:s + 1])
                            m.then_inc(s_ex2, 1)
                        for g in range(2):
                            copy_flipped(g, 2)
                            for s in range(G):
                                act.wait_ge(s_agp, 1)
                                act.sem_inc(s_agp, -1)
                                nc.scalar.activation(aggT[:, g, s, :], banks(g)[0:D_PV, s, 0:P], ACT.Copy).then_inc(s_ag, 1)
                            for s in range(G):
                                act.wait_ge(s_a3p, 1)
                                act.sem_inc(s_a3p, -1)
                                m = nc.scalar.activation(act1[:, g, s, :], banks(g)[:, s, :], ACT.Gelu, scale=rden[:, g, s:s + 1], accum_out=total[:, g, s:s + 1])
                            m.then_inc(s_achain, 1)
                            act.wait_ge(s_achain, 1)
                            act.sem_inc(s_achain, -1)
                            act.sem_inc(s_a1, 1)
                            act.sem_inc(s_o3, 1)
                            if after and g == 1:
                                copy_xT()
                            count(g, act1[:, g, :, :], N_OUT)
                        if after:
                            in_acts()
                        for g in range(2):
                            if after:
                                count(2 + g, act0[:, g, :, :], N_IN, lambda c: copy_flipped(g, 4, range(2 * c, 2 * c + 2)) if c < 2 else None)
                            else:
                                copy_flipped(g, 4)
                            act.wait_ge(s_op, 1)
                            act.sem_inc(s_op, -1)
                            act.wait_ge(s_ocf, 1)
                            act.sem_inc(s_ocf, -1)
                            nc.scalar.activation(ffn_out[:, g, :, :], banks(g)[:, :, 0:P], ACT.Copy).then_inc(s_oc, 1)

                    copy_xT()
                    in_acts()
                    for g in range(2):
                        count(2 + g, act0[:, g, :, :], N_IN)
                    with act.Fori(0, STEPS - 1) as i:
                        step()
                    step(after=False)

                @block.tensor
                def _(pe):
                    def in_acts(first=False):
                        for g in range(2):
                            if not first:
                                pe.wait_ge(s_o3, 1)
                                pe.sem_inc(s_o3, -1)
                            pe.wait_ge(s_xn, G)
                            pe.sem_inc(s_xn, -G)
                            for s in range(G):
                                m = nc.tensor.transpose(banks(g)[:, s, 0:P], xn[:, G * g + s, :], ident[:, :])
                            m.then_inc(s_xTp, 1)
                        for g in range(2):
                            pe.wait_ge(s_xT, 1)
                            pe.sem_inc(s_xT, -1)
                            for s in range(G):
                                nc.tensor.matmul(banks(g)[:, s, :], xT[:, G * g + s, :], in_pat[:, :], start=True, stop=True).then_inc(s_a1p, 1)

                    def flip(g, n):
                        pe.wait_ge(s_miss, 1)
                        pe.sem_inc(s_miss, -1)
                        for s in range(G):
                            m = nc.tensor.matmul(banks(g)[0:1, 0, 0:1], ones[:, 0:1], missed[:, g, s:s + 1], start=(s == 0), stop=(s == G - 1))
                        m.then_inc(s_flag, 1)
                        pe.wait_ge(s_kept, 1)
                        pe.sem_inc(s_kept, -1)
                        for s in range(G):
                            for c in range(n):
                                m = nc.tensor.transpose(banks(g)[:, s, c * P:(c + 1) * P], kept[:, g, s, c * P:(c + 1) * P], ident[:, :])
                            m.then_inc(s_ktp, 1)

                    def step(after=True):
                        for g in range(2):
                            pe.wait_ge(s_oc2, 1)
                            pe.sem_inc(s_oc2, -1)
                            flip(g, 4)
                            for s in range(G):
                                pe.wait_ge(s_kt, 1)
                                pe.sem_inc(s_kt, -1)
                                for c in range(4):
                                    m = nc.tensor.matmul(banks(g)[:, s, 0:N_PROC], keptT[:, g, s, c, :], proc_w[:, c, :], start=(c == 0), stop=(c == 3))
                                m.then_inc(s_prp, 1)
                        for g in range(2):
                            flip(g, 2)
                            for s in range(G):
                                pe.wait_ge(s_kt, 1)
                                pe.sem_inc(s_kt, -1)
                                for c in range(2):
                                    m = nc.tensor.matmul(banks(g)[0:D_PV, s, 0:P], proc_v[:, c, :], keptT[:, g, s, c, :], start=(c == 0), stop=(c == 1))
                                m.then_inc(s_agp, 1)
                            for s in range(G):
                                pe.wait_ge(s_ag, 1)
                                pe.sem_inc(s_ag, -1)
                                nc.tensor.matmul(banks(g)[:, s, :], aggT[:, g, s, :], out_w[:, :], start=True, stop=True).then_inc(s_a3p, 1)
                        if after:
                            in_acts()
                        else:
                            pe.wait_ge(s_o3, 2)
                            pe.sem_inc(s_o3, -2)
                        for g in range(2):
                            if after:
                                pe.wait_ge(s_g0, 1)
                                pe.sem_inc(s_g0, -1)
                            flip(g, 4)
                            for s in range(G):
                                pe.wait_ge(s_kt, 1)
                                pe.sem_inc(s_kt, -1)
                                for c in range(4):
                                    m = nc.tensor.matmul(banks(g)[:, s, 0:P], keptT[:, g, s, c, :], out_pat[:, c, :], start=(c == 0), stop=(c == 3))
                            m.then_inc(s_op, 1)

                    in_acts(first=True)
                    pe.wait_ge(s_g0, 2)
                    pe.sem_inc(s_g0, -2)
                    with pe.Fori(0, STEPS - 1) as i:
                        step()
                    step(after=False)

        tok_id = sb("tok_id", [P, B])
        top_p = sb("top_p", [P, TOPK, B])
        gates = sb("gates", [P, B, E])
        filled = sb("filled", [P, E])
        w2_all = sb("w2_all", [P, E, NC1, C])
        xr = sb("xr", [P, 2, 4, XW])
        posi = sb("posi", [P, 2, TOPK, 4], i32)
        s_xs = [sem("rows_scattered_a"), sem("rows_scattered_b")]
        s_xf = sem("rows_buffer_free")
        s_pos = sem("positions_ready")

        def scatter_rows(pool, g):
            pool.wait_ge(s_pos, 1)
            pool.sem_inc(s_pos, -1)
            for s in range(4):
                for k in range(TOPK):
                    nc.gpsimd.indirect_dma_start(xs_dram[:, :], bass.IndirectOffsetOnAxis(posi[:, g, k, s:s + 1], 0), xr[:, g, s, :], None).then_inc(s_xs[g], 16)

        s_w2, s_ids = sem("w2_loaded"), sem("token_numbers_loaded")

        with ExitStack() as ph:
            G, ORDER = 4, (1, 0)
            wedge = sb("wedge", [P, C], f32, ph)
            gram = sb("gram", [P, C], f32, ph)
            wedgeT = sb("wedgeT", [P, C], f32, ph)
            gate = sb("gate", [P, 2, G, C], f32, ph)
            kv = sb("kv", [P, 2, G, 2, C], f32, ph)
            gq = sb("gq", [P, 2, G, C], f32, ph)
            st2 = sb("st2", [P, 2, 2, G, 6], f32, ph)
            mv2 = sb("mv2", [P, 2, 2, G, 2], f32, ph)
            shift = sb("shift", [P, 2, G], f32, ph)
            spread = sb("spread", [P, 2, 2, G], f32, ph)
            unit = sb("unit", [P, 2, G], f32, ph)
            qkn = sb("qkn", [P, G, 2, 2, 64], f32, ph)
            tc = sb("tc", [P, G, 2, 2, 64], f32, ph)
            ts_ = sb("ts_", [P, G, 2, 2, 64], f32, ph)
            rot = sb("rot", [P, 2, G, 2, C], f32, ph)
            rotT = sb("rotT", [P, 2, G, 2, C], f32, ph)
            zT = sb("zT", [P, 2, G, C], f32, ph)
            sm = sb("sm", [P, 2, G, P], f32, ph)
            mx1 = sb("mx1", [P, 2, G], f32, ph)
            nmx1 = sb("nmx1", [P, 2, G], f32, ph)
            rsum = sb("rsum", [P, 2, G], f32, ph)
            esink = sb("esink", [P, 2, G], f32, ph)
            den = sb("den", [P, 2, G], f32, ph)
            rden1 = sb("rden1", [P, 2, G], f32, ph)
            pT = sb("pT", [P, 2, G, P], f32, ph)
            o1 = sb("o1", [P, 2, G, C], f32, ph)
            lg = sb("lg", [P, 2, G, E], f32, ph)
            pe_ = sb("pe_", [P, 2, G, E], f32, ph)
            wk = sb("wk", [P, 2, G, E], f32, ph)
            pm = sb("pm", [P, 2, G, E], f32, ph)
            red = sb("red", [P, 2, G], f32, ph)
            hot2 = sb("hot2", [P, 2, TOPK, G, E], f32, ph)
            both = sb("both", [P, 2, G, E], bf16, ph)
            tri_h = sb("tri_h", [P, P], bf16, ph)
            ones_h = sb("ones_h", [P, P], bf16, ph)
            place = sb("place", [P, 2, G, E], f32, ph)
            hp = sb("hp", [P, 2, TOPK, G, E], f32, ph)
            posf = sb("posf", [P, 2, TOPK, G], f32, ph)
            s_pj, s_gb, s_kvc, s_ge, s_gq, s_qc, s_mv, s_un, s_rot, s_rtp, s_rt, s_zp, s_z, s_s, s_mx, s_p, s_pr1, s_pp, s_pt, s_o1 = (sem(n) for n in (
                "proj_psum", "gate_logits", "kv_ready", "gate_tanh", "gated_q", "state_psum", "moments", "unit_scale", "rotated",
                "rotT_psum", "rotT_ready", "z_psum", "z_ready", "l1_scores", "l1_max", "l1_row_sums", "l1_probs", "l1_probsT_psum", "l1_probsT", "l1_out_psum"))
            s_wd, s_wdt, s_wdc, s_gr = sem("wedge_ready"), sem("wedgeT_psum"), sem("wedgeT_ready"), sem("gram_psum")
            s_lgp, s_lg, s_le, s_both, s_rank = (sem(n) for n in (
                "router_logits", "logits_shifted", "router_exp", "choice_ready", "ranks_psum"))
            s_lr, s_rr = sem("logits_read"), sem("ranks_read")
            STEPS1 = B // (2 * G)

            def banks(g):
                return acc[:, G * g:G * g + G, :]

            with nc.Block() as block:
                @block.sync
                def _(sp):
                    sp.dma_start(tok_id[:, :], a["tok_id"]).then_inc(s_ids, 16)
                    sp.dma_start(w2_all[:, :, :, :], a["w2"]).then_inc(s_w2, 16)

                @block.vector
                def _(dve):
                    v = nc.vector

                    def L(ins):
                        link(dve, s_chain, ins)

                    L(v.tensor_tensor(wedge[:, :], a_m[:, :], a_t[:, :], ALU.subtract))
                    v.tensor_tensor(wedge[:, :], wedge[:, :], ident[:, :], ALU.add).then_inc(s_wd, 1)
                    dve.wait_ge(s_wdt, 1)
                    dve.sem_inc(s_wdt, -1)
                    v.tensor_copy(wedgeT[:, :], bank[6][:, 0:P]).then_inc(s_wdc, 1)
                    dve.wait_ge(s_gr, 1)
                    dve.sem_inc(s_gr, -1)
                    v.tensor_copy(gram[:, :], bank[6][:, P:2 * P]).then_inc(s_wdc, 1)
                    L(v.tensor_copy(filled[:, :], region[:, :]))
                    L(v.tensor_copy(tri_h[:, :], tri[:, :]))
                    L(v.tensor_copy(ones_h[:, :], ones[:, :]))
                    L(v.memset(xr[:, :, :, :], 0.0))
                    dve.wait_ge(s_ids, 16)
                    def rows(i, g):
                        return [tile_of(2 * G * i + G * g + s) for s in range(G)]

                    def next_rows(i):
                        for g in ORDER:
                            norm_rows(dve, G * g, rows(i, g), [xn[:, G * g + s, :] for s in range(G)])

                    def next_stats(i):
                        for g in ORDER:
                            norm_stats(dve, G * g, rows(i, g))

                    def step(i, after=True):
                        for g in ORDER:
                            dve.wait_ge(s_pj, 1)
                            dve.sem_inc(s_pj, -1)
                            v.tensor_tensor(gate[:, g, :, :], banks(g)[:, :, 3 * C:4 * C], bg_rows[:, :].unsqueeze(1).to_broadcast([P, G, C]), ALU.add).then_inc(s_gb, 1)
                        for g in ORDER:
                            dve.wait_ge(s_ge, 1)
                            dve.sem_inc(s_ge, -1)
                            v.scalar_tensor_tensor(gq[:, g, :, :], gate[:, g, :, :], 1.0, banks(g)[:, :, 0:C], ALU.add, ALU.mult).then_inc(s_gq, 1)
                        for g in ORDER:
                            for s in range(G):
                                v.bn_stats(st2[:, g, 1, s, :], kv[:, g, s, 0, :]).then_inc(s_chain, 1)
                            dve.wait_ge(s_qc, 1)
                            dve.sem_inc(s_qc, -1)
                            for s in range(G):
                                v.bn_stats(st2[:, g, 0, s, :], banks(g)[:, s, 0:C]).then_inc(s_chain, 1)
                            for x in (1, 0):
                                for s in range(G):
                                    dve.wait_ge(s_chain, 1)
                                    dve.sem_inc(s_chain, -1)
                                    v.bn_aggr(mv2[:, g, x, s, :], st2[:, g, x, s, :]).then_inc(s_mv, 1)
                        for g in ORDER:
                            dve.wait_ge(s_un, 1)
                            dve.sem_inc(s_un, -1)
                            for s in range(G):
                                v.tensor_scalar(qkn[:, s, 0, :, :].rearrange("p a b -> p (a b)"), banks(g)[:, s, 0:C],
                                                shift[:, g, s:s + 1], unit[:, g, s:s + 1], ALU.subtract, ALU.mult).then_inc(s_chain, 1)
                                v.tensor_scalar(qkn[:, s, 1, :, :].rearrange("p a b -> p (a b)"), kv[:, g, s, 0, :],
                                                shift[:, g, s:s + 1], unit[:, g, s:s + 1], ALU.subtract, ALU.mult).then_inc(s_chain, 1)
                            dve.wait_ge(s_chain, 2 * G)
                            dve.sem_inc(s_chain, -2 * G)
                            v4 = qkn[:, :, :, :, :].rearrange("p s q x j -> p (s q x) j")
                            v.tensor_tensor(tc[:, :, :, :, :].rearrange("p s q x j -> p (s q x) j"), v4,
                                            cos_t[:, :].unsqueeze(1).to_broadcast([P, 4 * G, 64]), ALU.mult).then_inc(s_chain, 1)
                            L(v.tensor_tensor(ts_[:, :, :, :, :].rearrange("p s q x j -> p (s q x) j"), v4,
                                              sin_t[:, :].unsqueeze(1).to_broadcast([P, 4 * G, 64]), ALU.mult))
                            dve.wait_ge(s_chain, 1)
                            dve.sem_inc(s_chain, -1)
                            r4 = rot[:, g, :, :, :].rearrange("p s q c -> p (s q) c")
                            c4 = tc[:, :, :, :, :].rearrange("p s q x j -> p (s q) x j")
                            n4 = ts_[:, :, :, :, :].rearrange("p s q x j -> p (s q) x j")
                            v.tensor_tensor(r4[:, :, 0:64], c4[:, :, 0, :], n4[:, :, 1, :], ALU.subtract).then_inc(s_chain, 1)
                            v.tensor_tensor(r4[:, :, 64:128], n4[:, :, 0, :], c4[:, :, 1, :], ALU.add).then_inc(s_rot, 1)
                            dve.wait_ge(s_chain, 1)
                            dve.sem_inc(s_chain, -1)
                        for g in ORDER:
                            dve.wait_ge(s_s, 1)
                            dve.sem_inc(s_s, -1)
                            v.tensor_tensor(sm[:, g, :, :], banks(g)[:, :, P:2 * P], causal[:, :].unsqueeze(1).to_broadcast([P, G, P]), ALU.add).then_inc(s_chain, 1)
                        for g in ORDER:
                            dve.wait_ge(s_chain, 1)
                            dve.sem_inc(s_chain, -1)
                            v.tensor_reduce(mx1[:, g, :], sm[:, g, :, :], AX.X, ALU.max).then_inc(s_chain, 1)
                        for g in ORDER:
                            dve.wait_ge(s_chain, 1)
                            dve.sem_inc(s_chain, -1)
                            v.tensor_scalar(nmx1[:, g, :], mx1[:, g, :], sink_c[:, :], -1.0, ALU.max, ALU.mult).then_inc(s_mx, 1)
                        for g in ORDER:
                            dve.wait_ge(s_p, 1)
                            dve.sem_inc(s_p, -1)
                            v.tensor_tensor(den[:, g, :], rsum[:, g, :], esink[:, g, :], ALU.add).then_inc(s_chain, 1)
                        for g in ORDER:
                            dve.wait_ge(s_chain, 1)
                            dve.sem_inc(s_chain, -1)
                            v.reciprocal(rden1[:, g, :], den[:, g, :]).then_inc(s_chain, 1)
                        dve.wait_ge(s_chain, 2)
                        dve.sem_inc(s_chain, -2)
                        for g in ORDER:
                            dve.wait_ge(s_o1, 1)
                            dve.sem_inc(s_o1, -1)
                            for s in range(G):
                                v.scalar_tensor_tensor(o1[:, g, s, :], vnull_rows[:, :], esink[:, g, s:s + 1], banks(g)[:, s, 3 * P:4 * P], ALU.mult, ALU.add).then_inc(s_chain, 1)
                            for s in range(G):
                                dve.wait_ge(s_chain, 1)
                                dve.sem_inc(s_chain, -1)
                                hr = rows(i, g)[s]
                                v.scalar_tensor_tensor(hr, o1[:, g, s, :], rden1[:, g, s:s + 1], hr, ALU.mult, ALU.add).then_inc(s_chain, 1)
                            dve.wait_ge(s_chain, G)
                            dve.sem_inc(s_chain, -G)
                            norm_stats(dve, NSLOT + G * g, rows(i, g))
                        if after:
                            next_stats(i + 1)
                        for g in ORDER:
                            dve.wait_ge(s_xf, 1)
                            dve.sem_inc(s_xf, -1)
                            norm_rows(dve, NSLOT + G * g, rows(i, g), [xr[:, g, s, 0:C] for s in range(G)])
                            L(v.tensor_copy(xr[:, g, :, C], tok_id[:, bass.ds(2 * G * i + G * g, G)]))
                        for g in ORDER:
                            dve.wait_ge(s_lgp, 1)
                            dve.sem_inc(s_lgp, -1)
                            v.tensor_tensor(lg[:, g, :, :], banks(g)[:, :, P:P + E], rb_rows[:, :].unsqueeze(1).to_broadcast([P, G, E]), ALU.add).then_inc(s_chain, 1)
                        dve.wait_ge(s_chain, 2)
                        dve.sem_inc(s_chain, -2)
                        dve.sem_inc(s_lr, 1)

                        def flat(x):
                            return x[:, :, :, :].rearrange("p g s e -> p (g s) e")

                        def over(x):
                            return x.rearrange("p g s -> p (g s)").unsqueeze(2).to_broadcast([P, 2 * G, E])

                        e_b = eid[:, :].unsqueeze(1).to_broadcast([P, 2 * G, E])
                        redf = red[:, :, :].rearrange("p g s -> p (g s)")
                        L(v.tensor_reduce(redf, flat(lg), AX.X, ALU.max))
                        v.tensor_tensor(flat(lg), flat(lg), over(red[:, :, :]), ALU.subtract).then_inc(s_lg, 1)
                        if after:
                            next_rows(i + 1)
                        dve.wait_ge(s_le, 1)
                        dve.sem_inc(s_le, -1)
                        L(v.tensor_reduce(redf, flat(pe_), AX.X, ALU.add))
                        L(v.reciprocal(redf, redf))
                        L(v.tensor_tensor(flat(pe_), flat(pe_), over(red[:, :, :]), ALU.mult))
                        cur = pe_
                        for k in range(TOPK):
                            topk_k = top_p[:, k, bass.ds(2 * G * i, 2 * G)]
                            L(v.tensor_reduce(redf, flat(cur), AX.X, ALU.max))
                            v.tensor_copy(topk_k, redf).then_inc(s_chain, 1)
                            v.tensor_tensor(flat(wk), flat(cur), over(red[:, :, :]), ALU.is_equal).then_inc(s_chain, 1)
                            dve.wait_ge(s_chain, 2)
                            dve.sem_inc(s_chain, -2)
                            L(v.scalar_tensor_tensor(flat(wk), e_b, -float(E), flat(wk), ALU.add, ALU.mult))
                            L(v.tensor_reduce(redf, flat(wk), AX.X, ALU.min))
                            L(v.tensor_scalar(redf, redf, float(E), None, ALU.add))
                            for g in ORDER:
                                if k == 0:
                                    v.tensor_copy(xr[:, g, :, C + 1], red[:, g, :]).then_inc(s_chain, 1)
                                v.tensor_tensor(hot2[:, g, k, :, :], eid[:, :].unsqueeze(1).to_broadcast([P, G, E]),
                                                red[:, g, :].unsqueeze(2).to_broadcast([P, G, E]), ALU.is_equal).then_inc(s_chain, 1)
                            dve.wait_ge(s_chain, 4 - 2 * k)
                            dve.sem_inc(s_chain, -(4 - 2 * k))
                            if k == 0:
                                L(v.scalar_tensor_tensor(pm[:, :, :, :], hot2[:, :, 0, :, :], -2.0, pe_[:, :, :, :], ALU.mult, ALU.add))
                                cur = pm
                        v.tensor_tensor(both[:, :, :, :], hot2[:, :, 0, :, :], hot2[:, :, 1, :, :], ALU.add).then_inc(s_both, 1)
                        dve.wait_ge(s_rank, 1)
                        dve.sem_inc(s_rank, -1)
                        L(v.tensor_tensor(gates[:, bass.ds(2 * G * i, 2 * G), :], flat(both), flat(pe_), ALU.mult))
                        L(v.tensor_tensor(flat(place), bank[0][:, 2 * P:3 * P].rearrange("p (t e) -> p t e", e=E),
                                          filled[:, :].unsqueeze(1).to_broadcast([P, 2 * G, E]), ALU.add))
                        L(v.tensor_tensor(filled[:, :], filled[:, :], bank[0][:, 3 * P:3 * P + E], ALU.add))
                        if after:
                            dve.sem_inc(s_rr, 1)
                        for k in range(TOPK):
                            v.tensor_tensor(hp[:, :, k, :, :], hot2[:, :, k, :, :], place[:, :, :, :], ALU.mult).then_inc(s_chain, 1)
                        dve.wait_ge(s_chain, 2)
                        dve.sem_inc(s_chain, -2)
                        for g in ORDER:
                            L(v.tensor_reduce(posf[:, g, :, :], hp[:, g, :, :, :], AX.X, ALU.add))
                            v.tensor_copy(posi[:, g, :, :], posf[:, g, :, :]).then_inc(s_pos, 1)

                    next_stats(0)
                    next_rows(0)
                    with dve.Fori(0, STEPS1 - 1) as i:
                        step(i)
                    step(STEPS1 - 1, after=False)

                @block.gpsimd
                def _(pool):
                    def L(ins):
                        link(pool, s_pchain, ins)

                    g_ = nc.gpsimd
                    def next_powers():
                        for g in ORDER:
                            norm_power(pool, G * g, G)

                    def units():
                        for g in ORDER:
                            pool.wait_ge(s_mv, 2 * G)
                            pool.sem_inc(s_mv, -2 * G)
                            L(g_.tensor_tensor(shift[:, g, :], mv2[:, g, 0, :, 0], mv2[:, g, 1, :, 0], ALU.add))
                            L(g_.tensor_scalar(shift[:, g, :], shift[:, g, :], 0.5, 0.0, ALU.mult, ALU.add))
                            L(g_.tensor_scalar(spread[:, g, :, :], mv2[:, g, :, :, 1], C / (C - 1.0), 0.0, ALU.mult, ALU.add))
                            sp2 = spread[:, g, :, :].rearrange("p q s -> p (q s)")
                            L(g_.tensor_tensor(sp2, sp2, cst[:, 1:2].to_broadcast([P, 2 * G]), ALU.pow))
                            L(g_.tensor_tensor(unit[:, g, :], spread[:, g, 0, :], spread[:, g, 1, :], ALU.add))
                            L(g_.tensor_scalar(unit[:, g, :], unit[:, g, :], 0.5, 1e-6, ALU.mult, ALU.add))
                            g_.tensor_tensor(unit[:, g, :], unit[:, g, :], cst[:, 2:3].to_broadcast([P, G]), ALU.pow).then_inc(s_un, 1)

                    def router_powers():
                        for g in ORDER:
                            norm_power(pool, NSLOT + G * g, G)

                    def buffers_free(steps):
                        for g in ORDER:
                            pool.wait_ge(s_xs[g], steps * (16 * TOPK * G))
                            pool.sem_inc(s_xf, 1)

                    pool.sem_inc(s_xf, 2)
                    next_powers()
                    units()
                    router_powers()
                    next_powers()
                    scatter_rows(pool, 1)
                    with pool.Fori(1, STEPS1 - 1) as i:
                        units()
                        scatter_rows(pool, 0)
                        buffers_free(i)
                        router_powers()
                        next_powers()
                        scatter_rows(pool, 1)
                    units()
                    scatter_rows(pool, 0)
                    buffers_free(STEPS1 - 1)
                    router_powers()

                @block.scalar
                def _(act):
                    def copy_xT():
                        for g in ORDER:
                            act.wait_ge(s_xTp, 1)
                            act.sem_inc(s_xTp, -1)
                            nc.scalar.activation(xT[:, G * g:G * g + G, :], banks(g)[:, :, 0:P], ACT.Copy).then_inc(s_xT, 1)

                    def step(after=True):
                        for g in ORDER:
                            act.wait_ge(s_gb, 1)
                            act.sem_inc(s_gb, -1)
                            nc.scalar.activation(kv[:, g, :, :, :], banks(g)[:, :, C:3 * C].rearrange("p s (a c) -> p s a c", a=2), ACT.Copy).then_inc(s_kvc, 1)
                            act.wait_ge(s_kvc, 1)
                            act.sem_inc(s_kvc, -1)
                            nc.scalar.activation(gate[:, g, :, :], gate[:, g, :, :], ACT.Tanh, scale=0.5).then_inc(s_ge, 1)
                        for g in ORDER:
                            act.wait_ge(s_rtp, 1)
                            act.sem_inc(s_rtp, -1)
                            nc.scalar.activation(rotT[:, g, :, :, :], banks(g)[:, :, P:3 * P].rearrange("p s (a c) -> p s a c", a=2), ACT.Copy).then_inc(s_rt, 1)
                        for g in ORDER:
                            act.wait_ge(s_zp, 1)
                            act.sem_inc(s_zp, -1)
                            nc.scalar.activation(zT[:, g, :, :], banks(g)[:, :, 0:P], ACT.Copy, scale=float(C) ** -0.5).then_inc(s_z, 1)
                        for g in ORDER:
                            act.wait_ge(s_mx, 1)
                            act.sem_inc(s_mx, -1)
                            for s in range(G):
                                m = nc.scalar.activation(sm[:, g, s, :], sm[:, g, s, :], ACT.Exp, bias=nmx1[:, g, s:s + 1], accum_out=rsum[:, g, s:s + 1])
                            m.then_inc(s_pr1, 1)
                            nc.scalar.activation(esink[:, g, :], nmx1[:, g, :], ACT.Exp, bias=sink_c[:, :]).then_inc(s_p, 1)
                        for g in ORDER:
                            act.wait_ge(s_pp, 1)
                            act.sem_inc(s_pp, -1)
                            nc.scalar.activation(pT[:, g, :, :], banks(g)[:, :, 2 * P:3 * P], ACT.Copy).then_inc(s_pt, 1)
                        copy_xT()
                        act.wait_ge(s_lg, 1)
                        act.sem_inc(s_lg, -1)
                        nc.scalar.activation(pe_[:, :, :, :], lg[:, :, :, :], ACT.Exp).then_inc(s_le, 1)
                        if after:
                            copy_xT()

                    copy_xT()
                    with act.Fori(0, STEPS1 - 1) as i:
                        step()
                    step(after=False)

                @block.tensor
                def _(pe):
                    pe.wait_ge(s_wd, 1)
                    pe.sem_inc(s_wd, -1)
                    nc.tensor.transpose(bank[6][:, 0:P], wedge[:, :], ident[:, :]).then_inc(s_wdt, 1)
                    pe.wait_ge(s_wdc, 1)
                    pe.sem_inc(s_wdc, -1)
                    nc.tensor.matmul(bank[6][:, P:2 * P], wedgeT[:, :], wedgeT[:, :], start=True, stop=True).then_inc(s_gr, 1)
                    pe.wait_ge(s_wdc, 1)
                    pe.sem_inc(s_wdc, -1)

                    def flip_rows(g, src):
                        pe.wait_ge(s_xn, G)
                        pe.sem_inc(s_xn, -G)
                        for s in range(G):
                            m = nc.tensor.transpose(banks(g)[:, s, 0:P], src(s), ident[:, :])
                        m.then_inc(s_xTp, 1)

                    def project(g, tiles):
                        for s in tiles:
                            m = nc.tensor.matmul(banks(g)[:, s, :], xT[:, G * g + s, :], w_qkvg[:, :], start=True, stop=True)
                        return m

                    def step(after=True):
                        for g in ORDER:
                            pe.wait_ge(s_gq, 1)
                            pe.sem_inc(s_gq, -1)
                            for s in range(G):
                                m = nc.tensor.matmul(banks(g)[:, s, 0:C], run_sum[:, :], gq[:, g, s, :], start=True, stop=True)
                            m.then_inc(s_qc, 1)
                        for g in ORDER:
                            pe.wait_ge(s_rot, 1)
                            pe.sem_inc(s_rot, -1)
                            for s in range(G):
                                for x in range(2):
                                    m = nc.tensor.transpose(banks(g)[:, s, (1 + x) * P:(2 + x) * P], rot[:, g, s, x, :], ident[:, :])
                            m.then_inc(s_rtp, 1)
                        for g in ORDER:
                            pe.wait_ge(s_rt, 1)
                            pe.sem_inc(s_rt, -1)
                            for s in range(G):
                                m = nc.tensor.matmul(banks(g)[:, s, 0:P], gram[:, :], rotT[:, g, s, 0, :], start=True, stop=True)
                            m.then_inc(s_zp, 1)
                        for g in ORDER:
                            pe.wait_ge(s_z, 1)
                            pe.sem_inc(s_z, -1)
                            for s in range(G):
                                m = nc.tensor.matmul(banks(g)[:, s, P:2 * P], zT[:, g, s, :], rotT[:, g, s, 1, :], start=True, stop=True)
                            m.then_inc(s_s, 1)
                        for g in ORDER:
                            pe.wait_ge(s_pr1, 1)
                            pe.sem_inc(s_pr1, -1)
                            for s in range(G):
                                m = nc.tensor.transpose(banks(g)[:, s, 2 * P:3 * P], sm[:, g, s, :], ident[:, :])
                            m.then_inc(s_pp, 1)
                        for g in ORDER:
                            pe.wait_ge(s_pt, 1)
                            pe.sem_inc(s_pt, -1)
                            for s in range(G):
                                m = nc.tensor.matmul(banks(g)[:, s, 3 * P:4 * P], pT[:, g, s, :], kv[:, g, s, 1, :], start=True, stop=True)
                            m.then_inc(s_o1, 1)
                        for g in ORDER:
                            flip_rows(g, lambda s: xr[:, g, s, 0:C])
                        for g in ORDER:
                            pe.wait_ge(s_xT, 1)
                            pe.sem_inc(s_xT, -1)
                            for s in range(G):
                                m = nc.tensor.matmul(banks(g)[:, s, P:P + E], xT[:, G * g + s, :], r_w[:, :], start=True, stop=True)
                            m.then_inc(s_lgp, 1)
                        if after:
                            pe.wait_ge(s_lr, 1)
                            pe.sem_inc(s_lr, -1)
                            for g in ORDER:
                                flip_rows(g, lambda s: xn[:, G * g + s, :])
                            pe.wait_ge(s_xT, 1)
                            pe.sem_inc(s_xT, -1)
                            project(1, range(G)).then_inc(s_pj, 1)
                            pe.wait_ge(s_xT, 1)
                            pe.sem_inc(s_xT, -1)
                        pe.wait_ge(s_both, 1)
                        pe.sem_inc(s_both, -1)
                        rank = bank[0][:, 2 * P:3 * P]
                        bf = both[:, :, :, :].rearrange("p g s e -> p (g s e)")
                        nt = 2 * G
                        nc.tensor.matmul(rank, tri_h[:, :], bf, start=True, stop=False)
                        for d in range(1, nt):
                            nc.tensor.matmul(rank[:, d * E:nt * E], ones_h[:, :], bf[:, 0:(nt - d) * E], start=False, stop=(d == nt - 1))
                        for t in range(nt):
                            m = nc.tensor.matmul(bank[0][:, 3 * P:3 * P + E], ones_h[:, :], bf[:, t * E:(t + 1) * E], start=(t == 0), stop=(t == nt - 1))
                        m.then_inc(s_rank, 1)
                        if after:
                            project(0, range(1, G))
                            pe.wait_ge(s_rr, 1)
                            pe.sem_inc(s_rr, -1)
                            project(0, range(1)).then_inc(s_pj, 1)

                    for g in ORDER:
                        flip_rows(g, lambda s: xn[:, G * g + s, :])
                    for g in ORDER:
                        pe.wait_ge(s_xT, 1)
                        pe.sem_inc(s_xT, -1)
                        project(g, range(G)).then_inc(s_pj, 1)
                    with pe.Fori(0, STEPS1 - 1) as i:
                        step()
                    step(after=False)

        with ExitStack() as ph:
            G, SETS, PAIRS_E = 2, 3, WAYS // 2
            gatesT = sb("gatesT", [P, 4, P], f32, ph)
            count = sb("count", [P, E], f32, ph)
            ntile_i = sb("ntile_i", [P, E], i32, ph)
            ntile = sb("ntile", [P, E], f32, ph)
            last1 = sb("last1", [P, E], f32, ph)
            last2 = sb("last2", [P, E], f32, ph)
            inside = sb("inside", [P, E], f32, ph)
            start_r = sb("start_r", [P, E], f32, ph)
            wkE = sb("wkE", [P, E], f32, ph)
            tab = sb("tab", [P, 4], f32, ph)
            tab_e = sb("tab_e", [P, P], f32, ph)
            tabT = sb("tabT", [1, P], i32, ph)
            pad_at = sb("pad_at", [1, E], i32, ph)
            e_of = sb("e_of", [P, SLOTS], f32, ph)
            xg = sb("xg", [P, WAYS, XW], f32, ph)
            w1b = sb("w1b", [P, WAYS, FF + NC1], f32, ph)
            hid = sb("hid", [P, G * SETS, NC1, P], f32, ph)
            yo = sb("yo", [P, SETS, G, C], f32, ph)
            own = sb("own", [P, SETS, G], f32, ph)
            dest = sb("dest", [P, SETS, G], i32, ph)
            yg = sb("yg", [P, TOPK, B, C], f32, ph)
            s_gt, s_tab, s_tp2, s_ej, s_pad = (sem(n) for n in ("gatesT_psum", "table_ready", "table_psum", "expert_table", "pads_written"))
            s_pa = sem("pad_places")
            s_b2p, s_gtc = sem("b2_psum"), sem("gatesT_ready")
            s_ld = [sem(f"tile_loaded_{n}") for n in range(WAYS)]
            s_fr, s_xgp, s_xg, s_hp, s_hid, s_yp, s_bk, s_y = (sem(n) for n in (
                "weights_free", "xgT_psum", "xgT_ready", "hidden_psum", "hidden_ready", "y_psum", "y_out_of_psum", "y_ready"))
            s_ys = [sem(f"y_scattered_{m}") for m in range(SETS)]
            s_b2c = sem("b2_added")
            s_tabc, s_pa2, s_pad2, s_xa = (sem(n) for n in ("table_copied", "pad_places_b", "pads_written_b", "all_rows_scattered"))
            s_all, s_yf = sem("all_y_scattered"), sem("y_buffer_free")
            s_yg, s_out, s_fin = [sem(f"y_rows_loaded_{g}") for g in range(8)], sem("out_stored"), sem("out_ready")
            NSTEP = -(-SLOTS // WAYS)
            LAST = (SLOTS - (NSTEP - 1) * WAYS) // G
            FULL, ODD = divmod(SLOTS // G, SETS)
            flipped = bank[6]
            with nc.Block() as block:
                @block.vector
                def _(dve):
                    v = nc.vector

                    def L(ins):
                        link(dve, s_chain, ins)
                    dve.wait_ge(s_gt, 1)
                    dve.sem_inc(s_gt, -1)
                    v.tensor_copy(gatesT[:, :, :], bank[2][:, :].rearrange("p (g t) -> p g t", g=4)).then_inc(s_gtc, 1)
                    L(v.tensor_copy(pad_at[:, :], filled[0:1, :]))
                    dve.sem_inc(s_pa, 1)
                    dve.sem_inc(s_pa2, 1)
                    L(v.tensor_tensor(count[:, :], filled[:, :], region[:, :], ALU.subtract))
                    L(v.tensor_scalar(ntile_i[:, :], count[:, :], P - 1.0, None, ALU.add))
                    L(v.tensor_scalar(ntile_i[:, :], ntile_i[:, :], 7, None, ALU.logical_shift_right))
                    L(v.tensor_copy(ntile[:, :], ntile_i[:, :]))
                    s2, d2 = ntile, last1
                    step = 1
                    while step < E:
                        v.tensor_copy(d2[:, 0:step], s2[:, 0:step]).then_inc(s_chain, 1)
                        L(v.tensor_tensor(d2[:, step:E], s2[:, step:E], s2[:, 0:E - step], ALU.add))
                        dve.wait_ge(s_chain, 1)
                        dve.sem_inc(s_chain, -1)
                        s2, d2 = d2, (last2 if d2 is last1 else last1)
                        step *= 2
                    ends, base = s2, d2
                    me = cst[:, 3:4]
                    L(v.tensor_tensor(base[:, :], ends[:, :], ntile[:, :], ALU.subtract))
                    L(v.tensor_scalar(inside[:, :], ends[:, :], me, None, ALU.is_le))
                    L(v.tensor_reduce(tab[:, 0:1], inside[:, :], AX.X, ALU.add))
                    L(v.tensor_scalar(tab[:, 0:1], tab[:, 0:1], E - 1.0, None, ALU.min))
                    L(v.tensor_scalar(wkE[:, :], base[:, :], me, None, ALU.is_le))
                    L(v.tensor_tensor(inside[:, :], wkE[:, :], inside[:, :], ALU.subtract))
                    L(v.tensor_reduce(tab[:, 2:3], inside[:, :], AX.X, ALU.add))
                    L(v.tensor_scalar(start_r[:, :], base[:, :], me, -float(P), ALU.subtract, ALU.mult))
                    L(v.tensor_tensor(start_r[:, :], start_r[:, :], region[:, :], ALU.add))
                    L(v.tensor_tensor(start_r[:, :], start_r[:, :], inside[:, :], ALU.mult))
                    L(v.tensor_reduce(tab[:, 1:2], start_r[:, :], AX.X, ALU.add))
                    L(v.tensor_scalar(tab[:, 2:3], tab[:, 2:3], -float(E * REGION - P), float(E * REGION - P), ALU.mult, ALU.add))
                    L(v.tensor_tensor(tab[:, 1:2], tab[:, 1:2], tab[:, 2:3], ALU.add))
                    v.tensor_copy(tab_e[:, :], tab[:, 0:1].to_broadcast([P, P])).then_inc(s_tab, 1)
                    dve.wait_ge(s_tp2, 1)
                    dve.sem_inc(s_tp2, -1)
                    L(v.tensor_copy(tabT[:, :], bank[3][0:1, 0:P]))
                    dve.sem_inc(s_ej, 1)
                    L(v.tensor_copy(e_of[:, :], bank[3][:, P:P + SLOTS]))
                    dve.sem_inc(s_tabc, 1)

                    for g in range(8):
                        dve.wait_ge(s_b2p, 1)
                        dve.sem_inc(s_b2p, -1)
                        v.tensor_tensor(h[:, 4 * g:4 * g + 4, :], h[:, 4 * g:4 * g + 4, :], bank[g % 2][:, :].rearrange("p (t c) -> p t c", t=4), ALU.add).then_inc(s_b2c, 1)

                    def rows_in(j, q):
                        m = q % SETS
                        sl = slice(G * q, G * q + G)
                        dve.wait_ge(s_xgp, 1)
                        dve.sem_inc(s_xgp, -1)
                        v.tensor_copy(xT[:, G * m:G * m + G, :], flipped[:, 0:G * P].rearrange("p (s t) -> p s t", s=G)).then_inc(s_xg, 1)
                        L(v.tensor_tensor(own[:, m, :], xg[:, sl, C + 1], e_of[:, bass.ds(WAYS * j + G * q, G)], ALU.not_equal))
                        L(v.scalar_tensor_tensor(own[:, m, :], own[:, m, :], float(B * P), xg[:, sl, C], ALU.mult, ALU.add))

                    def rows_out(q):
                        m = q % SETS
                        dve.wait_ge(s_yf, 1)
                        dve.sem_inc(s_yf, -1)
                        v.tensor_copy(dest[:, m, :], own[:, m, :]).then_inc(s_chain, 1)
                        dve.wait_ge(s_yp, 1)
                        dve.sem_inc(s_yp, -1)
                        v.tensor_copy(yo[:, m, :, :], acc[:, G * m:G * m + G, 0:P]).then_inc(s_y, 1)
                        dve.wait_ge(s_chain, 1)
                        dve.sem_inc(s_chain, -1)

                    rows_in(0, 0)
                    rows_in(0, 1)
                    with dve.Fori(0, NSTEP - 1) as j:
                        for q in range(PAIRS_E):
                            rows_in(j + 1 if q >= PAIRS_E - 2 else j, (q + 2) % PAIRS_E)
                            rows_out(q)
                    for q in range(LAST):
                        if q < LAST - 2:
                            rows_in(NSTEP - 1, q + 2)
                        rows_out(q)
                    for g in range(8):
                        dve.wait_ge(s_yg[g], 16 * TOPK)
                        for n in range(TOPK):
                            for t in range(4 * g, 4 * g + 4):
                                v.scalar_tensor_tensor(h[:, t, :], yg[:, n, t, :], top_p[:, n, t:t + 1], h[:, t, :], ALU.mult, ALU.add).then_inc(s_fin if n else s_chain, 1)
                            if n == 0:
                                dve.wait_ge(s_chain, 4)
                                dve.sem_inc(s_chain, -4)

                @block.gpsimd
                def _(pool):
                    def scatter_y(m):
                        pool.wait_ge(s_y, 1)
                        pool.sem_inc(s_y, -1)
                        pool.sem_inc(s_bk, 1)
                        for n in range(G):
                            nc.gpsimd.indirect_dma_start(ys_dram[:, :], bass.IndirectOffsetOnAxis(dest[:, m, n:n + 1], 0), yo[:, m, n, :], None,
                                                         bounds_check=TOPK * B * P - 1, oob_is_err=False).then_inc(s_ys[m], 16)

                    for g in range(2):
                        scatter_rows(pool, g)
                    for g in range(2):
                        pool.wait_ge(s_xs[g], 16 * TOPK * 4 * (B // NSLOT))
                    pool.sem_inc(s_xa, 1)
                    pool.sem_inc(s_yf, SETS)
                    for m in range(SETS):
                        scatter_y(m)
                        if m:
                            pool.wait_ge(s_ys[m - 1], 16 * G)
                            pool.sem_inc(s_yf, 1)
                    with pool.Fori(1, FULL) as j:
                        scatter_y(0)
                        pool.wait_ge(s_ys[SETS - 1], j * (16 * G))
                        pool.sem_inc(s_yf, 1)
                        for m in range(1, SETS):
                            scatter_y(m)
                            pool.wait_ge(s_ys[m - 1], j * (16 * G) + 16 * G)
                            pool.sem_inc(s_yf, 1)
                    for m in range(ODD):
                        scatter_y(m)
                        pool.sem_inc(s_yf, 1)
                    for m in range(SETS):
                        pool.wait_ge(s_ys[m], (FULL + (m < ODD)) * 16 * G)
                    pool.sem_inc(s_all, 1)

                @block.sync
                def _(sp):
                    sp.wait_ge(s_w2, 16)
                    sp.dma_start(xs_dram[E * REGION - P:E * REGION, :], pad_rows[:, :]).then_inc(s_pad, 16)
                    sp.wait_ge(s_pa, 1)
                    sp.sem_inc(s_pa, -1)
                    for e in range(E // 2):
                        at = sp.value_load(pad_at[0:1, e:e + 1], min_val=e * REGION, max_val=e * REGION + B * P)
                        sp.dma_start(xs_dram[bass.ds(at, P), :], pad_rows[:, :]).then_inc(s_pad, 16)
                    sp.wait_ge(s_ej, 1)
                    sp.sem_inc(s_ej, -1)
                    sp.wait_ge(s_pad, 16 * (E // 2 + 1))
                    sp.wait_ge(s_pad2, 16 * (E // 2))
                    sp.wait_ge(s_xa, 1)
                    sp.sem_inc(s_xa, -1)
                    def load(j, n):
                        sp.wait_ge(s_fr, 1)
                        sp.sem_inc(s_fr, -1)
                        row = sp.value_load(tabT[0:1, bass.ds(WAYS * j + n, 1)], min_val=0, max_val=E * REGION - P)
                        sp.dma_start(xg[:, n, :], xs_dram[bass.ds(row, P), :]).then_inc(s_ld[n], 16)
                        sp.dma_start(w1b[:, n, :], a["w1b"][bass.ds(row // REGION, 1), :, :].rearrange("a p f -> (a p) f")).then_inc(s_ld[n], 16)

                    with sp.Fori(0, NSTEP - 1) as j:
                        for n in range(WAYS):
                            load(j, n)
                    for n in range(G * LAST):
                        load(NSTEP - 1, n)
                    sp.wait_ge(s_all, 1)
                    sp.sem_inc(s_all, -1)
                    ysv = ys_dram.rearrange("(n b p) c -> n p b c", n=TOPK, p=P)
                    for g in range(8):
                        for n in range(TOPK):
                            sp.dma_start(yg[:, n, 4 * g:4 * g + 4, :], ysv[n, :, 4 * g:4 * g + 4, :]).then_inc(s_yg[g], 16)
                    for g in range(8):
                        sp.wait_ge(s_fin, 4 * (g + 1))
                        sp.dma_start(out[4 * g:4 * g + 4, :, :].rearrange("b p c -> p b c"), h[:, 4 * g:4 * g + 4, :]).then_inc(s_out, 16)
                    sp.wait_ge(s_out, 16 * 8)

                @block.scalar
                def _(act):
                    act.wait_ge(s_pa2, 1)
                    act.sem_inc(s_pa2, -1)
                    for e in range(E // 2, E):
                        at = act.value_load(pad_at[0:1, e:e + 1], min_val=e * REGION, max_val=e * REGION + B * P)
                        act.dma_start(xs_dram[bass.ds(at, P), :], pad_rows[:, :]).then_inc(s_pad2, 16)
                    def hidden(n):
                        act.wait_ge(s_hp, 1)
                        act.sem_inc(s_hp, -1)
                        at = n % (G * SETS)
                        for c in range(NC1):
                            m = nc.scalar.activation(hid[:, at, c, :], acc[:, at, c * P:(c + 1) * P], ACT.Gelu, bias=w1b[:, n, FF + c:FF + c + 1])
                        m.then_inc(s_hid, 1)

                    with act.Fori(0, NSTEP - 1) as j:
                        for n in range(WAYS):
                            hidden(n)
                    for n in range(G * LAST):
                        hidden(n)

                @block.tensor
                def _(pe):
                    for g in range(4):
                        m = nc.tensor.transpose(bank[2][:, g * P:(g + 1) * P], gates[:, 8 * g:8 * g + 8, :], ident[:, :])
                    m.then_inc(s_gt, 1)
                    pe.wait_ge(s_tab, 1)
                    pe.sem_inc(s_tab, -1)
                    nc.tensor.matmul(bank[3][0:1, 0:P], tab[:, 1:2], ident[:, :], start=True, stop=True)
                    nc.tensor.matmul(bank[3][:, P:P + SLOTS], tab_e[:, :], ident[:, 0:SLOTS], start=True, stop=True).then_inc(s_tp2, 1)
                    pe.wait_ge(s_gtc, 1)
                    pe.sem_inc(s_gtc, -1)
                    pe.wait_ge(s_tabc, 1)
                    pe.sem_inc(s_tabc, -1)
                    pe.sem_inc(s_fr, WAYS)
                    pe.sem_inc(s_bk, SETS)

                    def flip(q):
                        for n in range(G):
                            pe.wait_ge(s_ld[G * q + n], 32)
                            pe.sem_inc(s_ld[G * q + n], -32)
                            t = nc.tensor.transpose(flipped[:, n * P:(n + 1) * P], xg[:, G * q + n, 0:C], ident[:, :])
                        t.then_inc(s_xgp, 1)

                    def hidden(q):
                        pe.wait_ge(s_xg, 1)
                        pe.sem_inc(s_xg, -1)
                        pe.wait_ge(s_bk, 1)
                        pe.sem_inc(s_bk, -1)
                        for n in range(G * q, G * q + G):
                            at = n % (G * SETS)
                            for c in range(NC1):
                                t = nc.tensor.matmul(acc[:, at, c * P:(c + 1) * P], w1b[:, n, c * P:(c + 1) * P], xT[:, at, :], start=True, stop=True)
                            t.then_inc(s_hp, 1)

                    def result(j, q):
                        for n in range(G * q, G * q + G):
                            at = n % (G * SETS)
                            row = pe.value_load(tabT[0:1, bass.ds(WAYS * j + n, 1)], min_val=0, max_val=E * REGION - P)
                            pe.wait_ge(s_hid, 1)
                            pe.sem_inc(s_hid, -1)
                            pe.sem_inc(s_fr, 1)
                            for c in range(NC1):
                                t = nc.tensor.matmul(acc[:, at, 0:P], hid[:, at, c, :], w2_all[:, bass.ds(row // REGION, 1), c, :].rearrange("p a c -> p (a c)"), start=(c == 0), stop=(c == NC1 - 1))
                        t.then_inc(s_yp, 1)

                    for g in range(8):
                        if g >= 2:
                            pe.wait_ge(s_b2c, 1)
                            pe.sem_inc(s_b2c, -1)
                        nc.tensor.matmul(bank[g % 2][:, :], gatesT[:, g // 2, :], b2_blocks[:, 4 * (g % 2):4 * (g % 2) + 4, :], start=True, stop=True).then_inc(s_b2p, 1)
                    pe.wait_ge(s_b2c, 2)
                    pe.sem_inc(s_b2c, -2)

                    flip(0)
                    hidden(0)
                    flip(1)
                    with pe.Fori(0, NSTEP - 1) as j:
                        for q in range(PAIRS_E):
                            hidden((q + 1) % PAIRS_E)
                            flip((q + 2) % PAIRS_E)
                            result(j, q)
                    for q in range(LAST):
                        if q < LAST - 1:
                            hidden(q + 1)
                        if q < LAST - 2:
                            flip(q + 2)
                        result(NSTEP - 1, q)


def kernel(**inputs):
    import concourse.bacc as _bacc
    from concourse.bass_utils import run_bass_kernel_spmd as _run

    x = {k: np.asarray(v) for k, v in inputs.items()}
    f = np.float32
    n = np.arange(64)
    win = 0.5 - 0.5 * np.cos(2.0 * np.pi * n / 64)
    dft = np.zeros((P, 2, NFRAME, NFREQ), np.float64)
    for fr in range(NFRAME):
        at = fr * 64 + n - 32
        at = np.where(at < 0, -at, at)
        at = np.where(at > P - 1, 2 * (P - 1) - at, at)
        for k in range(NFREQ):
            np.add.at(dft[:, 0, fr, k], at, win * np.cos(2 * np.pi * k * n / 64))
            np.add.at(dft[:, 1, fr, k], at, -win * np.sin(2 * np.pi * k * n / 64))
    l = np.arange(P)
    inv = (1.0 / 10000.0 ** (np.arange(0, C, 2, dtype=f) / f(C))).astype(f)
    fr = l[:, None].astype(f) * inv[None, :]
    same = (l[:, None] // 64) == (l[None, :] // 64)
    run = (same & (l[:, None] <= l[None, :])) + 2.0 * ((l[:, None] < 64) & (l[None, :] >= 64))
    cst = np.tile(np.array([-0.5, 0.5, -1.0, 0.0], f), (P, 1))
    cst[:, 3] = l
    pad = np.zeros((P, XW), f)
    pad[:, C], pad[:, C + 1] = SKIP, -1.0
    tok = x["x"].astype(np.int32)
    proj = x["L0_tok_proj_w"].reshape(NFREQ, V, D_STFT)
    eo = np.concatenate([np.arange(0, C, 2), np.arange(1, C, 2)])
    w1 = x["L1_ffn_w1"].transpose(0, 2, 1)
    b1 = x["L1_ffn_b1"].reshape(E, NC1, P).transpose(0, 2, 1)
    A = x["L1_attn_A"][0]
    arrays = {
        "idsT": tok.T, "ids": tok.reshape(-1), "emb": x["L0_tok_emb_table"], "dft": dft.reshape(P, 2 * NFRAME, NFREQ).astype(f),
        "pw": proj, "pb": x["L0_tok_proj_b"], "up": ((l[None, :] * 3 // P) == np.arange(3)[:, None]).astype(f),
        "eid": np.arange(E).astype(f), "region": (REGION * np.arange(E)).astype(f), "pad_rows": pad,
        "rank_no": np.arange(WIDEST).astype(f), "tok_id": (P * np.arange(B)[None, :] + l[:, None]).astype(f), "cst": cst, "ident": np.eye(P, dtype=f),
        "w_q": x["L0_attn_q_w"].T.reshape(C, 2, HG, DH), "w_k": x["L0_attn_kv_w"][:C].T.reshape(C, 2, HG, DH),
        "w_v": x["L0_attn_kv_w"][C:].T, "in_pat": x["L0_ffn_input_patterns"].T,
        "proc_w": x["L0_ffn_process_input_weights"].T.reshape(4, P, N_PROC).transpose(1, 0, 2),
        "proc_v": x["L0_ffn_process_values"].reshape(2, P, D_PV).transpose(1, 0, 2),
        "out_w": x["L0_ffn_output_input_weights"].T,
        "out_pat": x["L0_ffn_output_patterns"].reshape(4, P, C).transpose(1, 0, 2),
        "w_qkvg": np.concatenate([x["L1_attn_Wq"][eo], x["L1_attn_Wk"][eo], x["L1_attn_Wv"], x["L1_attn_Wg"][eo]]).T,
        "bg": x["L1_attn_bg"][eo], "A": A, "AT": A.T, "sink": x["L1_attn_sink"].reshape(1), "v_null": x["L1_attn_v_null"].reshape(C),
        "cos": np.cos(fr).astype(f), "sin": np.sin(fr).astype(f), "run_sum": (0.5 * run).astype(f),
        "causal": np.where(l[:, None] >= l[None, :], 0.0, -BIG).astype(f),
        "r_w": x["L1_ffn_router_w"].T, "r_b": x["L1_ffn_router_b"], "tri": (l[:, None] < l[None, :]).astype(f),
        "w2": x["L1_ffn_w2"].reshape(E, C, NC1, P).transpose(3, 0, 2, 1), "b2": x["L1_ffn_b2"],
        "w1b": np.concatenate([w1, b1], axis=2),
    }
    nc = _bacc.Bacc("TRN2", target_bir_lowering=False, num_devices=1)
    args, ins = {}, {}
    for k, v in arrays.items():
        v = np.ascontiguousarray(v)
        ins["in_" + k] = v
        args[k] = nc.dram_tensor("in_" + k, v.shape, mybir.dt.from_np(v.dtype), kind="ExternalInput").ap()
    out = nc.dram_tensor("out_0", (B, P, C), mybir.dt.float32, kind="ExternalOutput").ap()
    build(nc, args, out)
    r = _run(nc, [ins], core_ids=[0])
    return r.results[0]["out_0"]
```
